# Optimizing a Trainium2 kernel written in Bass

```python
import numpy as np
import jax
import jax.numpy as jnp

def _softmax(x, axis=-1):
    return jax.nn.softmax(x, axis=axis)

def _gelu(x):
    return jax.nn.gelu(x, approximate=True)

def _silu(x):
    return jax.nn.silu(x)

def _sigmoid(x):
    return jax.nn.sigmoid(x)

def _layernorm(x, axis=-1, eps=1e-05):
    m = jnp.mean(x, axis=axis, keepdims=True)
    v = jnp.var(x, axis=axis, keepdims=True)
    return (x - m) / jnp.sqrt(v + eps)

def _scatter_add(tgt, idx, src, axis=0):
    return tgt.at[idx].add(src)

def _segment_sum(src, seg, n):
    return jax.ops.segment_sum(src, seg, n)
kernel_name = 'mk_decoder_preln_d2_seqx_r4_160f4c'

def setup_inputs(seed: int=0):
    np.random.seed(seed)
    _w = jnp.asarray

    def _rec_inputs():
        import jax
        import jax.numpy as jnp
        _rk = jax.random.key(seed)
        x = -0.0003929 + 0.9999 * jax.random.normal(jax.random.fold_in(_rk, 1), (8, 256, 256), jnp.float32)
        _lenS = 256 - jax.random.randint(jax.random.fold_in(_rk, 7), (8,), 0, max(1, 256 // 4) + 1, jnp.int32)
        _lenS2 = 256 - jax.random.randint(jax.random.fold_in(_rk, 8), (8,), 0, max(1, 256 // 4) + 1, jnp.int32)
        _ctx_768P = jax.random.normal(jax.random.fold_in(_rk, 11), (8, 16, 192), jnp.float32)
        _ctx_768c = jax.random.dirichlet(jax.random.fold_in(_rk, 511), 0.3 * jnp.ones((16,), jnp.float32), (8, 256))
        _ctx_768t = jnp.einsum('bsk,bkd->bsd', _ctx_768c, _ctx_768P)
        _ctx_768t = _ctx_768t * jax.lax.rsqrt(jnp.mean(jnp.square(_ctx_768t)) + 1e-12) * 0.953939
        ctx_768 = -7.36909e-05 + 0.999899 * (_ctx_768t + 0.3 * jax.random.normal(jax.random.fold_in(_rk, 611), (8, 256, 192), jnp.float32))
        _validS = jnp.arange(256)[None, :] < _lenS[:, None]
        _validS2 = jnp.arange(256)[None, :] < _lenS2[:, None]
        _causal = jnp.tril(jnp.ones((256, 256), dtype=bool))
        mask_BxS2_bk0 = jnp.logical_not(jnp.broadcast_to(_validS2[:, :], (8, 256)))
        return (x, ctx_768, mask_BxS2_bk0)
    x, ctx_768, mask_BxS2_bk0 = _rec_inputs()

    def _L0_attn_setup():
        import jax, jax.numpy as jnp
        import numpy as np
        D_MODEL = 256
        D_STATE = 16
        D_CONV = 4
        EXPAND = 2
        D_INNER = EXPAND * D_MODEL
        DT_RANK = 64
        B = 2
        L = 256

        def _dir_params(key):
            k1, k2, k3, k4 = jax.random.split(key, 4)
            conv_w = (jax.random.normal(k1, (D_INNER, D_CONV)) * D_CONV ** (-0.5)).astype(jnp.float32)
            conv_b = jnp.zeros((D_INNER,), jnp.float32)
            x_proj_w = (jax.random.normal(k2, (DT_RANK + 2 * D_STATE, D_INNER)) * D_INNER ** (-0.5)).astype(jnp.float32)
            dt_std = DT_RANK ** (-0.5)
            dt_w = jax.random.uniform(k3, (D_INNER, DT_RANK), minval=-dt_std, maxval=dt_std).astype(jnp.float32)
            dt = jnp.exp(jax.random.uniform(k4, (D_INNER,)) * (np.log(0.1) - np.log(0.001)) + np.log(0.001))
            dt = jnp.clip(dt, 0.0001)
            dt_b = (dt + jnp.log(-jnp.expm1(-dt))).astype(jnp.float32)
            A_log = jnp.log(jnp.tile(jnp.arange(1, D_STATE + 1, dtype=jnp.float32)[None, :], (D_INNER, 1)))
            Dp = jnp.ones((D_INNER,), jnp.float32)
            return (conv_w, conv_b, x_proj_w, dt_w, dt_b, A_log, Dp)

        def _causal_conv(x, w, b):
            y = jax.lax.conv_general_dilated(x, w[:, None, :], window_strides=(1,), padding=[(w.shape[1] - 1, 0)], dimension_numbers=('NCH', 'OIH', 'NCH'), feature_group_count=x.shape[1])
            return y + b[None, :, None]

        def _mamba_inner(xz, conv_w, conv_b, x_proj_w, dt_w, dt_b, A_log, Dp):
            x, z = jnp.split(xz, 2, axis=1)
            x = jax.nn.silu(_causal_conv(x, conv_w, conv_b))
            x_dbl = jnp.einsum('bdl,ed->bel', x, x_proj_w)
            dtr = x_dbl[:, :DT_RANK]
            Bm = x_dbl[:, DT_RANK:DT_RANK + D_STATE]
            Cm = x_dbl[:, DT_RANK + D_STATE:]
            delta = jax.nn.softplus(jnp.einsum('brl,dr->bdl', dtr, dt_w) + dt_b[None, :, None])
            A = -jnp.exp(A_log)
            dA = jnp.exp(jnp.einsum('bdl,dn->lbdn', delta, A))
            dBu = jnp.einsum('bdl,bnl,bdl->lbdn', delta, Bm, x)
            Ct = jnp.transpose(Cm, (2, 0, 1))

            def step(h, inp):
                dA_l, dBu_l, C_l = inp
                h = dA_l * h + dBu_l
                return (h, jnp.einsum('bdn,bn->bd', h, C_l))
            h0 = jnp.zeros((x.shape[0], D_INNER, D_STATE), x.dtype)
            _, ys = jax.lax.scan(step, h0, (dA, dBu, Ct))
            y = jnp.transpose(ys, (1, 2, 0)) + x * Dp[None, :, None]
            return y * jax.nn.silu(z)
        key = jax.random.key(seed)
        ks = jax.random.split(key, 5)
        hidden_states = jax.random.normal(ks[0], (B, L, D_MODEL), dtype=jnp.float32)
        in_proj_w = (jax.random.normal(ks[1], (2 * D_INNER, D_MODEL)) * D_MODEL ** (-0.5)).astype(jnp.float32)
        cw, cb, xw, dw, db, al, dp = _dir_params(ks[2])
        cwb, cbb, xwb, dwb, dbb, alb, dpb = _dir_params(ks[3])
        out_proj_w = (jax.random.normal(ks[4], (D_MODEL, D_INNER)) * D_INNER ** (-0.5)).astype(jnp.float32)
        return {'hidden_states': hidden_states, 'in_proj_w': in_proj_w, 'conv_w': cw, 'conv_b': cb, 'x_proj_w': xw, 'dt_proj_w': dw, 'dt_proj_b': db, 'A_log': al, 'D': dp, 'conv_w_b': cwb, 'conv_b_b': cbb, 'x_proj_w_b': xwb, 'dt_proj_w_b': dwb, 'dt_proj_b_b': dbb, 'A_b_log': alb, 'D_b': dpb, 'out_proj_w': out_proj_w}
    _L0_attn_all = _L0_attn_setup()
    _L0_attn_in = {k: v for k, v in _L0_attn_all.items() if k in ('in_proj_w', 'conv_w', 'conv_b', 'x_proj_w', 'dt_proj_w', 'dt_proj_b', 'A_log', 'D', 'conv_w_b', 'conv_b_b', 'x_proj_w_b', 'dt_proj_w_b', 'dt_proj_b_b', 'A_b_log', 'D_b', 'out_proj_w')}
    del _L0_attn_all

    def _L0_xattn_setup():
        import jax, jax.numpy as jnp
        import numpy as np
        EPS = 1e-05

        def layernorm(x, g, b):
            mu = jnp.mean(x, axis=-1, keepdims=True)
            var = jnp.mean(jnp.square(x - mu), axis=-1, keepdims=True)
            return (x - mu) * jax.lax.rsqrt(var + EPS) * g + b
        key = jax.random.key(seed)
        ks = jax.random.split(key, 12)
        B, L1, L2 = (8, 512, 512)
        D1, D2, E = (256, 192, 256)
        s1, s2, se = (D1 ** (-0.5), D2 ** (-0.5), E ** (-0.5))
        return {'modality1': jax.random.normal(ks[0], (B, L1, D1), jnp.float32), 'modality2': jax.random.normal(ks[1], (B, L2, D2), jnp.float32), 'ln1_g': jnp.ones((D1,), jnp.float32), 'ln1_b': jnp.zeros((D1,), jnp.float32), 'ln2_g': jnp.ones((D2,), jnp.float32), 'ln2_b': jnp.zeros((D2,), jnp.float32), 'Wq': jax.random.normal(ks[2], (D1, E), jnp.float32) * s1, 'bq': jax.random.normal(ks[3], (E,), jnp.float32) * 0.01, 'Wk': jax.random.normal(ks[4], (D2, E), jnp.float32) * s2, 'bk': jax.random.normal(ks[5], (E,), jnp.float32) * 0.01, 'Wv': jax.random.normal(ks[6], (D2, E), jnp.float32) * s2, 'bv': jax.random.normal(ks[7], (E,), jnp.float32) * 0.01, 'Wo': jax.random.normal(ks[8], (E, D1), jnp.float32) * se, 'bo': jax.random.normal(ks[9], (D1,), jnp.float32) * 0.01}
    _L0_xattn_all = _L0_xattn_setup()
    _L0_xattn_in = {k: v for k, v in _L0_xattn_all.items() if k in ('ln1_g', 'ln1_b', 'ln2_g', 'ln2_b', 'Wq', 'bq', 'Wk', 'bk', 'Wv', 'bv', 'Wo', 'bo')}
    del _L0_xattn_all

    def _L0_ffn_setup():
        import jax, jax.numpy as jnp
        import numpy as np
        EPS = 1e-05

        @jax.custom_vjp
        def ste_quantize(w):
            scale = jnp.maximum(jnp.mean(jnp.abs(w)), EPS)
            return jnp.clip(jnp.round(w / scale), -1.0, 1.0)

        def _ste_fwd(w):
            return (ste_quantize(w), None)

        def _ste_bwd(_, g):
            return (g,)
        ste_quantize.defvjp(_ste_fwd, _ste_bwd)
        key = jax.random.key(seed)
        k1, k2 = jax.random.split(key)
        x = jax.random.normal(k1, (8, 2048, 256), dtype=jnp.float32)
        weight = jax.random.normal(k2, (256, 256), dtype=jnp.float32) * 0.02
        return {'x': x, 'weight': weight}
    _L0_ffn_all = _L0_ffn_setup()
    _L0_ffn_in = {k: v for k, v in _L0_ffn_all.items() if k in ('weight',)}
    del _L0_ffn_all

    def _L1_attn_setup():
        import jax, jax.numpy as jnp
        import numpy as np
        import math
        D_MODEL, N_HEADS, D_K, D_C, D_HR = (256, 8, 128, 32, 32)
        B, S = (4, 512)
        key = jax.random.key(seed)
        ks = jax.random.split(key, 17)

        def lin(k, fan_in, fan_out):
            lim = 1.0 / math.sqrt(fan_in)
            kw, kb = jax.random.split(k)
            W = jax.random.uniform(kw, (fan_in, fan_out), jnp.float32, -lim, lim)
            b = jax.random.uniform(kb, (fan_out,), jnp.float32, -lim, lim)
            return (W, b)
        W_DQ, b_DQ = lin(ks[0], D_MODEL, D_C)
        W_UQ, b_UQ = lin(ks[1], D_C, N_HEADS * D_K)
        W_DKV, b_DKV = lin(ks[2], D_MODEL, D_C)
        W_UK, b_UK = lin(ks[3], D_C, N_HEADS * D_K)
        W_UV, b_UV = lin(ks[4], D_C, N_HEADS * D_K)
        W_QR, b_QR = lin(ks[5], D_C, N_HEADS * D_HR)
        W_KR, b_KR = lin(ks[6], D_MODEL, D_HR)
        W_O, b_O = lin(ks[7], N_HEADS * D_K, D_MODEL)
        h_t = jax.random.normal(ks[8], (B, S, D_MODEL), jnp.float32)
        return {'h_t': h_t, 'W_DQ': W_DQ, 'b_DQ': b_DQ, 'W_UQ': W_UQ, 'b_UQ': b_UQ, 'W_DKV': W_DKV, 'b_DKV': b_DKV, 'W_UK': W_UK, 'b_UK': b_UK, 'W_UV': W_UV, 'b_UV': b_UV, 'W_QR': W_QR, 'b_QR': b_QR, 'W_KR': W_KR, 'b_KR': b_KR, 'W_O': W_O, 'b_O': b_O}
    _L1_attn_all = _L1_attn_setup()
    _L1_attn_in = {k: v for k, v in _L1_attn_all.items() if k in ('W_DQ', 'b_DQ', 'W_UQ', 'b_UQ', 'W_DKV', 'b_DKV', 'W_UK', 'b_UK', 'W_UV', 'b_UV', 'W_QR', 'b_QR', 'W_KR', 'b_KR', 'W_O', 'b_O')}
    del _L1_attn_all

    def _L1_xattn_setup():
        import jax, jax.numpy as jnp
        import numpy as np
        DIM_IN, DIM_LAT, DIM_HEAD = (192, 256, 64)
        INNER = max(DIM_LAT, DIM_IN)
        HEADS = INNER // DIM_HEAD
        SCALE = DIM_HEAD ** (-0.5)
        RMS_EPS = 1e-08
        LN_EPS = 1e-05

        def layernorm(x, g, b):
            mu = jnp.mean(x, axis=-1, keepdims=True)
            var = jnp.mean((x - mu) ** 2, axis=-1, keepdims=True)
            return (x - mu) * jax.lax.rsqrt(var + LN_EPS) * g + b

        def rmsnorm(x, gamma):
            norm = jnp.sqrt(jnp.sum(x * x, axis=-1, keepdims=True)) * x.shape[-1] ** (-0.5)
            return x / jnp.maximum(norm, RMS_EPS) * gamma
        key = jax.random.key(seed)
        ks = jax.random.split(key, 12)
        b, n, m = (4, 1024, 128)
        x = jax.random.normal(ks[0], (b, n, DIM_IN), jnp.float32)
        latents = jax.random.normal(ks[1], (b, m, DIM_LAT), jnp.float32)
        mask = jax.random.randint(ks[2], (b, n), 0, 2).astype(bool)
        s = lambda k, sh, fan: jax.random.normal(k, sh, jnp.float32) * fan ** (-0.5)
        return {'x': x, 'latents': latents, 'mask': mask, 'ln_x_g': jnp.ones((DIM_IN,), jnp.float32), 'ln_x_b': jnp.zeros((DIM_IN,), jnp.float32), 'ln_l_g': jnp.ones((DIM_LAT,), jnp.float32), 'ln_l_b': jnp.zeros((DIM_LAT,), jnp.float32), 'qn_g': jnp.ones((DIM_HEAD,), jnp.float32), 'kn_g': jnp.ones((DIM_HEAD,), jnp.float32), 'Wq': s(ks[3], (INNER, DIM_LAT), DIM_LAT), 'Wkv': s(ks[4], (2 * INNER, DIM_IN), DIM_IN), 'Wlkv': s(ks[5], (2 * INNER, DIM_LAT), DIM_LAT), 'Wo': s(ks[6], (DIM_LAT, INNER), INNER), 'bo': jnp.zeros((DIM_LAT,), jnp.float32)}
    _L1_xattn_all = _L1_xattn_setup()
    _L1_xattn_in = {k: v for k, v in _L1_xattn_all.items() if k in ('ln_x_g', 'ln_x_b', 'ln_l_g', 'ln_l_b', 'qn_g', 'kn_g', 'Wq', 'Wkv', 'Wlkv', 'Wo', 'bo')}
    del _L1_xattn_all

    def _L1_ffn_setup():
        import jax, jax.numpy as jnp
        import numpy as np
        D_MODEL, D_FF, RANK = (256, 1024, 64)
        B, S = (4, 1024)
        key = jax.random.key(seed)
        ks = jax.random.split(key, 7)
        return {'x': jax.random.normal(ks[0], (B, S, D_MODEL), dtype=jnp.float32), 'U1': jax.random.normal(ks[1], (D_MODEL, RANK), dtype=jnp.float32) * 0.02, 'V1': jax.random.normal(ks[2], (RANK, D_FF), dtype=jnp.float32) * 0.02, 'b1': jnp.zeros((D_FF,), dtype=jnp.float32), 'U2': jax.random.normal(ks[3], (D_FF, RANK), dtype=jnp.float32) * 0.02, 'V2': jax.random.normal(ks[4], (RANK, D_MODEL), dtype=jnp.float32) * 0.02, 'b2': jnp.zeros((D_MODEL,), dtype=jnp.float32)}
    _L1_ffn_all = _L1_ffn_setup()
    _L1_ffn_in = {k: v for k, v in _L1_ffn_all.items() if k in ('U1', 'V1', 'b1', 'U2', 'V2', 'b2')}
    del _L1_ffn_all
    return {'x': x, 'ctx_768': ctx_768, 'mask_BxS2_bk0': mask_BxS2_bk0, 'L0_attn_in_proj_w': _L0_attn_in['in_proj_w'], 'L0_attn_conv_w': _L0_attn_in['conv_w'], 'L0_attn_conv_b': _L0_attn_in['conv_b'], 'L0_attn_x_proj_w': _L0_attn_in['x_proj_w'], 'L0_attn_dt_proj_w': _L0_attn_in['dt_proj_w'], 'L0_attn_dt_proj_b': _L0_attn_in['dt_proj_b'], 'L0_attn_A_log': _L0_attn_in['A_log'], 'L0_attn_D': _L0_attn_in['D'], 'L0_attn_conv_w_b': _L0_attn_in['conv_w_b'], 'L0_attn_conv_b_b': _L0_attn_in['conv_b_b'], 'L0_attn_x_proj_w_b': _L0_attn_in['x_proj_w_b'], 'L0_attn_dt_proj_w_b': _L0_attn_in['dt_proj_w_b'], 'L0_attn_dt_proj_b_b': _L0_attn_in['dt_proj_b_b'], 'L0_attn_A_b_log': _L0_attn_in['A_b_log'], 'L0_attn_D_b': _L0_attn_in['D_b'], 'L0_attn_out_proj_w': _L0_attn_in['out_proj_w'], 'L0_xattn_ln1_g': _L0_xattn_in['ln1_g'], 'L0_xattn_ln1_b': _L0_xattn_in['ln1_b'], 'L0_xattn_ln2_g': _L0_xattn_in['ln2_g'], 'L0_xattn_ln2_b': _L0_xattn_in['ln2_b'], 'L0_xattn_Wq': _L0_xattn_in['Wq'], 'L0_xattn_bq': _L0_xattn_in['bq'], 'L0_xattn_Wk': _L0_xattn_in['Wk'], 'L0_xattn_bk': _L0_xattn_in['bk'], 'L0_xattn_Wv': _L0_xattn_in['Wv'], 'L0_xattn_bv': _L0_xattn_in['bv'], 'L0_xattn_Wo': _L0_xattn_in['Wo'], 'L0_xattn_bo': _L0_xattn_in['bo'], 'L0_ffn_weight': _L0_ffn_in['weight'], 'L1_attn_W_DQ': _L1_attn_in['W_DQ'], 'L1_attn_b_DQ': _L1_attn_in['b_DQ'], 'L1_attn_W_UQ': _L1_attn_in['W_UQ'], 'L1_attn_b_UQ': _L1_attn_in['b_UQ'], 'L1_attn_W_DKV': _L1_attn_in['W_DKV'], 'L1_attn_b_DKV': _L1_attn_in['b_DKV'], 'L1_attn_W_UK': _L1_attn_in['W_UK'], 'L1_attn_b_UK': _L1_attn_in['b_UK'], 'L1_attn_W_UV': _L1_attn_in['W_UV'], 'L1_attn_b_UV': _L1_attn_in['b_UV'], 'L1_attn_W_QR': _L1_attn_in['W_QR'], 'L1_attn_b_QR': _L1_attn_in['b_QR'], 'L1_attn_W_KR': _L1_attn_in['W_KR'], 'L1_attn_b_KR': _L1_attn_in['b_KR'], 'L1_attn_W_O': _L1_attn_in['W_O'], 'L1_attn_b_O': _L1_attn_in['b_O'], 'L1_xattn_ln_x_g': _L1_xattn_in['ln_x_g'], 'L1_xattn_ln_x_b': _L1_xattn_in['ln_x_b'], 'L1_xattn_ln_l_g': _L1_xattn_in['ln_l_g'], 'L1_xattn_ln_l_b': _L1_xattn_in['ln_l_b'], 'L1_xattn_qn_g': _L1_xattn_in['qn_g'], 'L1_xattn_kn_g': _L1_xattn_in['kn_g'], 'L1_xattn_Wq': _L1_xattn_in['Wq'], 'L1_xattn_Wkv': _L1_xattn_in['Wkv'], 'L1_xattn_Wlkv': _L1_xattn_in['Wlkv'], 'L1_xattn_Wo': _L1_xattn_in['Wo'], 'L1_xattn_bo': _L1_xattn_in['bo'], 'L1_ffn_U1': _L1_ffn_in['U1'], 'L1_ffn_V1': _L1_ffn_in['V1'], 'L1_ffn_b1': _L1_ffn_in['b1'], 'L1_ffn_U2': _L1_ffn_in['U2'], 'L1_ffn_V2': _L1_ffn_in['V2'], 'L1_ffn_b2': _L1_ffn_in['b2']}

def reference(x, ctx_768, mask_BxS2_bk0, L0_attn_in_proj_w, L0_attn_conv_w, L0_attn_conv_b, L0_attn_x_proj_w, L0_attn_dt_proj_w, L0_attn_dt_proj_b, L0_attn_A_log, L0_attn_D, L0_attn_conv_w_b, L0_attn_conv_b_b, L0_attn_x_proj_w_b, L0_attn_dt_proj_w_b, L0_attn_dt_proj_b_b, L0_attn_A_b_log, L0_attn_D_b, L0_attn_out_proj_w, L0_xattn_ln1_g, L0_xattn_ln1_b, L0_xattn_ln2_g, L0_xattn_ln2_b, L0_xattn_Wq, L0_xattn_bq, L0_xattn_Wk, L0_xattn_bk, L0_xattn_Wv, L0_xattn_bv, L0_xattn_Wo, L0_xattn_bo, L0_ffn_weight, L1_attn_W_DQ, L1_attn_b_DQ, L1_attn_W_UQ, L1_attn_b_UQ, L1_attn_W_DKV, L1_attn_b_DKV, L1_attn_W_UK, L1_attn_b_UK, L1_attn_W_UV, L1_attn_b_UV, L1_attn_W_QR, L1_attn_b_QR, L1_attn_W_KR, L1_attn_b_KR, L1_attn_W_O, L1_attn_b_O, L1_xattn_ln_x_g, L1_xattn_ln_x_b, L1_xattn_ln_l_g, L1_xattn_ln_l_b, L1_xattn_qn_g, L1_xattn_kn_g, L1_xattn_Wq, L1_xattn_Wkv, L1_xattn_Wlkv, L1_xattn_Wo, L1_xattn_bo, L1_ffn_U1, L1_ffn_V1, L1_ffn_b1, L1_ffn_U2, L1_ffn_V2, L1_ffn_b2):
    import jax
    import jax.numpy as jnp

    def _L0_attn_ref(hidden_states, in_proj_w, conv_w, conv_b, x_proj_w, dt_proj_w, dt_proj_b, A_log, D, conv_w_b, conv_b_b, x_proj_w_b, dt_proj_w_b, dt_proj_b_b, A_b_log, D_b, out_proj_w):
        import jax, jax.numpy as jnp
        import numpy as np
        D_MODEL = 256
        D_STATE = 16
        D_CONV = 4
        EXPAND = 2
        D_INNER = EXPAND * D_MODEL
        DT_RANK = 64
        B = 2
        L = 256

        def _dir_params(key):
            k1, k2, k3, k4 = jax.random.split(key, 4)
            conv_w = (jax.random.normal(k1, (D_INNER, D_CONV)) * D_CONV ** (-0.5)).astype(jnp.float32)
            conv_b = jnp.zeros((D_INNER,), jnp.float32)
            x_proj_w = (jax.random.normal(k2, (DT_RANK + 2 * D_STATE, D_INNER)) * D_INNER ** (-0.5)).astype(jnp.float32)
            dt_std = DT_RANK ** (-0.5)
            dt_w = jax.random.uniform(k3, (D_INNER, DT_RANK), minval=-dt_std, maxval=dt_std).astype(jnp.float32)
            dt = jnp.exp(jax.random.uniform(k4, (D_INNER,)) * (np.log(0.1) - np.log(0.001)) + np.log(0.001))
            dt = jnp.clip(dt, 0.0001)
            dt_b = (dt + jnp.log(-jnp.expm1(-dt))).astype(jnp.float32)
            A_log = jnp.log(jnp.tile(jnp.arange(1, D_STATE + 1, dtype=jnp.float32)[None, :], (D_INNER, 1)))
            Dp = jnp.ones((D_INNER,), jnp.float32)
            return (conv_w, conv_b, x_proj_w, dt_w, dt_b, A_log, Dp)

        def _causal_conv(x, w, b):
            y = jax.lax.conv_general_dilated(x, w[:, None, :], window_strides=(1,), padding=[(w.shape[1] - 1, 0)], dimension_numbers=('NCH', 'OIH', 'NCH'), feature_group_count=x.shape[1])
            return y + b[None, :, None]

        def _mamba_inner(xz, conv_w, conv_b, x_proj_w, dt_w, dt_b, A_log, Dp):
            x, z = jnp.split(xz, 2, axis=1)
            x = jax.nn.silu(_causal_conv(x, conv_w, conv_b))
            x_dbl = jnp.einsum('bdl,ed->bel', x, x_proj_w)
            dtr = x_dbl[:, :DT_RANK]
            Bm = x_dbl[:, DT_RANK:DT_RANK + D_STATE]
            Cm = x_dbl[:, DT_RANK + D_STATE:]
            delta = jax.nn.softplus(jnp.einsum('brl,dr->bdl', dtr, dt_w) + dt_b[None, :, None])
            A = -jnp.exp(A_log)
            dA = jnp.exp(jnp.einsum('bdl,dn->lbdn', delta, A))
            dBu = jnp.einsum('bdl,bnl,bdl->lbdn', delta, Bm, x)
            Ct = jnp.transpose(Cm, (2, 0, 1))

            def step(h, inp):
                dA_l, dBu_l, C_l = inp
                h = dA_l * h + dBu_l
                return (h, jnp.einsum('bdn,bn->bd', h, C_l))
            h0 = jnp.zeros((x.shape[0], D_INNER, D_STATE), x.dtype)
            _, ys = jax.lax.scan(step, h0, (dA, dBu, Ct))
            y = jnp.transpose(ys, (1, 2, 0)) + x * Dp[None, :, None]
            return y * jax.nn.silu(z)
        xz = jnp.einsum('bld,ed->bel', hidden_states, in_proj_w)
        out_f = _mamba_inner(xz, conv_w, conv_b, x_proj_w, dt_proj_w, dt_proj_b, A_log, D)
        out_b = _mamba_inner(xz[..., ::-1], conv_w_b, conv_b_b, x_proj_w_b, dt_proj_w_b, dt_proj_b_b, A_b_log, D_b)
        out = (out_f + out_b[..., ::-1]) / 2
        return jnp.einsum('bdl,od->blo', out, out_proj_w)

    def _L0_xattn_ref(modality1, modality2, ln1_g, ln1_b, ln2_g, ln2_b, Wq, bq, Wk, bk, Wv, bv, Wo, bo):
        import jax, jax.numpy as jnp
        import numpy as np
        EPS = 1e-05

        def layernorm(x, g, b):
            mu = jnp.mean(x, axis=-1, keepdims=True)
            var = jnp.mean(jnp.square(x - mu), axis=-1, keepdims=True)
            return (x - mu) * jax.lax.rsqrt(var + EPS) * g + b
        E = Wq.shape[1]
        scaling = E ** (-0.5)
        x1 = layernorm(modality1, ln1_g, ln1_b)
        x2 = layernorm(modality2, ln2_g, ln2_b)
        q = x1 @ Wq + bq
        k = x2 @ Wk + bk
        v = x2 @ Wv + bv
        scores = jnp.einsum('bqe,bke->bqk', q, k) * scaling
        attn = jax.nn.softmax(scores, axis=-1)
        ctx = jnp.einsum('bqk,bke->bqe', attn, v)
        return ctx @ Wo + bo

    def _L0_ffn_ref(x, weight):
        import jax, jax.numpy as jnp
        import numpy as np
        EPS = 1e-05

        @jax.custom_vjp
        def ste_quantize(w):
            scale = jnp.maximum(jnp.mean(jnp.abs(w)), EPS)
            return jnp.clip(jnp.round(w / scale), -1.0, 1.0)

        def _ste_fwd(w):
            return (ste_quantize(w), None)

        def _ste_bwd(_, g):
            return (g,)
        ste_quantize.defvjp(_ste_fwd, _ste_bwd)
        w_ternary = ste_quantize(weight)
        scale = jnp.maximum(jnp.mean(jnp.abs(weight)), EPS)
        return jnp.einsum('bsi,oi->bso', x, w_ternary * scale)

    def _L1_attn_ref(h_t, W_DQ, b_DQ, W_UQ, b_UQ, W_DKV, b_DKV, W_UK, b_UK, W_UV, b_UV, W_QR, b_QR, W_KR, b_KR, W_O, b_O):
        import jax, jax.numpy as jnp
        import numpy as np
        import math
        D_MODEL, N_HEADS, D_K, D_C, D_HR = (256, 8, 128, 32, 32)
        B, S = (4, 512)
        b, s, _ = h_t.shape
        c_q = h_t @ W_DQ + b_DQ
        c_kv = h_t @ W_DKV + b_DKV
        q_c = (c_q @ W_UQ + b_UQ).reshape(b, s, N_HEADS, D_K).transpose(0, 2, 1, 3)
        k_c = (c_kv @ W_UK + b_UK).reshape(b, s, N_HEADS, D_K).transpose(0, 2, 1, 3)
        v_c = (c_kv @ W_UV + b_UV).reshape(b, s, N_HEADS, D_K).transpose(0, 2, 1, 3)
        q_r = (c_q @ W_QR + b_QR).reshape(b, s, N_HEADS, D_HR).transpose(0, 2, 1, 3)
        k_r = (h_t @ W_KR + b_KR)[:, None, :, :]
        k_r = jnp.broadcast_to(k_r, (b, N_HEADS, s, D_HR))
        q = jnp.concatenate([q_c, q_r], axis=-1)
        k = jnp.concatenate([k_c, k_r], axis=-1)
        scale = 1.0 / math.sqrt(D_K + D_HR)
        scores = jnp.einsum('bhsd,bhtd->bhst', q, k) * scale
        attn = jax.nn.softmax(scores, axis=-1)
        o = jnp.einsum('bhst,bhtd->bhsd', attn, v_c)
        o = o.transpose(0, 2, 1, 3).reshape(b, s, N_HEADS * D_K)
        return o @ W_O + b_O

    def _L1_xattn_ref(x, latents, mask, ln_x_g, ln_x_b, ln_l_g, ln_l_b, qn_g, kn_g, Wq, Wkv, Wlkv, Wo, bo):
        import jax, jax.numpy as jnp
        import numpy as np
        DIM_IN, DIM_LAT, DIM_HEAD = (192, 256, 64)
        INNER = max(DIM_LAT, DIM_IN)
        HEADS = INNER // DIM_HEAD
        SCALE = DIM_HEAD ** (-0.5)
        RMS_EPS = 1e-08
        LN_EPS = 1e-05

        def layernorm(x, g, b):
            mu = jnp.mean(x, axis=-1, keepdims=True)
            var = jnp.mean((x - mu) ** 2, axis=-1, keepdims=True)
            return (x - mu) * jax.lax.rsqrt(var + LN_EPS) * g + b

        def rmsnorm(x, gamma):
            norm = jnp.sqrt(jnp.sum(x * x, axis=-1, keepdims=True)) * x.shape[-1] ** (-0.5)
            return x / jnp.maximum(norm, RMS_EPS) * gamma
        b, n, _ = x.shape
        m = latents.shape[1]
        xn = layernorm(x, ln_x_g, ln_x_b)
        ln = layernorm(latents, ln_l_g, ln_l_b)
        q = ln @ Wq.T
        kv = jnp.concatenate([xn @ Wkv.T, ln @ Wlkv.T], axis=1)
        k, v = (kv[..., :INNER], kv[..., INNER:])
        split_heads = lambda t: t.reshape(t.shape[0], t.shape[1], HEADS, DIM_HEAD).transpose(0, 2, 1, 3)
        q, k, v = (split_heads(q), split_heads(k), split_heads(v))
        qn = rmsnorm(q, qn_g) * SCALE
        kn = rmsnorm(k, kn_g)
        attn = jnp.einsum('bhid,bhjd->bhij', qn, kn)
        full_mask = jnp.pad(mask, ((0, 0), (0, m)), constant_values=True)
        attn = jnp.where(full_mask[:, None, None, :], attn, -jnp.finfo(attn.dtype).max)
        attn = jax.nn.softmax(attn, axis=-1)
        out = jnp.einsum('bhij,bhjd->bhid', attn, v)
        out = out.transpose(0, 2, 1, 3).reshape(b, m, INNER)
        return out @ Wo.T + bo

    def _L1_ffn_ref(x, U1, V1, b1, U2, V2, b2):
        import jax, jax.numpy as jnp
        import numpy as np
        D_MODEL, D_FF, RANK = (256, 1024, 64)
        B, S = (4, 1024)
        P = jnp.einsum('bsd,dr->bsr', x, U1)
        H = jax.nn.gelu(jnp.einsum('bsr,rf->bsf', P, V1) + b1)
        Q = jnp.einsum('bsf,fr->bsr', H, U2)
        return jnp.einsum('bsr,rd->bsd', Q, V2) + b2
    x = x + _L0_attn_ref(_layernorm(x, axis=-1), L0_attn_in_proj_w, L0_attn_conv_w, L0_attn_conv_b, L0_attn_x_proj_w, L0_attn_dt_proj_w, L0_attn_dt_proj_b, L0_attn_A_log, L0_attn_D, L0_attn_conv_w_b, L0_attn_conv_b_b, L0_attn_x_proj_w_b, L0_attn_dt_proj_w_b, L0_attn_dt_proj_b_b, L0_attn_A_b_log, L0_attn_D_b, L0_attn_out_proj_w)
    x = x + _L0_xattn_ref(_layernorm(x, axis=-1), ctx_768, L0_xattn_ln1_g, L0_xattn_ln1_b, L0_xattn_ln2_g, L0_xattn_ln2_b, L0_xattn_Wq, L0_xattn_bq, L0_xattn_Wk, L0_xattn_bk, L0_xattn_Wv, L0_xattn_bv, L0_xattn_Wo, L0_xattn_bo)
    x = x + _L0_ffn_ref(_layernorm(x, axis=-1), L0_ffn_weight)
    x = x + _L1_attn_ref(_layernorm(x, axis=-1), L1_attn_W_DQ, L1_attn_b_DQ, L1_attn_W_UQ, L1_attn_b_UQ, L1_attn_W_DKV, L1_attn_b_DKV, L1_attn_W_UK, L1_attn_b_UK, L1_attn_W_UV, L1_attn_b_UV, L1_attn_W_QR, L1_attn_b_QR, L1_attn_W_KR, L1_attn_b_KR, L1_attn_W_O, L1_attn_b_O)
    x = x + _L1_xattn_ref(ctx_768, _layernorm(x, axis=-1), mask_BxS2_bk0, L1_xattn_ln_x_g, L1_xattn_ln_x_b, L1_xattn_ln_l_g, L1_xattn_ln_l_b, L1_xattn_qn_g, L1_xattn_kn_g, L1_xattn_Wq, L1_xattn_Wkv, L1_xattn_Wlkv, L1_xattn_Wo, L1_xattn_bo)
    x = x + _L1_ffn_ref(_layernorm(x, axis=-1), L1_ffn_U1, L1_ffn_V1, L1_ffn_b1, L1_ffn_U2, L1_ffn_V2, L1_ffn_b2)
    return x

_drawn_inputs = setup_inputs


def setup_inputs(seed=0):
    import zlib

    import numpy as np

    out = dict(_drawn_inputs(seed))
    spreads = {'L0_attn_conv_b': (0.0, 0.428),
     'L0_attn_D': (1.0, 0.2),
     'L0_attn_conv_b_b': (0.0, 0.459),
     'L0_attn_D_b': (1.0, 0.2),
     'L0_xattn_ln1_g': (1.0, 0.2),
     'L0_xattn_ln1_b': (0.0, 0.389),
     'L0_xattn_ln2_g': (1.0, 0.2),
     'L0_xattn_ln2_b': (0.0, 0.1),
     'L1_xattn_ln_x_g': (1.0, 0.6),
     'L1_xattn_ln_x_b': (0.0, 0.711),
     'L1_xattn_ln_l_g': (1.0, 0.2),
     'L1_xattn_ln_l_b': (0.0, 0.1),
     'L1_xattn_qn_g': (1.0, 0.6),
     'L1_xattn_kn_g': (1.0, 0.6),
     'L1_xattn_bo': (0.0, 0.1),
     'L1_ffn_b1': (0.0, 0.8),
     'L1_ffn_b2': (0.0, 0.8)}
    factors = {'L0_attn_dt_proj_w': 5.681,
     'L0_attn_dt_proj_b': 3.648,
     'L0_attn_A_log': 4.406,
     'L0_attn_dt_proj_w_b': 6.93,
     'L0_attn_dt_proj_b_b': 4.293,
     'L0_attn_A_b_log': 5.517,
     'L0_xattn_bq': 25.25,
     'L0_xattn_bk': 64.0,
     'L0_xattn_bv': 5.91,
     'L0_xattn_bo': 5.655,
     'L1_attn_W_DQ': 8.0,
     'L1_attn_b_DQ': 8.0,
     'L1_attn_W_UQ': 8.0,
     'L1_attn_b_UQ': 8.0,
     'L1_attn_b_DKV': 5.548,
     'L1_attn_W_UK': 8.0,
     'L1_attn_b_UK': 64.0,
     'L1_attn_W_QR': 8.0,
     'L1_attn_b_QR': 22.765,
     'L1_attn_W_KR': 8.0,
     'L1_attn_b_KR': 64.0,
     'L1_attn_b_O': 3.185,
     'L1_ffn_U1': 8.0,
     'L1_ffn_V1': 8.0,
     'L1_ffn_U2': 8.0,
     'L1_ffn_V2': 8.0}
    for name, (base, spread) in spreads.items():
        noise = np.random.default_rng([zlib.crc32(name.encode()), seed]).standard_normal(out[name].shape)
        drawn = base * np.exp(spread * noise) if base else spread * noise
        out[name] = jnp.asarray(drawn.astype(out[name].dtype))
    for name, factor in factors.items():
        out[name] = (out[name] * factor).astype(out[name].dtype)
    return out
```

```python
from contextlib import ExitStack

import concourse.bass as bass
from concourse import mybir

F32 = mybir.dt.float32
U8 = mybir.dt.uint8
ALU = mybir.AluOpType
ACT = mybir.ActivationFunctionType
AX_X = mybir.AxisListType.X

P = 128
NBATCH, SEQ, DM = 8, 256, 256
TILES = NBATCH * SEQ // P
EPS = 1e-5

DIN, NSTATE, TAPS, RANK = 512, 16, 4, 64
CH = DIN // P
HALVES = 2
HB = NBATCH // HALVES
HT = HB * SEQ
HTILES = HT // P
PAD = TAPS - 1
ROW = PAD + SEQ + PAD
BANK = 512
XD = RANK + 2 * NSTATE

C_CONVW, C_CONVB, C_DTB, C_D, C_ALOG = 0, CH * TAPS, CH * TAPS + CH, CH * TAPS + 2 * CH, CH * TAPS + 3 * CH
NCOLS = C_ALOG + CH * NSTATE


def mamba_block(nc, dram, x_sb, ident):
    with ExitStack() as ctx:
        def sb(name, shape, dt=F32):
            return ctx.enter_context(nc.sbuf_tensor(name, shape, dt))

        def sem(name):
            return ctx.enter_context(nc.semaphore(name))

        in_w = sb("in_w", [P, 2, 2 * DIN])
        xp_w = sb("xp_w", [P, 2, CH, XD])
        dt_w = sb("dt_w", [RANK, 2, DIN])
        out_w = sb("out_w", [P, CH, DM])
        cols = sb("cols", [P, 2, NCOLS])
        a_neg = sb("a_neg", [P, 2, CH * NSTATE])
        a_exp = sb("a_exp", [P, 2, CH * NSTATE])
        d_diag = sb("d_diag", [P, 2, CH, P])
        pow_c = sb("pow_c", [P, 2, HTILES])

        stats = sb("stats", [P, HTILES, 6])
        meanvar = sb("meanvar", [P, HTILES, 2])
        rider = sb("rider", [P, 1])
        vareps = sb("vareps", [P, HTILES])
        rstd = sb("rstd", [P, HTILES])
        work = sb("work", [P, CH, HT])
        normed = work[:, 0:2, :].rearrange("p a (t d) -> p (a t) d", d=DM)
        norm_t = sb("norm_t", [P, 2, HT])
        xpad = sb("xpad", [P, CH, HB, ROW])
        gate = sb("gate", [P, CH, HT])
        xc = sb("xc", [P, CH, HT])
        delta = work
        gated = work
        du = sb("du", [P, CH, HT])
        xdbl = sb("xdbl", [XD, HT])
        bc = sb("bc", [P, 2, 2, HT])
        decay = sb("decay", [P, 2, HT])
        inject = sb("inject", [P, 2, HT])
        state = sb("state", [P, 2, HT])
        readout = sb("readout", [P, 2, HT])
        y_tail = sb("y_tail", [P, 2, HT])
        y_fwd = [norm_t[:, 0, :], norm_t[:, 1, :], y_tail[:, 0, :], y_tail[:, 1, :]]
        psum = ctx.enter_context(nc.psum_tensor("mamba_psum", [P, CH, 2 * BANK], F32))
        bc_dram = nc.dram_tensor("bc_rows", [2, 2 * NSTATE, HT], F32, kind="Internal").ap()

        names = """x_loaded w_loaded pads_zero consts_set a_exped a_ready diag_ready stats_done mean_ready
            vareps_ready rstd_ready norm_ready tr_ready norm_t_ready inproj_ready inproj_read xpad_ready
            conv_first conv_step conv_sum_ready xc_ready xproj_ready xdbl_ready bc_stored bc_even bc_odd
            dtproj_ready sp_abs sp_exp sp_w sp_ln sp_corr sp_sum sp_relu delta_ready du_ready
            strip_and_scan decay_ready inject_ready readout_ready y_added y_saved y_summed gated_ready
            outproj_ready x_updated""".split()
        s = {n: sem(n) for n in names}
        bc_loaded = [s["bc_even"], s["bc_odd"]]
        sums = [psum[:, c, :] for c in range(CH)]
        banks = psum[:, :, :].rearrange("p c n -> p (c n)")

        block = ctx.enter_context(nc.Block())

        def direction(hf, d):
            return hf * 2 + d

        @block.sync
        def _(sp):
            sp.dma_start(x_sb[:, :, :], dram["x"].rearrange("(t p) d -> p t d", p=P)).then_inc(s["x_loaded"], 16)
            sp.dma_start(ident[:, :], dram["ident"]).then_inc(s["w_loaded"], 16)
            sp.dma_start(cols[:, :, :], dram["mamba_cols"]).then_inc(s["w_loaded"], 16)
            sp.dma_start(in_w[:, :, :], dram["in_w"].rearrange("(c p) n -> p c n", p=P)).then_inc(s["w_loaded"], 16)
            sp.dma_start(xp_w[:, :, :, :], dram["xp_w"].rearrange("d (c p) n -> p d c n", p=P)).then_inc(s["w_loaded"], 16)
            sp.dma_start(dt_w[:, :, :], dram["dt_w"].rearrange("d p n -> p d n")).then_inc(s["w_loaded"], 16)
            sp.dma_start(out_w[:, :, :], dram["out_w"].rearrange("(c p) n -> p c n", p=P)).then_inc(s["w_loaded"], 16)

            def load_bc(slot, d, n):
                rows = bc_dram[d].rearrange("(k n) t -> n k t", k=2)
                src = rows[bass.ds(n, 1)].partition_broadcast(P) if not isinstance(n, int) else rows[n:n + 1].partition_broadcast(P)
                src = src.rearrange("p a k t -> p (a k) t")
                sp.dma_start(bc[:, slot, :, :], src).then_inc(bc_loaded[slot], 16)

            with sp.Fori(0, HALVES) as hf:
                for d in range(2):
                    sp.wait_ge(s["xdbl_ready"], direction(hf, d) * 2 + 2)
                    sp.dma_start(bc_dram[d], xdbl[RANK:XD, :]).then_inc(s["bc_stored"], 16)
                    sp.wait_ge(s["bc_stored"], direction(hf, d) * 16 + 16)
                    load_bc(0, d, 0)
                    load_bc(1, d, 1)
                    with sp.Fori(0, NSTATE // 2 - 1) as j:
                        for k in range(2):
                            sp.wait_ge(s["readout_ready"],
                                       direction(hf, d) * (NSTATE * CH) + j * (2 * CH) + (k + 1) * CH)
                            load_bc(k, d, j * 2 + (2 + k))

        @block.gpsimd
        def _(pool):
            pool.memset(pow_c[:, 0, :], EPS).then_inc(s["consts_set"], 1)
            pool.memset(pow_c[:, 1, :], -0.5).then_inc(s["consts_set"], 1)
            pool.memset(xpad[:, :, :, 0:PAD], 0.0).then_inc(s["pads_zero"], 1)
            pool.memset(xpad[:, :, :, PAD + SEQ:ROW], 0.0).then_inc(s["pads_zero"], 1)
            pool.wait_ge(s["consts_set"], 2)
            with pool.Fori(0, HALVES) as hf:
                pool.wait_ge(s["mean_ready"], hf * HTILES + HTILES)
                pool.tensor_tensor(vareps[:, :], meanvar[:, :, 1], pow_c[:, 0, :], ALU.add).then_inc(s["vareps_ready"], 1)
                pool.wait_ge(s["vareps_ready"], hf + 1)
                pool.tensor_tensor(rstd[:, :], vareps[:, :], pow_c[:, 1, :], ALU.pow).then_inc(s["rstd_ready"], 1)
                for d in range(2):
                    dirs = direction(hf, d)
                    for c in range(CH):
                        pool.wait_ge(s["delta_ready"], dirs * CH + c + 1)
                        pool.tensor_tensor(du[:, c, :], delta[:, c, :], xc[:, c, :], ALU.mult).then_inc(s["du_ready"], 1)
                    with pool.Fori(0, NSTATE // 2) as j:
                        for k in range(2):
                            pool.wait_ge(s["du_ready"], dirs * CH + CH)
                            pool.wait_ge(bc_loaded[k], dirs * (8 * NSTATE) + j * 16 + 16)
                            for c in range(CH):
                                step = k * CH + c
                                pool.wait_ge(s["strip_and_scan"], dirs * (NSTATE * CH + 2) + j * (2 * CH) + step + 1)
                                pool.tensor_tensor(inject[:, c % 2, :], du[:, c, :], bc[:, k, 0, :], ALU.mult).then_inc(s["inject_ready"], 1)

        @block.scalar
        def _(act):
            act.wait_ge(s["w_loaded"], 96)
            act.activation(a_exp[:, :, :], cols[:, :, C_ALOG:NCOLS], ACT.Exp).then_inc(s["a_exped"], 1)
            with act.Fori(0, HALVES) as hf:
                act.wait_ge(s["tr_ready"], hf * 2 + 2)
                act.activation(norm_t[:, 1, :], sums[1], ACT.Copy).then_inc(s["norm_t_ready"], 1)
                for m in range(2 * CH):
                    act.wait_ge(s["inproj_ready"], hf * (2 * CH) + m + 1)
                    if m < CH:
                        act.activation(xpad[:, m, :, PAD:PAD + SEQ],
                                       sums[m % CH].rearrange("p (b l) -> p b l", b=HB), ACT.Copy).then_inc(s["inproj_read"], 1)
                    else:
                        act.activation(gate[:, m - CH, :], sums[m % CH], ACT.Silu).then_inc(s["inproj_read"], 1)
                for d in range(2):
                    dirs = direction(hf, d)
                    if d:
                        act.wait_ge(s["readout_ready"], dirs * (NSTATE * CH))
                    act.wait_ge(s["inproj_read"], hf * (2 * CH) + CH)
                    act.wait_ge(s["pads_zero"], 2)
                    for c in range(CH):
                        at = PAD * 2 if d else 0
                        act.activation(xc[:, c, :].rearrange("p (b l) -> p b l", b=HB), xpad[:, c, :, at:at + SEQ],
                                       ACT.Identity, bias=cols[:, d, C_CONVB + c:C_CONVB + c + 1],
                                       scale=cols[:, d, C_CONVW + TAPS * c:C_CONVW + TAPS * c + 1]).then_inc(s["conv_first"], 1)
                    for c in range(CH):
                        act.wait_ge(s["conv_sum_ready"], dirs * CH + c + 1)
                        act.activation(xc[:, c, :], xc[:, c, :], ACT.Silu).then_inc(s["xc_ready"], 1)
                    for b in range(2):
                        act.wait_ge(s["xproj_ready"], dirs * 2 + b + 1)
                        act.activation(xdbl[:, b * BANK:(b + 1) * BANK], sums[0][0:XD, b * BANK:(b + 1) * BANK],
                                       ACT.Copy).then_inc(s["xdbl_ready"], 1)
                    for c in range(CH):
                        act.wait_ge(s["dtproj_ready"], dirs * CH + c + 1)
                        if c >= 2:
                            act.wait_ge(s["delta_ready"], dirs * CH + c - 1)
                        act.activation(decay[:, c % 2, :], sums[c], ACT.Abs,
                                       bias=cols[:, d, C_DTB + c:C_DTB + c + 1]).then_inc(s["sp_abs"], 1)
                        act.wait_ge(s["sp_abs"], dirs * CH + c + 1)
                        act.activation(inject[:, c % 2, :], decay[:, c % 2, :], ACT.Exp, scale=-1.0).then_inc(s["sp_exp"], 1)
                        act.wait_ge(s["sp_exp"], dirs * CH + c + 1)
                        act.activation(state[:, c % 2, :], inject[:, c % 2, :], ACT.Ln, bias=1.0).then_inc(s["sp_ln"], 1)
                    act.wait_ge(s["a_ready"], 1)
                    act.wait_ge(s["delta_ready"], dirs * CH + CH)
                    lo, hi = (1, SEQ) if d == 0 else (0, SEQ - 1)
                    with act.Fori(0, NSTATE // 2) as j:
                        for k in range(2):
                            for c in range(CH):
                                step = k * CH + c
                                act.wait_ge(s["strip_and_scan"], dirs * (NSTATE * CH + 2) + j * (2 * CH) + step + 1)
                                act.activation(decay[:, c % 2, :].rearrange("p (b l) -> p b l", b=HB)[:, :, lo:hi],
                                               delta[:, c, :].rearrange("p (b l) -> p b l", b=HB)[:, :, lo:hi],
                                               ACT.Exp, scale=a_neg[:, d, bass.ds(j * 2 + (c * NSTATE + k), 1)]).then_inc(s["decay_ready"], 1)
                    if d == 0:
                        act.wait_ge(s["y_added"], hf * (2 * NSTATE * CH + 4) + (NSTATE * CH + 2))
                        for c in range(CH):
                            act.activation(y_fwd[c], sums[c], ACT.Copy, scale=0.5).then_inc(s["y_saved"], 1)

        @block.tensor
        def _(pe):
            pe.wait_ge(s["w_loaded"], 96)
            pe.wait_ge(s["diag_ready"], 2 * CH)
            with pe.Fori(0, HALVES) as hf:
                for c in range(2):
                    for t in range(HTILES):
                        pe.wait_ge(s["norm_ready"], hf * HTILES + t + 1)
                        last = pe.transpose(sums[c][:, t * P:(t + 1) * P], normed[:, t, c * P:(c + 1) * P], ident[:, :])
                    last.then_inc(s["tr_ready"], 1)
                pe.wait_ge(s["norm_t_ready"], hf * 2 + 2)
                for m in range(2 * CH):
                    if m >= CH:
                        pe.wait_ge(s["inproj_read"], hf * (2 * CH) + m - CH + 1)
                    for b in range(2):
                        for c in range(2):
                            last = pe.matmul(sums[m % CH][:, b * BANK:(b + 1) * BANK], in_w[:, c, m * P:(m + 1) * P],
                                             norm_t[:, c, b * BANK:(b + 1) * BANK], start=c == 0, stop=c == 1)
                    last.then_inc(s["inproj_ready"], 1)
                for d in range(2):
                    dirs = direction(hf, d)
                    pe.wait_ge(s["xc_ready"], dirs * CH + CH)
                    pe.wait_ge(s["inproj_read"], hf * (2 * CH) + 2 * CH)
                    if d:
                        pe.wait_ge(s["y_saved"], hf * CH + CH)
                    for b in range(2):
                        for c in range(CH):
                            last = pe.matmul(sums[0][0:XD, b * BANK:(b + 1) * BANK], xp_w[:, d, c, :],
                                             xc[:, c, b * BANK:(b + 1) * BANK], start=c == 0, stop=c == CH - 1)
                        last.then_inc(s["xproj_ready"], 1)
                    pe.wait_ge(s["xdbl_ready"], dirs * 2 + 2)
                    for c in range(CH):
                        for b in range(2):
                            last = pe.matmul(sums[c][:, b * BANK:(b + 1) * BANK], dt_w[:, d, c * P:(c + 1) * P],
                                             xdbl[0:RANK, b * BANK:(b + 1) * BANK], start=True, stop=True)
                        last.then_inc(s["dtproj_ready"], 1)
                    for c in range(CH):
                        pe.wait_ge(s["sp_relu"], dirs * CH + c + 1)
                        for b in range(2):
                            last = pe.matmul(sums[c][:, b * BANK:(b + 1) * BANK], d_diag[:, d, c, :],
                                             xc[:, c, b * BANK:(b + 1) * BANK], start=True, stop=False, skip_group_check=True)
                        if c >= 2:
                            last.then_inc(s["y_added"], 1)
                    with pe.Fori(0, NSTATE // 2) as j:
                        for k in range(2):
                            for c in range(CH):
                                pe.wait_ge(s["readout_ready"], dirs * (NSTATE * CH) + j * (2 * CH) + k * CH + c + 1)
                                for b in range(2):
                                    last = pe.matmul(sums[c][:, b * BANK:(b + 1) * BANK], ident[:, :],
                                                     readout[:, c % 2, b * BANK:(b + 1) * BANK], start=False, stop=False, skip_group_check=True)
                                last.then_inc(s["y_added"], 1)
                pe.wait_ge(s["gated_ready"], hf * CH + CH)
                for t in range(HTILES):
                    dst = banks[:, t * DM:(t + 1) * DM]
                    for c in range(CH):
                        last = pe.matmul(dst, gated[:, c, t * P:(t + 1) * P], out_w[:, c, :], start=c == 0, stop=c == CH - 1)
                    if t % 4 == 3:
                        last.then_inc(s["outproj_ready"], 1)

        @block.vector
        def _(dve):
            dve.wait_ge(s["w_loaded"], 96)
            dve.wait_ge(s["a_exped"], 1)
            dve.tensor_scalar(a_neg[:, :, :], a_exp[:, :, :], -1.0, None, ALU.mult).then_inc(s["a_ready"], 1)
            for d in range(2):
                for c in range(CH):
                    dve.tensor_scalar(d_diag[:, d, c, :], ident[:, :], cols[:, d, C_D + c:C_D + c + 1], None,
                                      ALU.mult).then_inc(s["diag_ready"], 1)
            dve.wait_ge(s["x_loaded"], 16)
            with dve.Fori(0, HALVES) as hf:
                for t in range(HTILES):
                    dve.bn_stats(stats[:, t, :], x_sb[:, bass.ds(hf * HTILES + t, 1), :].rearrange("p a d -> p (a d)")).then_inc(s["stats_done"], 1)
                dve.wait_ge(s["stats_done"], hf * HTILES + HTILES)
                dve.memset(rider[:, :], 0.0)
                for t in range(HTILES):
                    dve.bn_aggr(meanvar[:, t, :], stats[:, t, :]).then_inc(s["mean_ready"], 1)
                dve.wait_ge(s["rstd_ready"], hf + 1)
                for t in range(HTILES):
                    dve.tensor_scalar(normed[:, t, :], x_sb[:, bass.ds(hf * HTILES + t, 1), :].rearrange("p a d -> p (a d)"),
                                      meanvar[:, t, 0:1], rstd[:, t:t + 1], ALU.subtract, ALU.mult).then_inc(s["norm_ready"], 1)
                dve.wait_ge(s["tr_ready"], hf * 2 + 1)
                dve.tensor_copy(norm_t[:, 0, :], sums[0]).then_inc(s["norm_t_ready"], 1)
                for d in range(2):
                    dirs = direction(hf, d)
                    for c in range(CH):
                        dve.wait_ge(s["conv_first"], dirs * CH + c + 1)
                        acc = xc[:, c, :].rearrange("p (b l) -> p b l", b=HB)
                        for k in range(1, TAPS):
                            at = PAD * 2 - k if d else k
                            if k > 1:
                                dve.wait_ge(s["conv_step"], dirs * (CH * 2) + c * 2 + k - 1)
                            w = cols[:, d, C_CONVW + TAPS * c + k:C_CONVW + TAPS * c + k + 1]
                            step = dve.scalar_tensor_tensor(out=acc, in0=xpad[:, c, :, at:at + SEQ], scalar=w, in1=acc,
                                                            op0=ALU.mult, op1=ALU.add)
                            step.then_inc(s["conv_sum_ready"] if k == TAPS - 1 else s["conv_step"], 1)
                    for c in range(CH):
                        dve.wait_ge(s["sp_exp"], dirs * CH + c + 1)
                        dve.tensor_scalar(readout[:, c % 2, :], inject[:, c % 2, :], 1.0, None, ALU.add).then_inc(s["sp_w"], 1)
                        dve.wait_ge(s["sp_w"], dirs * CH + c + 1)
                        dve.wait_ge(s["sp_ln"], dirs * CH + c + 1)
                        dve.scalar_tensor_tensor(out=inject[:, c % 2, :], in0=readout[:, c % 2, :], scalar=1.0,
                                                 in1=inject[:, c % 2, :], op0=ALU.subtract, op1=ALU.subtract).then_inc(s["sp_corr"], 1)
                        dve.tensor_scalar(delta[:, c, :], sums[c], cols[:, d, C_DTB + c:C_DTB + c + 1], 0.0,
                                          ALU.add, ALU.max).then_inc(s["sp_relu"], 1)
                        dve.wait_ge(s["sp_corr"], dirs * CH + c + 1)
                        dve.tensor_tensor(state[:, c % 2, :], state[:, c % 2, :], inject[:, c % 2, :], ALU.subtract).then_inc(s["sp_sum"], 1)
                        dve.wait_ge(s["sp_sum"], dirs * CH + c + 1)
                        dve.wait_ge(s["sp_relu"], dirs * CH + c + 1)
                        dve.tensor_tensor(delta[:, c, :], delta[:, c, :], state[:, c % 2, :], ALU.add).then_inc(s["delta_ready"], 1)
                    at = SEQ - 1 if d else 0
                    for k in range(2):
                        dve.memset(decay[:, k, :].rearrange("p (b l) -> p b l", b=HB)[:, :, at:at + 1], 0.0).then_inc(s["strip_and_scan"], 1)
                    with dve.Fori(0, NSTATE // 2) as j:
                        for k in range(2):
                            for c in range(CH):
                                step = k * CH + c
                                nth = dirs * (NSTATE * CH) + j * (2 * CH) + step
                                dve.wait_ge(s["decay_ready"], nth + 1)
                                dve.wait_ge(s["inject_ready"], nth + 1)
                                way = slice(None, None, -1) if d else slice(None)
                                dve.tensor_tensor_scan(state[:, c % 2, :][:, way], decay[:, c % 2, :][:, way],
                                                       inject[:, c % 2, :][:, way], 0.0, ALU.mult, ALU.add).then_inc(s["strip_and_scan"], 1)
                                dve.wait_ge(s["strip_and_scan"], dirs * (NSTATE * CH + 2) + j * (2 * CH) + step + 3)
                                dve.wait_ge(s["y_added"], dirs * (NSTATE * CH + 2) + j * (2 * CH) + step + 1)
                                dve.tensor_tensor(readout[:, c % 2, :], state[:, c % 2, :], bc[:, k, 1, :], ALU.mult).then_inc(s["readout_ready"], 1)
                dve.wait_ge(s["y_added"], hf * (2 * NSTATE * CH + 4) + (2 * NSTATE * CH + 4))
                for c in range(CH):
                    dve.scalar_tensor_tensor(out=gated[:, c, :], in0=sums[c], scalar=0.5, in1=y_fwd[c],
                                             op0=ALU.mult, op1=ALU.add).then_inc(s["y_summed"], 1)
                for c in range(CH):
                    dve.wait_ge(s["y_summed"], hf * CH + c + 1)
                    dve.tensor_tensor(gated[:, c, :], gated[:, c, :], gate[:, c, :], ALU.mult).then_inc(s["gated_ready"], 1)
                for g in range(HTILES // 4):
                    dve.wait_ge(s["outproj_ready"], hf * (HTILES // 4) + g + 1)
                    x_rows = x_sb[:, bass.ds(hf * HTILES + 4 * g, 4), :]
                    dve.tensor_tensor(x_rows, banks[:, g * 4 * DM:(g + 1) * 4 * DM].rearrange("p (t d) -> p t d", d=DM),
                                      x_rows, ALU.add).then_inc(s["x_updated"], 1)
                dve.wait_ge(s["x_updated"], hf * (HTILES // 4) + HTILES // 4)


SETUP = 16
PAIRS = NBATCH // 2
PT_, PTOK = 2 * SEQ // P, 2 * SEQ
DC = 192
CK = (P, DC - P)
E0 = 256
NH, DK, LAT, ROPE = 8, 128, 32, 32
KEYW = LAT + ROPE + 1
H4, DH = 4, 64
FF, LR = 1024, 64
FLT_MAX = 3.4028234663852886e38
QUADS = 8

COLS = {}
for _name, _n in (("ln2_g", 2), ("ln2_b", 2), ("lnx_g", 2), ("lnx_b", 2), ("ln1_g", 2), ("ln1_b", 2), ("lnl_g", 2),
                  ("lnl_b", 2), ("bq", 2), ("bk", 2), ("qn", 1), ("kn", 1), ("bdq", 1), ("bkv", 1), ("b1", 8), ("buv", 8)):
    COLS[_name] = (sum(n for _, n in COLS.values()), _n)
NLCOLS = sum(n for _, n in COLS.values())
ROWS = {"bv": 0, "bo0": DM, "bo": 2 * DM, "bo1": 3 * DM, "b2": 4 * DM, "bdkv": 5 * DM}
NROWS = 5 * DM + LAT

PER = {
    "stats": 24, "moments": 24, "pool_step": 16, "rstd": 6, "normed": 24, "turned": 12, "turned_act": 7, "turned_dve": 7,
    "k0_mm": 2, "k0_saved": 2, "v0_mm": 1, "v0_saved": 1, "k1c_mm": 1, "v1c_mm": 1, "v1c_saved": 1,
    "sq": 3, "ss": 3, "ms": 3, "rms": 3, "k1c_normed": 1, "k1c_turned": 2, "k1c_act": 1, "k1c_dve": 1,
    "q0_mm": 2, "q0_act": 1, "q0_dve": 1, "score0": 1, "max0": 1, "exp0": 4, "rinv0": 1, "p0_turned": 2, "p0_act": 1, "p0_dve": 1,
    "ctx0_mm": 2, "ctx0_act": 1, "ctx0_dve": 1, "out0_mm": 1, "x_biased": 4, "x_added": 8,
    "ffn0_mm": 1, "c_mm": 2, "cq_saved": 1, "kk_saved": 1, "ckvn_mm": 1, "ckvn_saved": 1,
    "head_mm": 8, "head_saved": 8, "scored": 16, "masked": 8, "maxed": 16, "pexp": 48, "p_turned": 16, "pt_saved": 16,
    "rinv": 16, "pv_mm": 16, "u_read": 16, "o_turned": 4, "o_act": 2, "o_dve": 2, "out1_mm": 2,
    "q1_mm": 1, "k1l_mm": 1, "v1l_mm": 1, "v1l_saved": 1, "q1_normed": 1, "k1l_normed": 1, "q1_turned": 2, "k1l_turned": 2,
    "q1_act": 1, "q1_dve": 1, "k1l_act": 1, "k1l_dve": 1,
    "p5_mm": 1, "p5_saved": 1, "h_mm": 8, "gelu": 8, "qt_mm": 1, "qt_saved": 1, "y_mm": 1,
}


def pexp_before(quad):
    return 4 * quad if quad <= QUADS else 4 * QUADS + 2 * (quad - QUADS)


def layers_block(nc, dram, x_sb, ident):
    with ExitStack() as ctx:
        def sb(name, shape, dt=F32):
            return ctx.enter_context(nc.sbuf_tensor(name, shape, dt))

        s = {n: ctx.enter_context(nc.semaphore(n)) for n in PER}
        s_in = ctx.enter_context(nc.semaphore("inputs_loaded"))
        s_out = ctx.enter_context(nc.semaphore("out_stored"))
        s_const = ctx.enter_context(nc.semaphore("pool_consts"))
        s_set = ctx.enter_context(nc.semaphore("setup_dve"))
        s_abs = ctx.enter_context(nc.semaphore("ternary_abs"))
        s_fold = ctx.enter_context(nc.semaphore("folds_mm"))

        wq0 = sb("wq0", [P, 2, E0])
        wk0 = sb("wk0", [P, 2, E0])
        wv0 = sb("wv0", [P, 2, E0])
        wo0 = sb("wo0", [P, 2, DM])
        wf = sb("wf", [P, 2, DM])
        w_dq = sb("w_dq", [P, 2, LAT])
        w_kv = sb("w_kv", [P, 2, LAT + ROPE])
        uq_t = sb("uq_t", [DK, NH, LAT + 1])
        uk_t = sb("uk_t", [DK, NH, LAT + 1])
        uv_t = sb("uv_t", [DK, NH, LAT])
        w_o = sb("w_o", [DK, NH, DM])
        fold_q = sb("fold_q", [LAT + 1, NH, KEYW])
        fold_v = sb("fold_v", [P, 2, DM])
        wq1 = sb("wq1", [P, 2, DM])
        wkv1 = sb("wkv1", [P, 2, 2 * DM])
        wlkv1 = sb("wlkv1", [P, 2, 2 * DM])
        wo1 = sb("wo1", [P, 2, DM])
        u1 = sb("u1", [P, 2, LR])
        v1w = sb("v1w", [LR, FF])
        u2 = sb("u2", [P, FF // P, LR])
        v2w = sb("v2w", [LR, DM])
        cols = sb("lcols", [P, NLCOLS])
        rows = sb("lrows", [P, NROWS])
        ctx_sb = sb("ctx_sb", [P, TILES, DC])
        mask_u8 = sb("mask_u8", [P, NBATCH, SEQ], U8)
        mask = sb("mask_bias", [P, NBATCH, SEQ])
        ones = sb("ones", [P, P])
        h_sb = sb("h_sb", [P, FF // P, PTOK])
        shared = h_sb[:, :, :].rearrange("p m n -> p (m n)")
        tern = shared[:, 0:6 * DM].rearrange("p (k n) -> p k n", k=3)
        buv_rep = shared[:, 6 * DM:6 * DM + NH * P].rearrange("p (h n) -> p h n", h=NH)
        sq = shared[:, 0:2 * PT_ * DM].rearrange("p (k n) -> p k n", k=2)
        qk_n = shared[:, 2 * PT_ * DM:4 * PT_ * DM].rearrange("p (k t n) -> p k t n", k=2, t=PT_)
        scales = sb("scales", [P, 8])
        bqs = sb("bqs", [P, 2])
        gamma = sb("gamma", [P, 1])
        stats = sb("lstats", [P, 2, PT_, 6])
        moments = sb("lmoments", [P, 2, PT_, 2])
        rider = sb("lrider", [P, 2])
        prider = sb("prider", [P, 1])
        eps_c = sb("eps_c", [P, PT_])
        half_c = sb("half_c", [P, 4 * PT_])
        ptmp = sb("ptmp", [P, 2, 6, PT_])
        rstd = sb("lrstd", [P, 2, PT_])
        nrm = sb("nrm", [P, 2, PT_, DM])
        c0_t = sb("c0_t", [P, 2, PTOK])
        c1_t = sb("c1_t", [P, 2, PTOK])
        x_t = sb("x_t", [P, 2, PTOK])
        k0_t = sb("k0_t", [P, 2, PTOK])
        v0 = sb("v0", [P, PT_, E0])
        q0_t = sb("q0_t", [P, 2, PTOK])
        o_t = sb("o_t", [P, 2, PTOK])
        k1_t = sb("k1_t", [P, 2, 2, 2 * SEQ])
        q1_t = sb("q1_t", [P, 2, PTOK])
        v1 = sb("v1", [P, 2, 4, DM])
        ss = sb("ss", [P, 2, 4 * PT_])
        ms = sb("ms", [P, 2, 4 * PT_])
        rms = sb("rms", [P, 2, 4 * PT_])
        negm = sb("negm", [P, 2, 4])
        rsum = sb("rsum", [P, 2, 4])
        rinv = sb("rinv_sb", [P, 4, 4])
        pe_ = sb("pexp_sb", [P, 2, 1024])
        p_t = sb("p_t", [P, 2, 1024])
        cq = sb("cq", [LAT + 1, PTOK])
        kk = sb("kk", [KEYW, PTOK])
        ckvn = sb("ckvn", [P, PT_, LAT])
        qh = sb("qh", [KEYW, 4, PTOK])
        o_n = sb("o_n", [P, PT_, DM])
        p5_t = sb("p5_t", [LR, PTOK])
        qt5 = sb("qt5", [LR, PTOK])

        D = [ctx.enter_context(nc.psum_tensor(f"D{i}", [P, 1024], F32)) for i in range(4)]
        TB = D[2]
        HEADP = D[3][:, 0:BANK]
        UP = D[3][:, BANK:2 * BANK]

        def col(name, c=0, n=P):
            at = COLS[name][0] + c
            return cols[0:n, at:at + 1]

        def row(name, n=DM):
            return rows[:, ROWS[name]:ROWS[name] + n]

        sc_attn0 = float(E0) ** -0.5
        sc_mla = 1.0 / float(DK + ROPE) ** 0.5
        sc_attn1 = float(DH) ** -0.5
        LOADS = ("wq0", "wk0a", "wk0b", "wv0a", "wv0b", "wo0", "wf", "w_dq", "w_kv", "uq_t", "uk_t", "uv_t", "w_o", "fold_r",
                 "wq1", "wkv1a", "wkv1b", "wlkv1", "wo1", "u1", "v1w", "u2", "v2w", "cols", "rows", "ctx", "mask")
        loaded = 16 * len(LOADS)
        block = ctx.enter_context(nc.Block())

        @block.sync
        def _(sp):
            def load(dst, src):
                sp.dma_start(dst, src).then_inc(s_in, 16)

            def two(w):
                return w.rearrange("(c p) n -> p c n", p=P)

            load(ctx_sb[:, :, :], dram["ctx"].rearrange("(t p) d -> p t d", p=P))
            load(cols[:, :], dram["lcols"])
            load(wk0[:, 0, :], dram["wk0"][0:P])
            load(wk0[0:CK[1], 1, :], dram["wk0"][P:DC])
            load(wv0[:, 0, :], dram["wv0"][0:P])
            load(wv0[0:CK[1], 1, :], dram["wv0"][P:DC])
            load(wkv1[:, 0, :], dram["wkv1"][0:P])
            load(wkv1[0:CK[1], 1, :], dram["wkv1"][P:DC])
            load(rows[:, :], dram["lrows"].partition_broadcast(P).rearrange("p a n -> p (a n)"))
            load(wf[:, :, :], two(dram["wf"]))
            load(uq_t[:, :, :], dram["uq_t"])
            load(uk_t[:, :, :], dram["uk_t"])
            load(uv_t[:, :, :], dram["uv_t"])
            load(w_o[:, :, :], dram["w_o"].rearrange("(h p) n -> p h n", p=P))
            load(mask_u8[:, :, :], dram["mask"].partition_broadcast(P).rearrange("p a (b k) -> p (a b) k", k=SEQ))
            load(fold_q[:, :, LAT:LAT + ROPE], dram["fold_r"])
            load(wq0[:, :, :], two(dram["wq0"]))
            load(wo0[:, :, :], two(dram["wo0"]))
            load(w_dq[:, :, :], two(dram["w_dq"]))
            load(w_kv[:, :, :], two(dram["w_kv"]))
            load(wq1[:, :, :], two(dram["wq1"]))
            load(wlkv1[:, :, :], two(dram["wlkv1"]))
            load(wo1[:, :, :], two(dram["wo1"]))
            load(u1[:, :, :], two(dram["u1"]))
            load(v1w[:, :], dram["v1w"])
            load(u2[:, :, :], two(dram["u2"]))
            load(v2w[:, :], dram["v2w"])
            out_rows = dram["out"].rearrange("(t p) d -> p t d", p=P)
            with sp.Fori(0, PAIRS) as it:
                sp.wait_ge(s["x_added"], it * PER["x_added"] + 8)
                sp.dma_start(out_rows[:, bass.ds(it * PT_, PT_), :], x_sb[:, bass.ds(it * PT_, PT_), :]).then_inc(s_out, 16)
            sp.wait_ge(s_out, 16 * PAIRS)

        @block.gpsimd
        def _(pool):
            pool.memset(eps_c[:, :], EPS).then_inc(s_const, 1)
            pool.memset(half_c[:, :], -0.5).then_inc(s_const, 1)
            pool.memset(ones[:, :], 1.0).then_inc(s_const, 1)
            pool.memset(prider[:, :], 0.0).then_inc(s_const, 1)
            pool.wait_ge(s_const, 4)
            with pool.Fori(0, PAIRS) as it:
                def after(name, k):
                    pool.wait_ge(s[name], it * PER[name] + k)

                steps = [0]

                def link(ins):
                    steps[0] += 1
                    ins.then_inc(s["pool_step"], 1)
                    after("pool_step", steps[0])

                def inverse_root(n, double):
                    after("moments", 4 * n + 4)
                    var = moments[:, n % 2, :, 1]
                    dst = rstd[:, n % 2, :]
                    tmp = ptmp[:, n % 2, :, :]
                    link(pool.tensor_tensor(tmp[:, 0, :], var, eps_c[:, :], ALU.add))
                    if not double:
                        pool.tensor_tensor(dst, tmp[:, 0, :], half_c[:, 0:PT_], ALU.pow).then_inc(s["rstd"], 1)
                        return
                    link(pool.tensor_tensor(tmp[:, 1, :], tmp[:, 0, :], half_c[:, 0:PT_], ALU.pow))
                    link(pool.tensor_tensor(tmp[:, 2, :], var, tmp[:, 1, :], ALU.mult))
                    link(pool.tensor_tensor(tmp[:, 3, :], tmp[:, 2, :], tmp[:, 1, :], ALU.mult))
                    link(pool.tensor_tensor(tmp[:, 4, :], tmp[:, 3, :], eps_c[:, :], ALU.add))
                    link(pool.tensor_tensor(tmp[:, 5, :], tmp[:, 4, :], half_c[:, 0:PT_], ALU.pow))
                    pool.tensor_tensor(dst, tmp[:, 5, :], tmp[:, 1, :], ALU.mult).then_inc(s["rstd"], 1)

                def rms_root(k):
                    after("ms", k + 1)
                    pool.tensor_tensor(rms[:, k % 2, :], ms[:, k % 2, :], half_c[:, :], ALU.pow).then_inc(s["rms"], 1)

                def add_bias(n, bias):
                    after("normed", 4 * n + 4)
                    pool.tensor_tensor(prider[:, :], prider[:, :], prider[:, :], ALU.mult)
                    xr = x_sb[:, bass.ds(it * PT_, PT_), :]
                    pool.tensor_tensor(xr, xr, bias.unsqueeze(1).broadcast_to([P, PT_, DM]), ALU.add).then_inc(s["x_biased"], 1)

                inverse_root(0, False)
                inverse_root(1, True)
                rms_root(0)
                add_bias(1, row("bo0"))
                inverse_root(2, False)
                inverse_root(3, False)
                add_bias(3, row("bo"))
                inverse_root(4, True)
                rms_root(1)
                rms_root(2)
                add_bias(4, row("bo1"))
                inverse_root(5, False)
                add_bias(5, row("b2"))
                assert steps[0] == PER["pool_step"]

        @block.scalar
        def _(act):
            act.wait_ge(s_in, loaded)
            act.activation(tern[:, 0, :], wf[:, :, :].rearrange("p c n -> p (c n)"), ACT.Abs,
                           accum_out=scales[:, 0:1]).then_inc(s_abs, 1)
            act.wait_ge(s_set, SETUP)
            with act.Fori(0, PAIRS) as it:
                def after(name, k):
                    act.wait_ge(s[name], it * PER[name] + k)

                def turned(n, dst, g=None, b=None):
                    after("turned", 2 * n + 1)
                    if g is None:
                        act.activation(dst, TB[:, 0:BANK], ACT.Copy).then_inc(s["turned_act"], 1)
                    else:
                        act.activation(dst, TB[:, 0:BANK], ACT.Identity, scale=col(g), bias=col(b)).then_inc(s["turned_act"], 1)

                def exps(quad, sp, n, keys):
                    after("maxed", quad + 1)
                    if quad >= 2:
                        after("p_turned", quad - 1)
                        after("rinv", quad - 1)
                    for r in range(n):
                        act.activation(pe_[:, quad % 2, r * keys:(r + 1) * keys], sp[:, r * keys:(r + 1) * keys], ACT.Exp,
                                       bias=negm[:, quad % 2, r:r + 1], accum_out=rsum[:, quad % 2, r:r + 1]).then_inc(s["pexp"], 1)

                def o_saved(k):
                    after("o_turned", 2 * k + 1)
                    act.activation(o_t[:, 0, :], TB[:, 0:BANK], ACT.Copy).then_inc(s["o_act"], 1)

                turned(0, c0_t[:, 0, :], "ln2_g", "ln2_b")
                turned(0, c1_t[:, 0, :], "lnx_g", "lnx_b")
                for e in range(2):
                    after("k0_mm", e + 1)
                    act.activation(k0_t[:, e, :], D[0][:, e * BANK:(e + 1) * BANK], ACT.Identity, bias=col("bk", e)).then_inc(s["k0_saved"], 1)
                after("k1c_mm", 1)
                act.activation(sq[:, 0, :], D[3][:, :], ACT.Square).then_inc(s["sq"], 1)
                after("v1c_mm", 1)
                act.activation(v1[:, :, 0:2, :], D[0][:, :].rearrange("p (b k n) -> p b k n", b=2, k=2), ACT.Copy).then_inc(s["v1c_saved"], 1)
                turned(1, x_t[:, 0, :], "ln1_g", "ln1_b")
                after("k1c_turned", 1)
                act.activation(k1_t[:, 0, :, 0:SEQ], D[1][:, 0:BANK].rearrange("p (b k) -> p b k", b=2), ACT.Copy).then_inc(s["k1c_act"], 1)
                after("q0_mm", 1)
                act.activation(q0_t[:, 0, :], D[3][:, 0:BANK], ACT.Identity, scale=sc_attn0, bias=bqs[:, 0:1]).then_inc(s["q0_act"], 1)
                after("max0", 1)
                for r in range(4):
                    act.activation(pe_[:, 0, r * SEQ:(r + 1) * SEQ], D[0][:, r * SEQ:(r + 1) * SEQ], ACT.Exp,
                                   bias=negm[:, 0, r:r + 1], accum_out=rsum[:, 0, r:r + 1]).then_inc(s["exp0"], 1)
                after("p0_turned", 1)
                act.activation(p_t[:, 0, 0:BANK], TB[:, 0:BANK], ACT.Copy).then_inc(s["p0_act"], 1)
                after("ctx0_mm", 1)
                act.activation(o_t[:, 0, :], D[1][:, 0:BANK], ACT.Copy).then_inc(s["ctx0_act"], 1)
                turned(2, x_t[:, 0, :])
                turned(3, x_t[:, 0, :])
                after("c_mm", 1)
                act.activation(cq[0:LAT, :], D[1][0:LAT, 0:BANK], ACT.Identity, bias=col("bdq", 0, LAT)).then_inc(s["cq_saved"], 1)

                def head_saved(n):
                    after("head_mm", n + 1)
                    act.activation(qh[:, n % 4, :], HEADP[0:KEYW, :], ACT.Copy, scale=sc_mla).then_inc(s["head_saved"], 1)

                for n in range(3):
                    head_saved(n)
                exps(0, D[0], 4, SEQ)
                for q in range(QUADS):
                    if q + 3 < NH:
                        head_saved(q + 3)
                    if q + 1 < QUADS:
                        exps(q + 1, D[(q + 1) % 2], 4, SEQ)
                o_saved(0)
                turned(4, x_t[:, 0, :], "lnl_g", "lnl_b")
                after("q1_mm", 1)
                act.activation(sq[:, 1, :], D[0][:, :], ACT.Square).then_inc(s["sq"], 1)
                after("k1l_mm", 1)
                act.activation(sq[:, 0, :], D[1][:, :], ACT.Square).then_inc(s["sq"], 1)
                after("v1l_mm", 1)
                act.activation(v1[:, :, 2:4, :], D[3][:, :].rearrange("p (b k n) -> p b k n", b=2, k=2), ACT.Copy).then_inc(s["v1l_saved"], 1)
                after("q1_turned", 1)
                act.activation(q1_t[:, 0, :], TB[:, 0:BANK], ACT.Copy, scale=gamma[:, 0:1]).then_inc(s["q1_act"], 1)
                after("k1l_turned", 1)
                act.activation(k1_t[:, 0, :, SEQ:2 * SEQ], D[3][:, 0:BANK].rearrange("p (b k) -> p b k", b=2), ACT.Copy).then_inc(s["k1l_act"], 1)
                for q in range(QUADS):
                    exps(QUADS + q, D[q % 2], 2, 2 * SEQ)
                o_saved(1)
                turned(5, x_t[:, 0, :])
                after("p5_mm", 1)
                act.activation(p5_t[:, :], D[1][0:LR, 0:BANK], ACT.Copy).then_inc(s["p5_saved"], 1)
                for m in range(FF // P):
                    after("h_mm", m + 1)
                    act.activation(h_sb[:, m, :], [D[0], D[3]][m % 4 // 2][:, m % 2 * BANK:(m % 2 + 1) * BANK],
                                   ACT.Gelu_apprx_tanh, bias=col("b1", m)).then_inc(s["gelu"], 1)
                after("qt_mm", 1)
                act.activation(qt5[:, :], D[1][0:LR, BANK:2 * BANK], ACT.Copy).then_inc(s["qt_saved"], 1)

        @block.tensor
        def _(pe):
            pe.wait_ge(s_in, loaded)
            for h in range(NH):
                pe.matmul(D[0][0:LAT + 1, h * (LAT + 1):(h + 1) * (LAT + 1)], uq_t[:, h, :], uk_t[:, h, :], start=True, stop=True)
            for h in range(NH):
                at = h % 4 * LAT
                pe.matmul(D[1][at:at + LAT, h // 4 * DM:(h // 4 + 1) * DM], uv_t[:, h, :], w_o[:, h, :], start=True, stop=True)
            pe.wait_ge(s_set, 1)
            for h in range(NH):
                pe.matmul(D[2][:, 0:DM], buv_rep[:, h, :], w_o[:, h, :], start=h == 0, stop=h == NH - 1)
            pe.wait_ge(s_abs, 1)
            pe.matmul(D[3][:, 0:1], ones[:, :], scales[:, 0:1], start=True, stop=True).then_inc(s_fold, 1)
            pe.wait_ge(s_set, SETUP)
            with pe.Fori(0, PAIRS) as it:
                def after(name, k):
                    pe.wait_ge(s[name], it * PER[name] + k)

                def turn(n, width=DM):
                    for c in range(2):
                        w = min(P, width - c * P)
                        for t in range(PT_):
                            if c == 0:
                                after("normed", 4 * n + t + 1)
                            last = pe.transpose(TB[0:w, c * BANK + t * P:c * BANK + (t + 1) * P],
                                                nrm[:, n % 2, t, c * P:c * P + w], ident[:, :])
                        last.then_inc(s["turned"], 1)

                def turned(n):
                    after("turned_act", n + 2)
                    after("turned_dve", n + 2)

                def rows_times(dst, src_t, w, name, ks=(P, P), lo=0, n=DM):
                    for t in range(PT_):
                        for c in range(2):
                            last = pe.matmul(dst[:, t * n:(t + 1) * n], src_t[0:ks[c], c, t * P:(t + 1) * P],
                                             w[0:ks[c], c, lo:lo + n], start=c == 0, stop=c == 1)
                    last.then_inc(s[name], 1)

                def cols_times(dst, w, src_t, name, ks=(P, P)):
                    for e in range(2):
                        for c in range(2):
                            last = pe.matmul(dst[:, e * BANK:(e + 1) * BANK], w[0:ks[c], c, e * P:(e + 1) * P],
                                             src_t[0:ks[c], c, :], start=c == 0, stop=c == 1)
                        last.then_inc(s[name], 1)

                def turn_rows(dst, src, name):
                    for c in range(2):
                        for t in range(PT_):
                            last = pe.transpose(dst[:, c * BANK + t * P:c * BANK + (t + 1) * P], src[:, t, c * P:(c + 1) * P], ident[:, :])
                        last.then_inc(s[name], 1)

                turn(0, DC)
                after("turned_act", 1)
                after("turned_dve", 1)
                cols_times(D[0], wk0, c0_t, "k0_mm", CK)
                rows_times(D[1], c0_t, wv0, "v0_mm", CK)
                turned(0)
                rows_times(D[3], c1_t, wkv1, "k1c_mm", CK)
                after("k0_saved", 2)
                rows_times(D[0], c1_t, wkv1, "v1c_mm", CK, lo=DM)
                turn(1)
                after("v0_saved", 1)
                after("k1c_normed", 1)
                turn_rows(D[1], qk_n[:, 0, :, :], "k1c_turned")
                turned(1)
                cols_times(D[3], wq0, x_t, "q0_mm")
                after("v1c_saved", 1)
                after("q0_act", 1)
                after("q0_dve", 1)
                for r in range(4):
                    b, c = r // 2, r % 2
                    for e in range(2):
                        last = pe.matmul(D[0][:, r * SEQ:(r + 1) * SEQ], q0_t[:, e, b * SEQ + c * P:b * SEQ + (c + 1) * P],
                                         k0_t[:, e, b * SEQ:(b + 1) * SEQ], start=e == 0, stop=e == 1)
                last.then_inc(s["score0"], 1)
                after("exp0", 4)
                for b in range(2):
                    for kc in range(2):
                        for c in range(2):
                            at = (b * 2 + kc) * SEQ + c * P
                            src = (b * 2 + c) * SEQ + kc * P
                            last = pe.transpose(TB[:, at:at + P], pe_[:, 0, src:src + P], ident[:, :])
                    last.then_inc(s["p0_turned"], 1)
                after("k1c_act", 1)
                after("k1c_dve", 1)
                after("p0_act", 1)
                after("p0_dve", 1)
                for e in range(2):
                    for b in range(2):
                        for kc in range(2):
                            last = pe.matmul(D[1][:, e * BANK + b * SEQ:e * BANK + (b + 1) * SEQ], v0[:, b * 2 + kc, e * P:(e + 1) * P],
                                             p_t[:, 0, (b * 2 + kc) * SEQ:(b * 2 + kc + 1) * SEQ], start=kc == 0, stop=kc == 1)
                    last.then_inc(s["ctx0_mm"], 1)
                after("ctx0_act", 1)
                after("ctx0_dve", 1)
                rows_times(D[3], o_t, wo0, "out0_mm")
                turn(2)
                turned(2)
                rows_times(D[0], x_t, wf, "ffn0_mm")
                turn(3)
                turned(3)
                for c in range(2):
                    last = pe.matmul(D[1][0:LAT, 0:BANK], w_dq[:, c, :], x_t[:, c, :], start=c == 0, stop=c == 1)
                last.then_inc(s["c_mm"], 1)
                for c in range(2):
                    last = pe.matmul(D[1][0:LAT + ROPE, BANK:2 * BANK], w_kv[:, c, :], x_t[:, c, :], start=c == 0, stop=c == 1)
                last.then_inc(s["c_mm"], 1)
                rows_times(UP, x_t, w_kv, "ckvn_mm", n=LAT)
                after("cq_saved", 1)

                def head(n):
                    if n:
                        after("head_saved", n)
                    pe.matmul(HEADP[0:KEYW, :], fold_q[:, n, :], cq[:, :], start=True, stop=True).then_inc(s["head_mm"], 1)

                def score(q):
                    hp, b = q // 2, q % 2
                    after("head_saved", 2 * hp + 2)
                    if q >= 2:
                        after("pexp", pexp_before(q - 1))
                    for c in range(2):
                        for hh in range(2):
                            at = (c * 2 + hh) * SEQ
                            last = pe.matmul(D[q % 2][:, at:at + SEQ], qh[:, (2 * hp + hh) % 4, b * SEQ + c * P:b * SEQ + (c + 1) * P],
                                             kk[:, b * SEQ:(b + 1) * SEQ], start=True, stop=True)
                    last.then_inc(s["scored"], 1)

                def turn_p(quad, n, keys):
                    after("pexp", pexp_before(quad + 1))
                    if quad:
                        after("pt_saved", quad)
                    for r in range(n):
                        c, hh = r // (n // 2), r % (n // 2)
                        for kc in range(keys // P):
                            at = (hh * (keys // P) + kc) * SEQ + c * P
                            last = pe.transpose(TB[:, at:at + P], pe_[:, quad % 2, r * keys + kc * P:r * keys + (kc + 1) * P], ident[:, :])
                    last.then_inc(s["p_turned"], 1)

                def values(q):
                    b = q % 2
                    after("pt_saved", q + 1)
                    if q:
                        after("u_read", q)
                    for c in range(2):
                        for hh in range(2):
                            at = q % 2 * P + (c * 2 + hh) * LAT
                            for kc in range(2):
                                last = pe.matmul(UP[:, at:at + LAT], p_t[:, q % 2, (hh * 2 + kc) * SEQ + c * P:(hh * 2 + kc) * SEQ + (c + 1) * P],
                                                 ckvn[:, b * 2 + kc, :], start=kc == 0, stop=kc == 1)
                    last.then_inc(s["pv_mm"], 1)

                for n in range(3):
                    head(n)
                after("kk_saved", 1)
                score(0)
                after("ckvn_saved", 1)
                for q in range(QUADS):
                    if q + 1 < QUADS:
                        score(q + 1)
                    turn_p(q, 4, SEQ)
                    if q + 3 < NH:
                        head(q + 3)
                    if q:
                        values(q - 1)
                values(QUADS - 1)
                after("u_read", QUADS)
                turn_rows(TB, o_n, "o_turned")
                after("o_act", 1)
                after("o_dve", 1)
                rows_times(D[0], o_t, fold_v, "out1_mm")
                turn(4)
                turned(4)
                rows_times(D[0], x_t, wq1, "q1_mm")
                rows_times(D[1], x_t, wlkv1, "k1l_mm")
                rows_times(D[3], x_t, wlkv1, "v1l_mm", lo=DM)
                after("q1_normed", 1)
                turn_rows(TB, qk_n[:, 1, :, :], "q1_turned")
                after("v1l_saved", 1)
                after("k1l_normed", 1)
                turn_rows(D[3], qk_n[:, 0, :, :], "k1l_turned")

                def score1(q):
                    b, h = q // H4, q % H4
                    if q >= 2:
                        after("pexp", pexp_before(QUADS + q - 1))
                    at = h % 2 * DH
                    for c in range(2):
                        last = pe.matmul(D[q % 2][:, c * BANK:(c + 1) * BANK], q1_t[at:at + DH, h // 2, b * SEQ + c * P:b * SEQ + (c + 1) * P],
                                         k1_t[at:at + DH, h // 2, b, :], start=True, stop=True)
                    last.then_inc(s["scored"], 1)

                def values1(q):
                    b, h = q // H4, q % H4
                    after("pt_saved", QUADS + q + 1)
                    after("u_read", QUADS + q)
                    for c in range(2):
                        at = q % 2 * P + c * DH
                        for kc in range(4):
                            last = pe.matmul(UP[:, at:at + DH], p_t[:, q % 2, kc * SEQ + c * P:kc * SEQ + (c + 1) * P],
                                             v1[:, b, kc, h * DH:(h + 1) * DH], start=kc == 0, stop=kc == 3)
                    last.then_inc(s["pv_mm"], 1)

                for name in ("q1_act", "q1_dve", "k1l_act", "k1l_dve"):
                    after(name, 1)
                score1(0)
                for q in range(QUADS):
                    if q + 1 < QUADS:
                        score1(q + 1)
                    turn_p(QUADS + q, 2, 2 * SEQ)
                    if q:
                        values1(q - 1)
                values1(QUADS - 1)
                after("u_read", 2 * QUADS)
                turn_rows(TB, o_n, "o_turned")
                after("o_act", 2)
                after("o_dve", 2)
                rows_times(D[0], o_t, wo1, "out1_mm")
                turn(5)
                turned(5)
                for c in range(2):
                    last = pe.matmul(D[1][0:LR, 0:BANK], u1[:, c, :], x_t[:, c, :], start=c == 0, stop=c == 1)
                last.then_inc(s["p5_mm"], 1)
                after("p5_saved", 1)
                for m in range(FF // P + 2):
                    if m < FF // P:
                        if m >= 4:
                            after("gelu", m - 3)
                        pe.matmul([D[0], D[3]][m % 4 // 2][:, m % 2 * BANK:(m % 2 + 1) * BANK], v1w[:, m * P:(m + 1) * P],
                                  p5_t[:, :], start=True, stop=True).then_inc(s["h_mm"], 1)
                    if m >= 2:
                        after("gelu", m - 1)
                        last = pe.matmul(D[1][0:LR, BANK:2 * BANK], u2[:, m - 2, :], h_sb[:, m - 2, :], start=m == 2, stop=m == FF // P + 1)
                last.then_inc(s["qt_mm"], 1)
                after("qt_saved", 1)
                for t in range(PT_):
                    last = pe.matmul(TB[:, t * DM:(t + 1) * DM], qt5[:, t * P:(t + 1) * P], v2w[:, :], start=True, stop=True)
                last.then_inc(s["y_mm"], 1)

        @block.vector
        def _(dve):
            dve.wait_ge(s_in, loaded)
            dve.wait_ge(s_const, 4)
            for h in range(NH):
                last = dve.tensor_scalar(buv_rep[:, h, :], ones[:, :], col("buv", h), None, ALU.mult)
            last.then_inc(s_set, 1)
            dve.tensor_scalar(mask[:, :, :], mask_u8[:, :, :], 1.0, FLT_MAX, ALU.subtract, ALU.mult).then_inc(s_set, 1)
            dve.tensor_scalar(bqs[:, :], cols[:, COLS["bq"][0]:COLS["bq"][0] + 2], sc_attn0, None, ALU.mult).then_inc(s_set, 1)
            dve.scalar_tensor_tensor(out=gamma[:, :], in0=col("qn"), scalar=sc_attn1, in1=col("kn"),
                                     op0=ALU.mult, op1=ALU.mult).then_inc(s_set, 1)
            dve.wait_ge(s_fold, 1)
            prod = D[0][0:LAT + 1, 0:NH * (LAT + 1)].rearrange("p (h n) -> p h n", h=NH)
            dve.tensor_copy(fold_q[:, :, 0:LAT], prod[:, :, 0:LAT]).then_inc(s_set, 1)
            dve.tensor_copy(fold_q[:, :, KEYW - 1:KEYW], prod[:, :, LAT:LAT + 1]).then_inc(s_set, 1)
            dve.tensor_copy(fold_v[:, :, :], D[1][:, 0:2 * DM].rearrange("p (c n) -> p c n", c=2)).then_inc(s_set, 1)
            dve.tensor_tensor(row("bo"), D[2][:, 0:DM], row("bo"), ALU.add).then_inc(s_set, 1)
            dve.tensor_scalar(scales[:, 1:2], D[3][:, 0:1], 1.0 / (DM * DM), EPS, ALU.mult, ALU.max).then_inc(s_set, 1)
            dve.wait_ge(s_set, 9)
            dve.tensor_scalar(scales[:, 2:3], scales[:, 1:2], 0.5, None, ALU.mult).then_inc(s_set, 1)
            dve.tensor_scalar(scales[:, 3:4], scales[:, 1:2], -0.5, None, ALU.mult).then_inc(s_set, 1)
            dve.wait_ge(s_set, 11)
            flat = wf[:, :, :].rearrange("p c n -> p (c n)")
            dve.tensor_scalar(tern[:, 1, :], flat, scales[:, 2:3], scales[:, 1:2], ALU.is_gt, ALU.mult).then_inc(s_set, 1)
            dve.tensor_scalar(tern[:, 2, :], flat, scales[:, 3:4], scales[:, 1:2], ALU.is_lt, ALU.mult).then_inc(s_set, 1)
            dve.wait_ge(s_set, 13)
            dve.tensor_tensor(flat, tern[:, 1, :], tern[:, 2, :], ALU.subtract).then_inc(s_set, 1)
            dve.memset(cq[LAT:LAT + 1, :], 1.0).then_inc(s_set, 1)
            dve.memset(kk[LAT + ROPE:KEYW, :], 1.0).then_inc(s_set, 1)
            with dve.Fori(0, PAIRS) as it:
                def after(name, k):
                    dve.wait_ge(s[name], it * PER[name] + k)

                def tile_of(src, t):
                    return src[:, bass.ds(it * PT_ + t, 1), :].rearrange("p a d -> p (a d)")

                def measure(n, src):
                    dve.memset(rider[:, 0:1], 0.0)
                    for t in range(PT_):
                        dve.bn_stats(stats[:, n % 2, t, :], tile_of(src, t)).then_inc(s["stats"], 1)
                    after("stats", 4 * n + 4)
                    dve.memset(rider[:, 1:2], 0.0)
                    for t in range(PT_):
                        dve.bn_aggr(moments[:, n % 2, t, :], stats[:, n % 2, t, :]).then_inc(s["moments"], 1)

                def normalise(n, src, width=DM):
                    after("rstd", n + 1)
                    if n >= 2:
                        after("turned", 2 * (n - 1))
                    for t in range(PT_):
                        dve.tensor_scalar(nrm[:, n % 2, t, 0:width], tile_of(src, t), moments[:, n % 2, t, 0:1],
                                          rstd[:, n % 2, t:t + 1], ALU.subtract, ALU.mult).then_inc(s["normed"], 1)

                def turned(n, dst, g=None, b=None, rows_=P):
                    after("turned", 2 * n + 2)
                    src = TB[0:rows_, BANK:2 * BANK]
                    if g is None:
                        dve.tensor_copy(dst, src).then_inc(s["turned_dve"], 1)
                    else:
                        dve.tensor_scalar(dst, src, col(g, 1, rows_), col(b, 1, rows_), ALU.mult, ALU.add).then_inc(s["turned_dve"], 1)

                def mean_square(k, slot):
                    after("sq", k + 1)
                    dve.tensor_reduce(ss[:, k % 2, :], sq[:, slot, :].rearrange("p (a d) -> p a d", d=DH), AX_X, ALU.add).then_inc(s["ss"], 1)
                    after("ss", k + 1)
                    dve.tensor_scalar(ms[:, k % 2, :], ss[:, k % 2, :], 1.0 / DH, 1e-16, ALU.mult, ALU.max).then_inc(s["ms"], 1)

                def rms_norm(k, src, dst, name):
                    after("rms", k + 1)
                    dve.tensor_tensor(dst.rearrange("p t (h d) -> p (t h) d", d=DH), src.rearrange("p (a d) -> p a d", d=DH),
                                      rms[:, k % 2, :].unsqueeze(2).broadcast_to([P, 4 * PT_, DH]), ALU.mult).then_inc(s[name], 1)

                def x_rows():
                    return x_sb[:, bass.ds(it * PT_, PT_), :]

                def add_to_x(src, k):
                    dve.tensor_tensor(x_rows(), src[:, :].rearrange("p (t d) -> p t d", d=DM), x_rows(), ALU.add).then_inc(s["x_added"], 1)
                    after("x_added", k)

                measure(0, ctx_sb)
                measure(1, x_sb)
                normalise(0, ctx_sb, DC)
                normalise(1, x_sb)
                turned(0, c0_t[0:CK[1], 1, :], "ln2_g", "ln2_b", CK[1])
                turned(0, c1_t[0:CK[1], 1, :], "lnx_g", "lnx_b", CK[1])
                after("v0_mm", 1)
                dve.tensor_tensor(v0[:, :, :], D[1][:, :].rearrange("p (t d) -> p t d", d=E0),
                                  row("bv").unsqueeze(1).broadcast_to([P, PT_, E0]), ALU.add).then_inc(s["v0_saved"], 1)
                mean_square(0, 0)
                turned(1, x_t[:, 1, :], "ln1_g", "ln1_b")
                rms_norm(0, D[3][:, :], qk_n[:, 0, :, :], "k1c_normed")
                after("k1c_turned", 2)
                dve.tensor_copy(k1_t[:, 1, :, 0:SEQ], D[1][:, BANK:2 * BANK].rearrange("p (b k) -> p b k", b=2)).then_inc(s["k1c_dve"], 1)
                after("q0_mm", 2)
                dve.tensor_scalar(q0_t[:, 1, :], D[3][:, BANK:2 * BANK], sc_attn0, bqs[:, 1:2], ALU.mult, ALU.add).then_inc(s["q0_dve"], 1)
                after("score0", 1)
                dve.tensor_reduce(negm[:, 0, :], D[0][:, :].rearrange("p (r k) -> p r k", k=SEQ), AX_X, ALU.max, negate=True).then_inc(s["max0"], 1)
                after("p0_turned", 2)
                dve.tensor_copy(p_t[:, 0, BANK:2 * BANK], TB[:, BANK:2 * BANK]).then_inc(s["p0_dve"], 1)
                after("exp0", 4)
                dve.reciprocal(rinv[:, 0, :], rsum[:, 0, :]).then_inc(s["rinv0"], 1)
                after("ctx0_mm", 2)
                dve.tensor_copy(o_t[:, 1, :], D[1][:, BANK:2 * BANK]).then_inc(s["ctx0_dve"], 1)
                after("rinv0", 1)
                after("x_biased", 1)
                after("out0_mm", 1)
                for t in range(PT_):
                    dve.scalar_tensor_tensor(out=tile_of(x_sb, t), in0=D[3][:, t * DM:(t + 1) * DM], scalar=rinv[:, 0, t:t + 1],
                                             in1=tile_of(x_sb, t), op0=ALU.mult, op1=ALU.add).then_inc(s["x_added"], 1)
                after("x_added", 4)
                measure(2, x_sb)
                normalise(2, x_sb)
                turned(2, x_t[:, 1, :])
                after("ffn0_mm", 1)
                add_to_x(D[0], 5)
                measure(3, x_sb)
                normalise(3, x_sb)
                turned(3, x_t[:, 1, :])
                after("c_mm", 2)
                dve.tensor_scalar(kk[0:LAT + ROPE, :], D[1][0:LAT + ROPE, BANK:2 * BANK], col("bkv", 0, LAT + ROPE), None, ALU.add).then_inc(s["kk_saved"], 1)
                after("ckvn_mm", 1)
                dve.tensor_tensor(ckvn[:, :, :], UP[:, 0:PT_ * LAT].rearrange("p (t d) -> p t d", d=LAT),
                                  row("bdkv", LAT).unsqueeze(1).broadcast_to([P, PT_, LAT]), ALU.add).then_inc(s["ckvn_saved"], 1)

                def quad_max(quad, sp, n, batch=None):
                    after("scored", quad + 1)
                    if batch is not None:
                        keys = sp[:, :].rearrange("p (c k) -> p c k", c=2)[:, :, 0:SEQ]
                        m = mask[:, bass.ds(it * 2 + batch, 1), :].broadcast_to([P, 2, SEQ])
                        dve.tensor_tensor(keys, keys, m, ALU.add).then_inc(s["masked"], 1)
                        after("masked", quad - QUADS + 1)
                    if quad >= 2:
                        after("pexp", pexp_before(quad - 1))
                    dve.tensor_reduce(negm[:, quad % 2, 0:n], sp[:, :].rearrange("p (r k) -> p r k", r=n), AX_X, ALU.max,
                                      negate=True).then_inc(s["maxed"], 1)

                def quad_rest(quad, n):
                    after("p_turned", quad + 1)
                    if quad >= 2:
                        after("pv_mm", quad - 1)
                    dve.tensor_copy(p_t[:, quad % 2, :], TB[:, :]).then_inc(s["pt_saved"], 1)
                    dve.reciprocal(rinv[:, quad % 4, 0:n], rsum[:, quad % 2, 0:n]).then_inc(s["rinv"], 1)

                def latent_out(q):
                    hp, b = q // 2, q % 2
                    after("rinv", q + 1)
                    after("pv_mm", q + 1)
                    dst = o_n[:, 2 * b:2 * b + 2, 2 * hp * LAT:(2 * hp + 2) * LAT].rearrange("p c (h d) -> p c h d", h=2)
                    dve.tensor_tensor(dst, UP[:, q % 2 * P:(q % 2 + 1) * P].rearrange("p (c h d) -> p c h d", c=2, h=2),
                                      rinv[:, q % 4, :].rearrange("p (c h) -> p c h", c=2).unsqueeze(3).broadcast_to([P, 2, 2, LAT]),
                                      ALU.mult).then_inc(s["u_read"], 1)

                def cross_out(q):
                    b, h = q // H4, q % H4
                    after("rinv", QUADS + q + 1)
                    after("pv_mm", QUADS + q + 1)
                    dve.tensor_tensor(o_n[:, 2 * b:2 * b + 2, h * DH:(h + 1) * DH], UP[:, q % 2 * P:(q % 2 + 1) * P].rearrange("p (c d) -> p c d", c=2),
                                      rinv[:, q % 4, 0:2].unsqueeze(2).broadcast_to([P, 2, DH]), ALU.mult).then_inc(s["u_read"], 1)

                def o_saved(k):
                    after("o_turned", 2 * k + 2)
                    dve.tensor_copy(o_t[:, 1, :], TB[:, BANK:2 * BANK]).then_inc(s["o_dve"], 1)

                quad_max(0, D[0], 4)
                for q in range(QUADS):
                    if q + 1 < QUADS:
                        quad_max(q + 1, D[(q + 1) % 2], 4)
                    quad_rest(q, 4)
                    if q:
                        latent_out(q - 1)
                latent_out(QUADS - 1)
                o_saved(0)
                after("x_biased", 2)
                after("out1_mm", 1)
                add_to_x(D[0], 6)
                measure(4, x_sb)
                normalise(4, x_sb)
                turned(4, x_t[:, 1, :], "lnl_g", "lnl_b")
                mean_square(1, 1)
                mean_square(2, 0)
                rms_norm(1, D[0][:, :], qk_n[:, 1, :, :], "q1_normed")
                rms_norm(2, D[1][:, :], qk_n[:, 0, :, :], "k1l_normed")
                after("q1_turned", 2)
                dve.tensor_scalar(q1_t[:, 1, :], TB[:, BANK:2 * BANK], gamma[:, 0:1], None, ALU.mult).then_inc(s["q1_dve"], 1)
                after("k1l_turned", 2)
                dve.tensor_copy(k1_t[:, 1, :, SEQ:2 * SEQ], D[3][:, BANK:2 * BANK].rearrange("p (b k) -> p b k", b=2)).then_inc(s["k1l_dve"], 1)
                quad_max(QUADS, D[0], 2, 0)
                for q in range(QUADS):
                    if q + 1 < QUADS:
                        quad_max(QUADS + q + 1, D[(q + 1) % 2], 2, (q + 1) // H4)
                    quad_rest(QUADS + q, 2)
                    if q:
                        cross_out(q - 1)
                cross_out(QUADS - 1)
                o_saved(1)
                after("x_biased", 3)
                after("out1_mm", 2)
                add_to_x(D[0], 7)
                measure(5, x_sb)
                normalise(5, x_sb)
                turned(5, x_t[:, 1, :])
                after("x_biased", 4)
                after("y_mm", 1)
                add_to_x(TB, 8)



def layout(a):
    import numpy as np
    f = {k: np.asarray(v) for k, v in a.items()}

    def chunked(v):
        v = v.reshape(CH, P, -1)
        return v.transpose(1, 0, 2).reshape(P, -1)

    def column(v):
        v = np.concatenate([v, np.zeros(-len(v) % P, v.dtype)])
        return v.reshape(-1, P).T

    def with_bias(w, b):
        return np.concatenate([w, b[None]]).reshape(len(w) + 1, NH, -1)

    m, x0, a1, x1, f1 = "L0_attn_", "L0_xattn_", "L1_attn_", "L1_xattn_", "L1_ffn_"
    cols = np.stack([np.concatenate([chunked(f[m + n]) for n in names], axis=1) for names in (
        ("conv_w", "conv_b", "dt_proj_b", "D", "A_log"),
        ("conv_w_b", "conv_b_b", "dt_proj_b_b", "D_b", "A_b_log"))], axis=1)
    vectors = {
        "ln2_g": f[x0 + "ln2_g"], "ln2_b": f[x0 + "ln2_b"], "lnx_g": f[x1 + "ln_x_g"], "lnx_b": f[x1 + "ln_x_b"],
        "ln1_g": f[x0 + "ln1_g"], "ln1_b": f[x0 + "ln1_b"], "lnl_g": f[x1 + "ln_l_g"], "lnl_b": f[x1 + "ln_l_b"],
        "bq": f[x0 + "bq"], "bk": f[x0 + "bk"], "qn": np.tile(f[x1 + "qn_g"], 2), "kn": np.tile(f[x1 + "kn_g"], 2),
        "bdq": f[a1 + "b_DQ"], "bkv": np.concatenate([f[a1 + "b_DKV"], f[a1 + "b_KR"]]), "b1": f[f1 + "b1"],
        "buv": f[a1 + "b_UV"],
    }
    out = {
        "x": f["x"].reshape(NBATCH * SEQ, DM),
        "ident": np.eye(P, dtype=np.float32),
        "mamba_cols": cols,
        "in_w": f[m + "in_proj_w"].T,
        "xp_w": np.stack([f[m + "x_proj_w"].T, f[m + "x_proj_w_b"].T]),
        "dt_w": np.stack([f[m + "dt_proj_w"].T, f[m + "dt_proj_w_b"].T]),
        "out_w": f[m + "out_proj_w"].T,
        "ctx": f["ctx_768"].reshape(NBATCH * SEQ, DC),
        "mask": f["mask_BxS2_bk0"].reshape(1, NBATCH * SEQ),
        "lcols": np.concatenate([column(vectors[n]) for n in COLS], axis=1),
        "lrows": np.concatenate([f[x0 + "bv"], f[x0 + "bo"], f[a1 + "b_O"], f[x1 + "bo"], f[f1 + "b2"], f[a1 + "b_DKV"]])[None],
        "wq0": f[x0 + "Wq"], "wk0": f[x0 + "Wk"], "wv0": f[x0 + "Wv"], "wo0": f[x0 + "Wo"],
        "wf": f["L0_ffn_weight"].T,
        "w_dq": f[a1 + "W_DQ"], "w_kv": np.concatenate([f[a1 + "W_DKV"], f[a1 + "W_KR"]], axis=1),
        "uq_t": with_bias(f[a1 + "W_UQ"], f[a1 + "b_UQ"]).transpose(2, 1, 0),
        "uk_t": with_bias(f[a1 + "W_UK"], f[a1 + "b_UK"]).transpose(2, 1, 0),
        "uv_t": f[a1 + "W_UV"].reshape(LAT, NH, DK).transpose(2, 1, 0),
        "w_o": f[a1 + "W_O"],
        "fold_r": with_bias(f[a1 + "W_QR"], f[a1 + "b_QR"]),
        "wq1": f[x1 + "Wq"].T, "wkv1": f[x1 + "Wkv"].T, "wlkv1": f[x1 + "Wlkv"].T, "wo1": f[x1 + "Wo"].T,
        "u1": f[f1 + "U1"], "v1w": f[f1 + "V1"], "u2": f[f1 + "U2"], "v2w": f[f1 + "V2"],
    }
    return {k: np.ascontiguousarray(v) for k, v in out.items()}


def decoder_kernel(nc, dram):
    with nc.sbuf_tensor("x_sb", [P, TILES, DM], F32) as x_sb, nc.sbuf_tensor("ident_sb", [P, P], F32) as ident:
        mamba_block(nc, dram, x_sb, ident)
        layers_block(nc, dram, x_sb, ident)


def kernel(**inputs):
    import numpy as _np
    import concourse.bacc as _bacc
    from concourse.bass_utils import run_bass_kernel_spmd as _run

    nc = _bacc.Bacc("TRN2", target_bir_lowering=False, num_devices=1)
    arrays, dram = {}, {}
    for name, v in layout(inputs).items():
        arrays[f"{name}_dram"] = v
        dram[name] = nc.dram_tensor(f"{name}_dram", v.shape, mybir.dt.from_np(v.dtype), kind="ExternalInput").ap()
    dram["out"] = nc.dram_tensor("out_dram", (NBATCH * SEQ, DM), F32, kind="ExternalOutput").ap()
    decoder_kernel(nc, dram)
    r = _run(nc, [arrays], core_ids=[0])
    return _np.asarray(r.results[0]["out_dram"]).reshape(NBATCH, SEQ, DM)
```

```python
from contextlib import ExitStack

import concourse.bass as bass
from concourse import mybir

F32 = mybir.dt.float32
U8 = mybir.dt.uint8
ALU = mybir.AluOpType
ACT = mybir.ActivationFunctionType
AX_X = mybir.AxisListType.X

P = 128
NBATCH, SEQ, DM = 8, 256, 256
TILES = NBATCH * SEQ // P
EPS = 1e-5

DIN, NSTATE, TAPS, RANK = 512, 16, 4, 64
CH = DIN // P
HALVES = 2
HB = NBATCH // HALVES
HT = HB * SEQ
HTILES = HT // P
PAD = TAPS - 1
ROW = PAD + SEQ + PAD
BANK = 512
XD = RANK + 2 * NSTATE

C_CONVW, C_CONVB, C_DTB, C_D, C_ALOG = 0, CH * TAPS, CH * TAPS + CH, CH * TAPS + 2 * CH, CH * TAPS + 3 * CH
NCOLS = C_ALOG + CH * NSTATE


def mamba_block(nc, dram, x_sb, ident):
    with ExitStack() as ctx:
        def sb(name, shape, dt=F32):
            return ctx.enter_context(nc.sbuf_tensor(name, shape, dt))

        def sem(name):
            return ctx.enter_context(nc.semaphore(name))

        in_w = sb("in_w", [P, 2, 2 * DIN])
        xp_w = sb("xp_w", [P, 2, CH, XD])
        dt_w = sb("dt_w", [RANK, 2, DIN])
        out_w = sb("out_w", [P, CH, DM])
        cols = sb("cols", [P, 2, NCOLS])
        a_neg = sb("a_neg", [P, 2, CH * NSTATE])
        a_exp = sb("a_exp", [P, 2, CH * NSTATE])
        d_diag = sb("d_diag", [P, 2, CH, P])
        pow_c = sb("pow_c", [P, 2, HTILES])

        stats = sb("stats", [P, HTILES, 6])
        meanvar = sb("meanvar", [P, HTILES, 2])
        rider = sb("rider", [P, 1])
        vareps = sb("vareps", [P, HTILES])
        rstd = sb("rstd", [P, HTILES])
        work = sb("work", [P, CH, HT])
        normed = work[:, 0:2, :].rearrange("p a (t d) -> p (a t) d", d=DM)
        norm_t = sb("norm_t", [P, 2, HT])
        xpad = sb("xpad", [P, CH, HB, ROW])
        gate = sb("gate", [P, CH, HT])
        xc = sb("xc", [P, CH, HT])
        delta = work
        gated = work
        du = sb("du", [P, CH, HT])
        xdbl = sb("xdbl", [XD, HT])
        bc = sb("bc", [P, 2, 2, HT])
        decay = sb("decay", [P, 2, HT])
        inject = sb("inject", [P, 2, HT])
        state = sb("state", [P, 2, HT])
        readout = sb("readout", [P, 2, HT])
        y_tail = sb("y_tail", [P, 2, HT])
        y_fwd = [norm_t[:, 0, :], norm_t[:, 1, :], y_tail[:, 0, :], y_tail[:, 1, :]]
        psum = ctx.enter_context(nc.psum_tensor("mamba_psum", [P, CH, 2 * BANK], F32))
        bc_dram = nc.dram_tensor("bc_rows", [2, 2 * NSTATE, HT], F32, kind="Internal").ap()

        names = """x_loaded w_loaded pads_zero consts_set a_exped a_ready diag_ready stats_done mean_ready
            vareps_ready rstd_ready norm_ready tr_ready norm_t_ready inproj_ready inproj_read xpad_ready
            conv_first conv_step conv_sum_ready xc_ready xproj_ready xdbl_ready bc_stored bc_even bc_odd
            dtproj_ready sp_abs sp_exp sp_w sp_ln sp_corr sp_sum sp_relu delta_ready du_ready
            strip_and_scan decay_ready inject_ready readout_ready y_added y_saved y_summed gated_ready
            outproj_ready x_updated""".split()
        s = {n: sem(n) for n in names}
        bc_loaded = [s["bc_even"], s["bc_odd"]]
        sums = [psum[:, c, :] for c in range(CH)]
        banks = psum[:, :, :].rearrange("p c n -> p (c n)")

        block = ctx.enter_context(nc.Block())

        def direction(hf, d):
            return hf * 2 + d

        @block.sync
        def _(sp):
            sp.dma_start(x_sb[:, :, :], dram["x"].rearrange("(t p) d -> p t d", p=P)).then_inc(s["x_loaded"], 16)
            sp.dma_start(ident[:, :], dram["ident"]).then_inc(s["w_loaded"], 16)
            sp.dma_start(cols[:, :, :], dram["mamba_cols"]).then_inc(s["w_loaded"], 16)
            sp.dma_start(in_w[:, :, :], dram["in_w"].rearrange("(c p) n -> p c n", p=P)).then_inc(s["w_loaded"], 16)
            sp.dma_start(xp_w[:, :, :, :], dram["xp_w"].rearrange("d (c p) n -> p d c n", p=P)).then_inc(s["w_loaded"], 16)
            sp.dma_start(dt_w[:, :, :], dram["dt_w"].rearrange("d p n -> p d n")).then_inc(s["w_loaded"], 16)
            sp.dma_start(out_w[:, :, :], dram["out_w"].rearrange("(c p) n -> p c n", p=P)).then_inc(s["w_loaded"], 16)

            def load_bc(slot, d, n):
                rows = bc_dram[d].rearrange("(k n) t -> n k t", k=2)
                src = rows[bass.ds(n, 1)].partition_broadcast(P) if not isinstance(n, int) else rows[n:n + 1].partition_broadcast(P)
                src = src.rearrange("p a k t -> p (a k) t")
                sp.dma_start(bc[:, slot, :, :], src).then_inc(bc_loaded[slot], 16)

            with sp.Fori(0, HALVES) as hf:
                for d in range(2):
                    sp.wait_ge(s["xdbl_ready"], direction(hf, d) * 2 + 2)
                    sp.dma_start(bc_dram[d], xdbl[RANK:XD, :]).then_inc(s["bc_stored"], 16)
                    sp.wait_ge(s["bc_stored"], direction(hf, d) * 16 + 16)
                    load_bc(0, d, 0)
                    load_bc(1, d, 1)
                    with sp.Fori(0, NSTATE // 2 - 1) as j:
                        for k in range(2):
                            sp.wait_ge(s["readout_ready"],
                                       direction(hf, d) * (NSTATE * CH) + j * (2 * CH) + (k + 1) * CH)
                            load_bc(k, d, j * 2 + (2 + k))

        @block.gpsimd
        def _(pool):
            pool.memset(pow_c[:, 0, :], EPS).then_inc(s["consts_set"], 1)
            pool.memset(pow_c[:, 1, :], -0.5).then_inc(s["consts_set"], 1)
            pool.memset(xpad[:, :, :, 0:PAD], 0.0).then_inc(s["pads_zero"], 1)
            pool.memset(xpad[:, :, :, PAD + SEQ:ROW], 0.0).then_inc(s["pads_zero"], 1)
            pool.wait_ge(s["consts_set"], 2)
            with pool.Fori(0, HALVES) as hf:
                pool.wait_ge(s["mean_ready"], hf * HTILES + HTILES)
                pool.tensor_tensor(vareps[:, :], meanvar[:, :, 1], pow_c[:, 0, :], ALU.add).then_inc(s["vareps_ready"], 1)
                pool.wait_ge(s["vareps_ready"], hf + 1)
                pool.tensor_tensor(rstd[:, :], vareps[:, :], pow_c[:, 1, :], ALU.pow).then_inc(s["rstd_ready"], 1)
                for d in range(2):
                    dirs = direction(hf, d)
                    for c in range(CH):
                        pool.wait_ge(s["delta_ready"], dirs * CH + c + 1)
                        pool.tensor_tensor(du[:, c, :], delta[:, c, :], xc[:, c, :], ALU.mult).then_inc(s["du_ready"], 1)
                    with pool.Fori(0, NSTATE // 2) as j:
                        for k in range(2):
                            pool.wait_ge(s["du_ready"], dirs * CH + CH)
                            pool.wait_ge(bc_loaded[k], dirs * (8 * NSTATE) + j * 16 + 16)
                            for c in range(CH):
                                step = k * CH + c
                                pool.wait_ge(s["strip_and_scan"], dirs * (NSTATE * CH + 2) + j * (2 * CH) + step + 1)
                                pool.tensor_tensor(inject[:, c % 2, :], du[:, c, :], bc[:, k, 0, :], ALU.mult).then_inc(s["inject_ready"], 1)

        @block.scalar
        def _(act):
            act.wait_ge(s["w_loaded"], 96)
            act.activation(a_exp[:, :, :], cols[:, :, C_ALOG:NCOLS], ACT.Exp).then_inc(s["a_exped"], 1)
            with act.Fori(0, HALVES) as hf:
                act.wait_ge(s["tr_ready"], hf * 2 + 2)
                act.activation(norm_t[:, 1, :], sums[1], ACT.Copy).then_inc(s["norm_t_ready"], 1)
                for m in range(2 * CH):
                    act.wait_ge(s["inproj_ready"], hf * (2 * CH) + m + 1)
                    if m < CH:
                        act.activation(xpad[:, m, :, PAD:PAD + SEQ],
                                       sums[m % CH].rearrange("p (b l) -> p b l", b=HB), ACT.Copy).then_inc(s["inproj_read"], 1)
                    else:
                        act.activation(gate[:, m - CH, :], sums[m % CH], ACT.Silu).then_inc(s["inproj_read"], 1)
                for d in range(2):
                    dirs = direction(hf, d)
                    if d:
                        act.wait_ge(s["readout_ready"], dirs * (NSTATE * CH))
                    act.wait_ge(s["inproj_read"], hf * (2 * CH) + CH)
                    act.wait_ge(s["pads_zero"], 2)
                    for c in range(CH):
                        at = PAD * 2 if d else 0
                        act.activation(xc[:, c, :].rearrange("p (b l) -> p b l", b=HB), xpad[:, c, :, at:at + SEQ],
                                       ACT.Identity, bias=cols[:, d, C_CONVB + c:C_CONVB + c + 1],
                                       scale=cols[:, d, C_CONVW + TAPS * c:C_CONVW + TAPS * c + 1]).then_inc(s["conv_first"], 1)
                    for c in range(CH):
                        act.wait_ge(s["conv_sum_ready"], dirs * CH + c + 1)
                        act.activation(xc[:, c, :], xc[:, c, :], ACT.Silu).then_inc(s["xc_ready"], 1)
                    for b in range(2):
                        act.wait_ge(s["xproj_ready"], dirs * 2 + b + 1)
                        act.activation(xdbl[:, b * BANK:(b + 1) * BANK], sums[0][0:XD, b * BANK:(b + 1) * BANK],
                                       ACT.Copy).then_inc(s["xdbl_ready"], 1)
                    for c in range(CH):
                        act.wait_ge(s["dtproj_ready"], dirs * CH + c + 1)
                        if c >= 2:
                            act.wait_ge(s["delta_ready"], dirs * CH + c - 1)
                        act.activation(decay[:, c % 2, :], sums[c], ACT.Abs,
                                       bias=cols[:, d, C_DTB + c:C_DTB + c + 1]).then_inc(s["sp_abs"], 1)
                        act.wait_ge(s["sp_abs"], dirs * CH + c + 1)
                        act.activation(inject[:, c % 2, :], decay[:, c % 2, :], ACT.Exp, scale=-1.0).then_inc(s["sp_exp"], 1)
                        act.wait_ge(s["sp_exp"], dirs * CH + c + 1)
                        act.activation(state[:, c % 2, :], inject[:, c % 2, :], ACT.Ln, bias=1.0).then_inc(s["sp_ln"], 1)
                    act.wait_ge(s["a_ready"], 1)
                    act.wait_ge(s["delta_ready"], dirs * CH + CH)
                    lo, hi = (1, SEQ) if d == 0 else (0, SEQ - 1)
                    with act.Fori(0, NSTATE // 2) as j:
                        for k in range(2):
                            for c in range(CH):
                                step = k * CH + c
                                act.wait_ge(s["strip_and_scan"], dirs * (NSTATE * CH + 2) + j * (2 * CH) + step + 1)
                                act.activation(decay[:, c % 2, :].rearrange("p (b l) -> p b l", b=HB)[:, :, lo:hi],
                                               delta[:, c, :].rearrange("p (b l) -> p b l", b=HB)[:, :, lo:hi],
                                               ACT.Exp, scale=a_neg[:, d, bass.ds(j * 2 + (c * NSTATE + k), 1)]).then_inc(s["decay_ready"], 1)
                    if d == 0:
                        act.wait_ge(s["y_added"], hf * (2 * NSTATE * CH + 4) + (NSTATE * CH + 2))
                        for c in range(CH):
                            act.activation(y_fwd[c], sums[c], ACT.Copy, scale=0.5).then_inc(s["y_saved"], 1)

        @block.tensor
        def _(pe):
            pe.wait_ge(s["w_loaded"], 96)
            pe.wait_ge(s["diag_ready"], 2 * CH)
            with pe.Fori(0, HALVES) as hf:
                for c in range(2):
                    for t in range(HTILES):
                        pe.wait_ge(s["norm_ready"], hf * HTILES + t + 1)
                        last = pe.transpose(sums[c][:, t * P:(t + 1) * P], normed[:, t, c * P:(c + 1) * P], ident[:, :])
                    last.then_inc(s["tr_ready"], 1)
                pe.wait_ge(s["norm_t_ready"], hf * 2 + 2)
                for m in range(2 * CH):
                    if m >= CH:
                        pe.wait_ge(s["inproj_read"], hf * (2 * CH) + m - CH + 1)
                    for b in range(2):
                        for c in range(2):
                            last = pe.matmul(sums[m % CH][:, b * BANK:(b + 1) * BANK], in_w[:, c, m * P:(m + 1) * P],
                                             norm_t[:, c, b * BANK:(b + 1) * BANK], start=c == 0, stop=c == 1)
                    last.then_inc(s["inproj_ready"], 1)
                for d in range(2):
                    dirs = direction(hf, d)
                    pe.wait_ge(s["xc_ready"], dirs * CH + CH)
                    pe.wait_ge(s["inproj_read"], hf * (2 * CH) + 2 * CH)
                    if d:
                        pe.wait_ge(s["y_saved"], hf * CH + CH)
                    for b in range(2):
                        for c in range(CH):
                            last = pe.matmul(sums[0][0:XD, b * BANK:(b + 1) * BANK], xp_w[:, d, c, :],
                                             xc[:, c, b * BANK:(b + 1) * BANK], start=c == 0, stop=c == CH - 1)
                        last.then_inc(s["xproj_ready"], 1)
                    pe.wait_ge(s["xdbl_ready"], dirs * 2 + 2)
                    for c in range(CH):
                        for b in range(2):
                            last = pe.matmul(sums[c][:, b * BANK:(b + 1) * BANK], dt_w[:, d, c * P:(c + 1) * P],
                                             xdbl[0:RANK, b * BANK:(b + 1) * BANK], start=True, stop=True)
                        last.then_inc(s["dtproj_ready"], 1)
                    for c in range(CH):
                        pe.wait_ge(s["sp_relu"], dirs * CH + c + 1)
                        for b in range(2):
                            last = pe.matmul(sums[c][:, b * BANK:(b + 1) * BANK], d_diag[:, d, c, :],
                                             xc[:, c, b * BANK:(b + 1) * BANK], start=True, stop=False, skip_group_check=True)
                        if c >= 2:
                            last.then_inc(s["y_added"], 1)
                    with pe.Fori(0, NSTATE // 2) as j:
                        for k in range(2):
                            for c in range(CH):
                                pe.wait_ge(s["readout_ready"], dirs * (NSTATE * CH) + j * (2 * CH) + k * CH + c + 1)
                                for b in range(2):
                                    last = pe.matmul(sums[c][:, b * BANK:(b + 1) * BANK], ident[:, :],
                                                     readout[:, c % 2, b * BANK:(b + 1) * BANK], start=False, stop=False, skip_group_check=True)
                                last.then_inc(s["y_added"], 1)
                pe.wait_ge(s["gated_ready"], hf * CH + CH)
                for t in range(HTILES):
                    dst = banks[:, t * DM:(t + 1) * DM]
                    for c in range(CH):
                        last = pe.matmul(dst, gated[:, c, t * P:(t + 1) * P], out_w[:, c, :], start=c == 0, stop=c == CH - 1)
                    if t % 4 == 3:
                        last.then_inc(s["outproj_ready"], 1)

        @block.vector
        def _(dve):
            dve.wait_ge(s["w_loaded"], 96)
            dve.wait_ge(s["a_exped"], 1)
            dve.tensor_scalar(a_neg[:, :, :], a_exp[:, :, :], -1.0, None, ALU.mult).then_inc(s["a_ready"], 1)
            for d in range(2):
                for c in range(CH):
                    dve.tensor_scalar(d_diag[:, d, c, :], ident[:, :], cols[:, d, C_D + c:C_D + c + 1], None,
                                      ALU.mult).then_inc(s["diag_ready"], 1)
            dve.wait_ge(s["x_loaded"], 16)
            with dve.Fori(0, HALVES) as hf:
                for t in range(HTILES):
                    dve.bn_stats(stats[:, t, :], x_sb[:, bass.ds(hf * HTILES + t, 1), :].rearrange("p a d -> p (a d)")).then_inc(s["stats_done"], 1)
                dve.wait_ge(s["stats_done"], hf * HTILES + HTILES)
                dve.memset(rider[:, :], 0.0)
                for t in range(HTILES):
                    dve.bn_aggr(meanvar[:, t, :], stats[:, t, :]).then_inc(s["mean_ready"], 1)
                dve.wait_ge(s["rstd_ready"], hf + 1)
                for t in range(HTILES):
                    dve.tensor_scalar(normed[:, t, :], x_sb[:, bass.ds(hf * HTILES + t, 1), :].rearrange("p a d -> p (a d)"),
                                      meanvar[:, t, 0:1], rstd[:, t:t + 1], ALU.subtract, ALU.mult).then_inc(s["norm_ready"], 1)
                dve.wait_ge(s["tr_ready"], hf * 2 + 1)
                dve.tensor_copy(norm_t[:, 0, :], sums[0]).then_inc(s["norm_t_ready"], 1)
                for d in range(2):
                    dirs = direction(hf, d)
                    for c in range(CH):
                        dve.wait_ge(s["conv_first"], dirs * CH + c + 1)
                        acc = xc[:, c, :].rearrange("p (b l) -> p b l", b=HB)
                        for k in range(1, TAPS):
                            at = PAD * 2 - k if d else k
                            if k > 1:
                                dve.wait_ge(s["conv_step"], dirs * (CH * 2) + c * 2 + k - 1)
                            w = cols[:, d, C_CONVW + TAPS * c + k:C_CONVW + TAPS * c + k + 1]
                            step = dve.scalar_tensor_tensor(out=acc, in0=xpad[:, c, :, at:at + SEQ], scalar=w, in1=acc,
                                                            op0=ALU.mult, op1=ALU.add)
                            step.then_inc(s["conv_sum_ready"] if k == TAPS - 1 else s["conv_step"], 1)
                    for c in range(CH):
                        dve.wait_ge(s["sp_exp"], dirs * CH + c + 1)
                        dve.tensor_scalar(readout[:, c % 2, :], inject[:, c % 2, :], 1.0, None, ALU.add).then_inc(s["sp_w"], 1)
                        dve.wait_ge(s["sp_w"], dirs * CH + c + 1)
                        dve.wait_ge(s["sp_ln"], dirs * CH + c + 1)
                        dve.scalar_tensor_tensor(out=inject[:, c % 2, :], in0=readout[:, c % 2, :], scalar=1.0,
                                                 in1=inject[:, c % 2, :], op0=ALU.subtract, op1=ALU.subtract).then_inc(s["sp_corr"], 1)
                        dve.tensor_scalar(delta[:, c, :], sums[c], cols[:, d, C_DTB + c:C_DTB + c + 1], 0.0,
                                          ALU.add, ALU.max).then_inc(s["sp_relu"], 1)
                        dve.wait_ge(s["sp_corr"], dirs * CH + c + 1)
                        dve.tensor_tensor(state[:, c % 2, :], state[:, c % 2, :], inject[:, c % 2, :], ALU.subtract).then_inc(s["sp_sum"], 1)
                        dve.wait_ge(s["sp_sum"], dirs * CH + c + 1)
                        dve.wait_ge(s["sp_relu"], dirs * CH + c + 1)
                        dve.tensor_tensor(delta[:, c, :], delta[:, c, :], state[:, c % 2, :], ALU.add).then_inc(s["delta_ready"], 1)
                    at = SEQ - 1 if d else 0
                    for k in range(2):
                        dve.memset(decay[:, k, :].rearrange("p (b l) -> p b l", b=HB)[:, :, at:at + 1], 0.0).then_inc(s["strip_and_scan"], 1)
                    with dve.Fori(0, NSTATE // 2) as j:
                        for k in range(2):
                            for c in range(CH):
                                step = k * CH + c
                                nth = dirs * (NSTATE * CH) + j * (2 * CH) + step
                                dve.wait_ge(s["decay_ready"], nth + 1)
                                dve.wait_ge(s["inject_ready"], nth + 1)
                                way = slice(None, None, -1) if d else slice(None)
                                dve.tensor_tensor_scan(state[:, c % 2, :][:, way], decay[:, c % 2, :][:, way],
                                                       inject[:, c % 2, :][:, way], 0.0, ALU.mult, ALU.add).then_inc(s["strip_and_scan"], 1)
                                dve.wait_ge(s["strip_and_scan"], dirs * (NSTATE * CH + 2) + j * (2 * CH) + step + 3)
                                dve.wait_ge(s["y_added"], dirs * (NSTATE * CH + 2) + j * (2 * CH) + step + 1)
                                dve.tensor_tensor(readout[:, c % 2, :], state[:, c % 2, :], bc[:, k, 1, :], ALU.mult).then_inc(s["readout_ready"], 1)
                dve.wait_ge(s["y_added"], hf * (2 * NSTATE * CH + 4) + (2 * NSTATE * CH + 4))
                for c in range(CH):
                    dve.scalar_tensor_tensor(out=gated[:, c, :], in0=sums[c], scalar=0.5, in1=y_fwd[c],
                                             op0=ALU.mult, op1=ALU.add).then_inc(s["y_summed"], 1)
                for c in range(CH):
                    dve.wait_ge(s["y_summed"], hf * CH + c + 1)
                    dve.tensor_tensor(gated[:, c, :], gated[:, c, :], gate[:, c, :], ALU.mult).then_inc(s["gated_ready"], 1)
                for g in range(HTILES // 4):
                    dve.wait_ge(s["outproj_ready"], hf * (HTILES // 4) + g + 1)
                    x_rows = x_sb[:, bass.ds(hf * HTILES + 4 * g, 4), :]
                    dve.tensor_tensor(x_rows, banks[:, g * 4 * DM:(g + 1) * 4 * DM].rearrange("p (t d) -> p t d", d=DM),
                                      x_rows, ALU.add).then_inc(s["x_updated"], 1)
                dve.wait_ge(s["x_updated"], hf * (HTILES // 4) + HTILES // 4)


SETUP = 18
PAIRS = NBATCH // 2
PT_, PTOK = 2 * SEQ // P, 2 * SEQ
DC = 192
CK = (P, DC - P)
E0 = 256
NH, DK, LAT, ROPE = 8, 128, 32, 32
KEYW = LAT + ROPE + 1
H4, DH = 4, 64
FF, LR = 1024, 64
FLT_MAX = 3.4028234663852886e38
QUADS = 8

COLS = {}
for _name, _n in (("ln2_g", 2), ("ln2_b", 2), ("lnx_g", 2), ("lnx_b", 2), ("ln1_g", 2), ("ln1_b", 2), ("lnl_g", 2),
                  ("lnl_b", 2), ("bq", 2), ("bk", 2), ("qn", 1), ("kn", 1), ("bdq", 1), ("bkv", 1), ("b1", 8), ("buv", 8),
                  ("bv", 2)):
    COLS[_name] = (sum(n for _, n in COLS.values()), _n)
NLCOLS = sum(n for _, n in COLS.values())
ROWS = {"bo0": 0, "bo": DM, "bo1": 2 * DM, "b2": 3 * DM, "bdkv": 4 * DM}
NROWS = 4 * DM + LAT

PER = {
    "c_loaded": 16, "c_stats": 4, "c_moments": 4, "c_var": 1, "c_rstd": 1, "c_normed": 4, "c_turned": 2, "c0_saved": 2, "c1_saved": 2,
    "k0_mm": 2, "k0_saved": 2, "v0_mm": 1, "v0_saved": 1, "k1c_mm": 1, "k1c_saved": 1, "c_sq": 1, "c_ss": 1, "c_ms": 1, "c_rms": 1,
    "k1c_normed": 1, "k1c_turned": 2, "k1c_placed": 2, "v1c_mm": 1, "v1c_saved": 1,
    "stats": 20, "moments": 20, "var": 5, "rstd": 5, "normed": 20, "turned": 10, "turned_act": 5, "turned_dve": 5,
    "q0_mm": 2, "q0_act": 1, "q0_dve": 1, "score0": 1, "max0": 1, "exp0": 4, "rinv0": 1, "p0_turned": 2, "p0_act": 1, "p0_dve": 1,
    "ctx0_mm": 2, "ctx0_act": 1, "ctx0_dve": 1, "out0_mm": 2, "x_biased": 4, "x_added": 12, "ffn0_mm": 2,
    "cq_mm": 2, "cq_saved": 1, "kk_saved": 1, "ckvn_mm": 1, "ckvn_saved": 1,
    "head_mm": 8, "head_saved": 8, "scored": 16, "masked": 8, "maxed": 16, "pexp": 48, "rinv": 16, "p_normed": 48,
    "p_turned": 16, "pt_dve": 16, "pt_act": 8, "pv_mm": 16, "o_act": 2, "o_dve": 2, "out1_mm": 4,
    "q1_mm": 1, "k1l_mm": 1, "v1l_mm": 1, "v1l_saved": 1, "sq": 2, "ss": 2, "ms": 2, "rms": 2, "q1_normed": 1, "k1l_normed": 1,
    "q1_turned": 2, "k1l_turned": 2, "q1_act": 1, "q1_dve": 1, "k1l_act": 1, "k1l_dve": 1,
    "p5_mm": 1, "p5_saved": 1, "h_mm": 8, "gelu": 8, "qt_mm": 1, "qt_saved": 1, "y_mm": 2,
}


def pexp_before(quad):
    return 4 * quad if quad <= QUADS else 4 * QUADS + 2 * (quad - QUADS)


def latent_quad(q):
    return q // 2, q % 2


def cross_quad(q):
    return q // 2 % 2, 2 * (q // 4) + q % 2


def layers_block(nc, dram, x_sb, ident):
    with ExitStack() as ctx:
        def sb(name, shape, dt=F32):
            return ctx.enter_context(nc.sbuf_tensor(name, shape, dt))

        s = {n: ctx.enter_context(nc.semaphore(n)) for n in PER}
        s_in = ctx.enter_context(nc.semaphore("inputs_loaded"))
        s_out = ctx.enter_context(nc.semaphore("out_stored"))
        s_const = ctx.enter_context(nc.semaphore("pool_consts"))
        s_set = ctx.enter_context(nc.semaphore("setup_dve"))
        s_abs = ctx.enter_context(nc.semaphore("ternary_abs"))
        s_fold = ctx.enter_context(nc.semaphore("folds_mm"))

        wq0 = sb("wq0", [P, 2, E0])
        wk0 = sb("wk0", [P, 2, E0])
        wv0 = sb("wv0", [P, 2, E0])
        wo0 = sb("wo0", [P, 2, DM])
        wf = sb("wf", [P, 2, DM])
        w_dq = sb("w_dq", [P, 2, LAT])
        w_kv = sb("w_kv", [P, 2, LAT + ROPE])
        uq_t = sb("uq_t", [DK, NH, LAT + 1])
        uk_t = sb("uk_t", [DK, NH, LAT + 1])
        uv_t = sb("uv_t", [DK, NH, LAT])
        w_o = sb("w_o", [DK, NH, DM])
        fold_q = sb("fold_q", [LAT + 1, NH, KEYW])
        fold_v = sb("fold_v", [P, 2, DM])
        wq1 = sb("wq1", [P, 2, DM])
        wkv1 = sb("wkv1", [P, 2, 2 * DM])
        wlkv1 = sb("wlkv1", [P, 2, 2 * DM])
        wo1 = sb("wo1", [P, 2, DM])
        u1 = sb("u1", [P, 2, LR])
        v1w = sb("v1w", [LR, FF])
        u2 = sb("u2", [P, FF // P, LR])
        v2w = sb("v2w", [LR, DM])
        cols = sb("lcols", [P, NLCOLS])
        rows = sb("lrows", [P, NROWS])
        ctx_sb = sb("ctx_sb", [P, PT_, DC])
        mask_u8 = sb("mask_u8", [P, NBATCH, SEQ], U8)
        mask = sb("mask_bias", [P, NBATCH, SEQ])
        ones = sb("ones", [P, P])
        h_sb = sb("h_sb", [P, FF // P, PTOK])
        shared = h_sb[:, :, :].rearrange("p m n -> p (m n)")
        tern = shared[:, 0:6 * DM].rearrange("p (k n) -> p k n", k=3)
        buv_rep = shared[:, 6 * DM:6 * DM + NH * P].rearrange("p (h n) -> p h n", h=NH)
        sq = shared[:, 0:2 * PT_ * DM].rearrange("p (k n) -> p k n", k=2)
        qk_n = shared[:, 2 * PT_ * DM:4 * PT_ * DM].rearrange("p (k t n) -> p k t n", k=2, t=PT_)
        scales = sb("scales", [P, 8])
        bqs = sb("bqs", [P, 2])
        gamma = sb("gamma", [P, 1])
        bv_rep = shared[:, 6 * DM + NH * P:6 * DM + NH * P + 2 * P].rearrange("p (c n) -> p c n", c=2)
        c_stats = sb("c_stats_sb", [P, PT_, 6])
        c_moments = sb("c_moments_sb", [P, PT_, 2])
        c_var = sb("c_var_sb", [P, PT_])
        c_rstd = sb("c_rstd_sb", [P, PT_])
        c_nrm = sb("c_nrm", [P, PT_, DC])
        c0_t = sb("c0_t", [P, 2, PTOK])
        c1_t = sb("c1_t", [P, 2, PTOK])
        k0_t = sb("k0_t", [P, 2, PTOK])
        v0 = sb("v0", [P, PT_, E0])
        k1c = sb("k1c", [P, PT_, DM])
        c_sq = sb("c_sq_sb", [P, PT_ * DM])
        c_ss = sb("c_ss_sb", [P, 4 * PT_])
        c_ms = sb("c_ms_sb", [P, 4 * PT_])
        c_rms = sb("c_rms_sb", [P, 4 * PT_])
        stats = sb("lstats", [P, 2, PT_, 6])
        moments = sb("lmoments", [P, 2, PT_, 2])
        var = sb("lvar", [P, 2, PT_])
        rider = sb("lrider", [P, 2])
        prider = sb("prider", [P, 1])
        half_c = sb("half_c", [P, 4 * PT_])
        rstd = sb("lrstd", [P, 2, PT_])
        nrm = sb("nrm", [P, 2, PT_, DM])
        x_t = sb("x_t", [P, 2, PTOK])
        q0_t = sb("q0_t", [P, 2, PTOK])
        o_t = sb("o_t", [P, 2, PTOK])
        k1_t = sb("k1_t", [P, 2, 2, 2 * SEQ])
        q1_t = q0_t
        v1 = sb("v1", [P, 2, 4, DM])
        ss = sb("ss", [P, 2, 4 * PT_])
        ms = sb("ms", [P, 2, 4 * PT_])
        rms = sb("rms_sb", [P, 2, 4 * PT_])
        negm = sb("negm", [P, 2, 4])
        rsum = sb("rsum", [P, 2, 4])
        rinv = sb("rinv_sb", [P, 2, 4])
        pe_ = sb("pexp_sb", [P, 2, 1024])
        p_t = sb("p_t", [P, 2, 1024])
        cq = sb("cq", [LAT + 1, PTOK])
        kk = sb("kk", [KEYW, PTOK])
        ckvn = sb("ckvn", [P, PT_, LAT])
        qh = sb("qh", [KEYW, 4, PTOK])
        p5_t = sb("p5_t", [LR, PTOK])
        qt5 = sb("qt5", [LR, PTOK])

        D = [ctx.enter_context(nc.psum_tensor(f"D{i}", [P, 1024], F32)) for i in range(4)]
        TB = D[2]
        OB = [D[3][:, BANK:2 * BANK], D[3][:, 0:BANK]]

        def head_bank(n):
            return OB[0] if n < 4 and n % 2 else OB[1]

        def col(name, c=0, n=P):
            at = COLS[name][0] + c
            return cols[0:n, at:at + 1]

        def row(name, n=DM):
            return rows[:, ROWS[name]:ROWS[name] + n]

        sc_attn0 = float(E0) ** -0.5
        sc_mla = 1.0 / float(DK + ROPE) ** 0.5
        sc_attn1 = float(DH) ** -0.5
        LOADS = ("wq0", "wk0a", "wk0b", "wv0a", "wv0b", "wo0", "wf", "w_dq", "w_kv", "uq_t", "uk_t", "uv_t", "w_o", "fold_r",
                 "wq1", "wkv1a", "wkv1b", "wlkv1", "wo1", "u1", "v1w", "u2", "v2w", "cols", "rows", "mask")
        loaded = 16 * len(LOADS)
        block = ctx.enter_context(nc.Block())

        @block.sync
        def _(sp):
            def load(dst, src):
                sp.dma_start(dst, src).then_inc(s_in, 16)

            def two(w):
                return w.rearrange("(c p) n -> p c n", p=P)

            ctx_rows = dram["ctx"].rearrange("(t p) d -> p t d", p=P)
            sp.dma_start(ctx_sb[:, :, :], ctx_rows[:, 0:PT_, :]).then_inc(s["c_loaded"], 16)
            load(cols[:, :], dram["lcols"])
            load(wk0[:, 0, :], dram["wk0"][0:P])
            load(wk0[0:CK[1], 1, :], dram["wk0"][P:DC])
            load(wv0[:, 0, :], dram["wv0"][0:P])
            load(wv0[0:CK[1], 1, :], dram["wv0"][P:DC])
            load(wkv1[:, 0, :], dram["wkv1"][0:P])
            load(wkv1[0:CK[1], 1, :], dram["wkv1"][P:DC])
            load(rows[:, :], dram["lrows"].partition_broadcast(P).rearrange("p a n -> p (a n)"))
            load(wf[:, :, :], two(dram["wf"]))
            load(uq_t[:, :, :], dram["uq_t"])
            load(uk_t[:, :, :], dram["uk_t"])
            load(uv_t[:, :, :], dram["uv_t"])
            load(w_o[:, :, :], dram["w_o"].rearrange("(h p) n -> p h n", p=P))
            load(mask_u8[:, :, :], dram["mask"].partition_broadcast(P).rearrange("p a (b k) -> p (a b) k", k=SEQ))
            load(fold_q[:, :, LAT:LAT + ROPE], dram["fold_r"])
            load(wq0[:, :, :], two(dram["wq0"]))
            load(wo0[:, :, :], two(dram["wo0"]))
            load(w_dq[:, :, :], two(dram["w_dq"]))
            load(w_kv[:, :, :], two(dram["w_kv"]))
            load(wq1[:, :, :], two(dram["wq1"]))
            load(wlkv1[:, :, :], two(dram["wlkv1"]))
            load(wo1[:, :, :], two(dram["wo1"]))
            load(u1[:, :, :], two(dram["u1"]))
            load(v1w[:, :], dram["v1w"])
            load(u2[:, :, :], two(dram["u2"]))
            load(v2w[:, :], dram["v2w"])
            out_rows = dram["out"].rearrange("(t p) d -> p t d", p=P)

            def store(it):
                sp.wait_ge(s["x_added"], it * PER["x_added"] + PER["x_added"])
                sp.dma_start(out_rows[:, bass.ds(it * PT_, PT_), :], x_sb[:, bass.ds(it * PT_, PT_), :]).then_inc(s_out, 16)

            with sp.Fori(0, PAIRS - 1) as it:
                sp.wait_ge(s["c_normed"], it * PER["c_normed"] + PT_)
                sp.dma_start(ctx_sb[:, :, :], ctx_rows[:, bass.ds(it * PT_ + PT_, PT_), :]).then_inc(s["c_loaded"], 16)
                store(it)
            store(PAIRS - 1)
            sp.wait_ge(s_out, 16 * PAIRS)

        @block.gpsimd
        def _(pool):
            pool.memset(half_c[:, :], -0.5).then_inc(s_const, 1)
            pool.memset(ones[:, :], 1.0).then_inc(s_const, 1)
            pool.memset(prider[:, :], 0.0).then_inc(s_const, 1)
            pool.wait_ge(s_const, 3)

            def context_norm(j):
                pool.wait_ge(s["c_var"], j * PER["c_var"] + 1)
                pool.tensor_tensor(c_rstd[:, :], c_var[:, :], half_c[:, 0:PT_], ALU.pow).then_inc(s["c_rstd"], 1)

            def context_keys(j):
                pool.wait_ge(s["c_ms"], j * PER["c_ms"] + 1)
                pool.tensor_tensor(c_rms[:, :], c_ms[:, :], half_c[:, :], ALU.pow).then_inc(s["c_rms"], 1)
                pool.wait_ge(s["c_rms"], j * PER["c_rms"] + 1)
                pool.wait_ge(s["k1c_saved"], j * PER["k1c_saved"] + 1)
                k = k1c[:, :, :].rearrange("p t (h d) -> p (t h) d", d=DH)
                pool.tensor_tensor(k, k, c_rms[:, :].unsqueeze(2).broadcast_to([P, 4 * PT_, DH]), ALU.mult).then_inc(s["k1c_normed"], 1)

            def pair(it, more):
                def after(name, k):
                    pool.wait_ge(s[name], it * PER[name] + k)

                def inverse_root(n):
                    after("var", n + 1)
                    pool.tensor_tensor(rstd[:, n % 2, :], var[:, n % 2, :], half_c[:, 0:PT_], ALU.pow).then_inc(s["rstd"], 1)

                def rms_root(k):
                    after("ms", k + 1)
                    pool.tensor_tensor(rms[:, k, :], ms[:, k, :], half_c[:, :], ALU.pow).then_inc(s["rms"], 1)

                def add_bias(n, bias):
                    after("normed", 4 * n + 4)
                    pool.tensor_tensor(prider[:, :], prider[:, :], prider[:, :], ALU.mult)
                    xr = x_sb[:, bass.ds(it * PT_, PT_), :]
                    pool.tensor_tensor(xr, xr, bias.unsqueeze(1).broadcast_to([P, PT_, DM]), ALU.add).then_inc(s["x_biased"], 1)

                inverse_root(0)
                add_bias(0, row("bo0"))
                if more:
                    context_norm(it + 1)
                inverse_root(1)
                inverse_root(2)
                add_bias(2, row("bo"))
                inverse_root(3)
                rms_root(0)
                rms_root(1)
                add_bias(3, row("bo1"))
                if more:
                    context_keys(it + 1)
                inverse_root(4)
                add_bias(4, row("b2"))

            context_norm(0)
            context_keys(0)
            with pool.Fori(0, PAIRS - 1) as it:
                pair(it, True)
            pair(PAIRS - 1, False)

        @block.scalar
        def _(act):
            act.wait_ge(s_in, loaded)
            act.activation(tern[:, 0, :], wf[:, :, :].rearrange("p c n -> p (c n)"), ACT.Abs,
                           accum_out=scales[:, 0:1]).then_inc(s_abs, 1)
            act.wait_ge(s_set, SETUP)

            def context_turned(j):
                for dst, g, b, name in ((c0_t, "ln2_g", "ln2_b", "c0_saved"), (c1_t, "lnx_g", "lnx_b", "c1_saved")):
                    for c in range(2):
                        act.wait_ge(s["c_turned"], j * PER["c_turned"] + c + 1)
                        act.activation(dst[0:CK[c], c, :], D[0][0:CK[c], c * BANK:(c + 1) * BANK], ACT.Identity,
                                       scale=col(g, c, CK[c]), bias=col(b, c, CK[c])).then_inc(s[name], 1)

            def context_k0(j):
                for e in range(2):
                    act.wait_ge(s["k0_mm"], j * PER["k0_mm"] + e + 1)
                    act.activation(k0_t[:, e, :], D[1][:, e * BANK:(e + 1) * BANK], ACT.Identity, bias=col("bk", e)).then_inc(s["k0_saved"], 1)

            def context_v0(j):
                act.wait_ge(s["v0_mm"], j * PER["v0_mm"] + 1)
                act.activation(v0[:, :, :].rearrange("p t d -> p (t d)"), D[3][:, :], ACT.Copy).then_inc(s["v0_saved"], 1)

            def context_k1(j):
                act.wait_ge(s["k1c_mm"], j * PER["k1c_mm"] + 1)
                act.activation(k1c[:, :, :].rearrange("p t d -> p (t d)"), D[1][:, :], ACT.Copy).then_inc(s["k1c_saved"], 1)
                act.activation(c_sq[:, :], D[1][:, :], ACT.Square).then_inc(s["c_sq"], 1)

            def context_k1_turned(j):
                for c in range(2):
                    act.wait_ge(s["k1c_turned"], j * PER["k1c_turned"] + c + 1)
                    act.activation(k1_t[:, c, :, 0:SEQ], D[1][:, c * BANK:(c + 1) * BANK].rearrange("p (b k) -> p b k", b=2),
                                   ACT.Copy).then_inc(s["k1c_placed"], 1)

            def context_v1(j):
                act.wait_ge(s["v1c_mm"], j * PER["v1c_mm"] + 1)
                act.activation(v1[:, :, 0:2, :], D[3][:, :].rearrange("p (b k n) -> p b k n", b=2, k=2), ACT.Copy).then_inc(s["v1c_saved"], 1)

            def pair(it, more):
                def after(name, k):
                    act.wait_ge(s[name], it * PER[name] + k)

                def turned(n, g=None, b=None):
                    after("turned", 2 * n + 1)
                    if g is None:
                        act.activation(x_t[:, 0, :], TB[:, 0:BANK], ACT.Copy).then_inc(s["turned_act"], 1)
                    else:
                        act.activation(x_t[:, 0, :], TB[:, 0:BANK], ACT.Identity, scale=col(g), bias=col(b)).then_inc(s["turned_act"], 1)

                def exps(quad, sp, n, keys):
                    after("maxed", quad + 1)
                    if quad >= 2:
                        after("p_turned", quad - 1)
                    for r in range(n):
                        act.activation(pe_[:, quad % 2, r * keys:(r + 1) * keys], sp[:, r * keys:(r + 1) * keys], ACT.Exp,
                                       bias=negm[:, quad % 2, r:r + 1], accum_out=rsum[:, quad % 2, r:r + 1]).then_inc(s["pexp"], 1)

                turned(0, "ln1_g", "ln1_b")
                after("q0_mm", 1)
                act.activation(q0_t[:, 0, :], D[3][:, 0:BANK], ACT.Identity, scale=sc_attn0, bias=bqs[:, 0:1]).then_inc(s["q0_act"], 1)
                after("max0", 1)
                for r in range(4):
                    act.activation(pe_[:, 0, r * SEQ:(r + 1) * SEQ], D[0][:, r * SEQ:(r + 1) * SEQ], ACT.Exp,
                                   bias=negm[:, 0, r:r + 1], accum_out=rsum[:, 0, r:r + 1]).then_inc(s["exp0"], 1)
                after("p0_turned", 1)
                act.activation(p_t[:, 0, 0:BANK], TB[:, 0:BANK], ACT.Copy).then_inc(s["p0_act"], 1)
                after("ctx0_mm", 1)
                act.activation(o_t[:, 0, :], D[1][:, 0:BANK], ACT.Copy).then_inc(s["ctx0_act"], 1)
                if more:
                    context_turned(it + 1)
                    context_k0(it + 1)
                turned(1)
                if more:
                    context_v0(it + 1)
                turned(2)
                after("cq_mm", 1)
                act.activation(cq[0:LAT, :], D[1][0:LAT, 0:BANK], ACT.Identity, bias=col("bdq", 0, LAT)).then_inc(s["cq_saved"], 1)

                def head_saved(n):
                    after("head_mm", n + 1)
                    act.activation(qh[:, n % 4, :], head_bank(n)[0:KEYW, :], ACT.Copy, scale=sc_mla).then_inc(s["head_saved"], 1)

                def o_saved(k):
                    after("pv_mm", k * QUADS + QUADS // 2)
                    act.activation(o_t[:, 0, :], OB[0], ACT.Copy).then_inc(s["o_act"], 1)

                for n in range(4):
                    head_saved(n)
                exps(0, D[0], 4, SEQ)
                exps(1, D[1], 4, SEQ)
                for q in range(QUADS):
                    if q + 4 < NH:
                        head_saved(q + 4)
                    if q + 2 < QUADS:
                        exps(q + 2, D[q % 2], 4, SEQ)
                    if q == QUADS // 2 + 1:
                        o_saved(0)
                if more:
                    context_k1(it + 1)
                turned(3, "lnl_g", "lnl_b")
                after("q1_mm", 1)
                act.activation(sq[:, 0, :], D[0][:, :], ACT.Square).then_inc(s["sq"], 1)
                after("k1l_mm", 1)
                act.activation(sq[:, 1, :], D[1][:, :], ACT.Square).then_inc(s["sq"], 1)
                after("v1l_mm", 1)
                act.activation(v1[:, :, 2:4, :], D[3][:, :].rearrange("p (b k n) -> p b k n", b=2, k=2), ACT.Copy).then_inc(s["v1l_saved"], 1)
                after("q1_turned", 1)
                act.activation(q1_t[:, 0, :], TB[:, 0:BANK], ACT.Copy, scale=gamma[:, 0:1]).then_inc(s["q1_act"], 1)
                after("k1l_turned", 1)
                act.activation(k1_t[:, 0, :, SEQ:2 * SEQ], D[3][:, 0:BANK].rearrange("p (b k) -> p b k", b=2), ACT.Copy).then_inc(s["k1l_act"], 1)
                exps(QUADS, D[0], 2, 2 * SEQ)
                exps(QUADS + 1, D[1], 2, 2 * SEQ)
                for q in range(QUADS):
                    after("p_turned", QUADS + q + 1)
                    if q >= 2:
                        after("pv_mm", QUADS + q - 1)
                    act.activation(p_t[:, q % 2, 0:BANK], TB[:, 0:BANK], ACT.Copy).then_inc(s["pt_act"], 1)
                    if q + 2 < QUADS:
                        exps(QUADS + q + 2, D[q % 2], 2, 2 * SEQ)
                    if q == QUADS // 2 + 1:
                        o_saved(1)
                if more:
                    context_k1_turned(it + 1)
                turned(4)
                after("p5_mm", 1)
                act.activation(p5_t[:, :], D[1][0:LR, 0:BANK], ACT.Copy).then_inc(s["p5_saved"], 1)
                for m in range(FF // P):
                    after("h_mm", m + 1)
                    act.activation(h_sb[:, m, :], [D[0], D[3]][m % 4 // 2][:, m % 2 * BANK:(m % 2 + 1) * BANK],
                                   ACT.Gelu_apprx_tanh, bias=col("b1", m)).then_inc(s["gelu"], 1)
                after("qt_mm", 1)
                act.activation(qt5[:, :], D[1][0:LR, BANK:2 * BANK], ACT.Copy).then_inc(s["qt_saved"], 1)
                if more:
                    context_v1(it + 1)

            context_turned(0)
            context_k0(0)
            context_v0(0)
            context_k1(0)
            context_k1_turned(0)
            context_v1(0)
            with act.Fori(0, PAIRS - 1) as it:
                pair(it, True)
            pair(PAIRS - 1, False)

        @block.tensor
        def _(pe):
            pe.wait_ge(s_in, loaded)
            for h in range(NH):
                pe.matmul(D[0][0:LAT + 1, h * (LAT + 1):(h + 1) * (LAT + 1)], uq_t[:, h, :], uk_t[:, h, :], start=True, stop=True)
            for h in range(NH):
                at = h % 4 * LAT
                pe.matmul(D[1][at:at + LAT, h // 4 * DM:(h // 4 + 1) * DM], uv_t[:, h, :], w_o[:, h, :], start=True, stop=True)
            pe.wait_ge(s_set, 2)
            for h in range(NH):
                pe.matmul(D[2][:, 0:DM], buv_rep[:, h, :], w_o[:, h, :], start=h == 0, stop=h == NH - 1)
            for c in range(2):
                pe.matmul(D[2][:, BANK:BANK + DM], bv_rep[:, c, :], wo0[:, c, :], start=c == 0, stop=c == 1)
            pe.wait_ge(s_abs, 1)
            pe.matmul(D[3][:, 0:1], ones[:, :], scales[:, 0:1], start=True, stop=True).then_inc(s_fold, 1)
            pe.wait_ge(s_set, SETUP)

            def wait(name, j, k):
                pe.wait_ge(s[name], j * PER[name] + k)

            def rows_times(dst, src_t, w, name, ks=(P, P), lo=0, n=DM, by_bank=False):
                for t in range(PT_):
                    for c in range(2):
                        last = pe.matmul(dst[:, t * n:(t + 1) * n], src_t[0:ks[c], c, t * P:(t + 1) * P],
                                         w[0:ks[c], c, lo:lo + n], start=c == 0, stop=c == 1)
                    if t == PT_ - 1 or (by_bank and t == 1):
                        last.then_inc(s[name], 1)

            def cols_times(dst, w, src_t, name, ks=(P, P)):
                for e in range(2):
                    for c in range(2):
                        last = pe.matmul(dst[:, e * BANK:(e + 1) * BANK], w[0:ks[c], c, e * P:(e + 1) * P],
                                         src_t[0:ks[c], c, :], start=c == 0, stop=c == 1)
                    last.then_inc(s[name], 1)

            def turn_rows(dst, src, name, width=DM):
                for c in range(2):
                    w = min(P, width - c * P)
                    for t in range(PT_):
                        last = pe.transpose(dst[0:w, c * BANK + t * P:c * BANK + (t + 1) * P], src[:, t, c * P:c * P + w], ident[:, :])
                    last.then_inc(s[name], 1)

            def context_turn(j):
                wait("c_normed", j, PT_)
                turn_rows(D[0], c_nrm, "c_turned", DC)

            def context_k0(j):
                wait("c0_saved", j, 2)
                cols_times(D[1], wk0, c0_t, "k0_mm", CK)

            def context_v0(j):
                rows_times(D[3], c0_t, wv0, "v0_mm", CK)

            def context_k1(j):
                wait("k0_saved", j, 2)
                wait("c1_saved", j, 2)
                rows_times(D[1], c1_t, wkv1, "k1c_mm", CK)

            def context_k1_turn(j):
                wait("c_sq", j, 1)
                wait("k1c_normed", j, 1)
                turn_rows(D[1], k1c, "k1c_turned")

            def context_v1(j):
                wait("v0_saved", j, 1)
                rows_times(D[3], c1_t, wkv1, "v1c_mm", CK, lo=DM)

            def pair(it, more):
                def after(name, k):
                    wait(name, it, k)

                def turn(n):
                    for c in range(2):
                        for t in range(PT_):
                            if c == 0:
                                after("normed", 4 * n + t + 1)
                            last = pe.transpose(TB[:, c * BANK + t * P:c * BANK + (t + 1) * P], nrm[:, n % 2, t, c * P:(c + 1) * P], ident[:, :])
                        last.then_inc(s["turned"], 1)

                def turned(n):
                    after("turned_act", n + 1)
                    after("turned_dve", n + 1)

                turn(0)
                turned(0)
                after("v1c_saved", 1)
                cols_times(D[3], wq0, x_t, "q0_mm")
                after("k0_saved", 2)
                after("c1_saved", 2)
                after("q0_act", 1)
                after("q0_dve", 1)
                for r in range(4):
                    b, c = r // 2, r % 2
                    for e in range(2):
                        last = pe.matmul(D[0][:, r * SEQ:(r + 1) * SEQ], q0_t[:, e, b * SEQ + c * P:b * SEQ + (c + 1) * P],
                                         k0_t[:, e, b * SEQ:(b + 1) * SEQ], start=e == 0, stop=e == 1)
                last.then_inc(s["score0"], 1)
                after("exp0", 4)
                for b in range(2):
                    for kc in range(2):
                        for c in range(2):
                            at = (b * 2 + kc) * SEQ + c * P
                            src = (b * 2 + c) * SEQ + kc * P
                            last = pe.transpose(TB[:, at:at + P], pe_[:, 0, src:src + P], ident[:, :])
                    last.then_inc(s["p0_turned"], 1)
                after("k1c_placed", 2)
                after("p0_act", 1)
                after("p0_dve", 1)
                for e in range(2):
                    for b in range(2):
                        for kc in range(2):
                            last = pe.matmul(D[1][:, e * BANK + b * SEQ:e * BANK + (b + 1) * SEQ], v0[:, b * 2 + kc, e * P:(e + 1) * P],
                                             p_t[:, 0, (b * 2 + kc) * SEQ:(b * 2 + kc + 1) * SEQ], start=kc == 0, stop=kc == 1)
                    last.then_inc(s["ctx0_mm"], 1)
                after("ctx0_act", 1)
                after("ctx0_dve", 1)
                rows_times(D[3], o_t, wo0, "out0_mm", by_bank=True)
                if more:
                    context_turn(it + 1)
                    context_k0(it + 1)
                turn(1)
                turned(1)
                if more:
                    wait("c1_saved", it + 1, 2)
                rows_times(D[0], x_t, wf, "ffn0_mm", by_bank=True)
                if more:
                    context_v0(it + 1)
                turn(2)
                turned(2)
                if more:
                    wait("k0_saved", it + 1, 2)
                for c in range(2):
                    last = pe.matmul(D[1][0:LAT, 0:BANK], w_dq[:, c, :], x_t[:, c, :], start=c == 0, stop=c == 1)
                last.then_inc(s["cq_mm"], 1)
                for c in range(2):
                    last = pe.matmul(D[1][0:LAT + ROPE, BANK:2 * BANK], w_kv[:, c, :], x_t[:, c, :], start=c == 0, stop=c == 1)
                last.then_inc(s["cq_mm"], 1)
                rows_times(D[0], x_t, w_kv, "ckvn_mm", n=LAT)
                after("cq_saved", 1)
                if more:
                    wait("v0_saved", it + 1, 1)

                def head(n):
                    if n >= 2:
                        after("head_saved", n if n >= 4 else n - 1)
                    pe.matmul(head_bank(n)[0:KEYW, :], fold_q[:, n, :], cq[:, :], start=True, stop=True).then_inc(s["head_mm"], 1)

                def score(q):
                    hp, b = latent_quad(q)
                    after("head_saved", 2 * hp + 2)
                    for c in range(2):
                        for hh in range(2):
                            at = (c * 2 + hh) * SEQ
                            last = pe.matmul(D[q % 2][:, at:at + SEQ], qh[:, (2 * hp + hh) % 4, b * SEQ + c * P:b * SEQ + (c + 1) * P],
                                             kk[:, b * SEQ:(b + 1) * SEQ], start=True, stop=True)
                    last.then_inc(s["scored"], 1)

                def turn_p(quad, n, keys):
                    after("p_normed", pexp_before(quad + 1))
                    if quad:
                        after("pt_dve", quad)
                    if quad > QUADS:
                        after("pt_act", quad - QUADS)
                    for r in range(n):
                        c, hh = r // (n // 2), r % (n // 2)
                        for kc in range(keys // P):
                            at = (hh * (keys // P) + kc) * SEQ + c * P
                            last = pe.transpose(TB[:, at:at + P], pe_[:, quad % 2, r * keys + kc * P:r * keys + (kc + 1) * P], ident[:, :])
                    last.then_inc(s["p_turned"], 1)

                def values(q):
                    hp, b = latent_quad(q)
                    after("pt_dve", q + 1)
                    for hh in range(2):
                        h = 2 * hp + hh
                        at = h % 4 * LAT
                        for kc in range(2):
                            last = pe.matmul(OB[h // 4][at:at + LAT, b * SEQ:(b + 1) * SEQ], ckvn[:, b * 2 + kc, :],
                                             p_t[:, q % 2, (hh * 2 + kc) * SEQ:(hh * 2 + kc + 1) * SEQ], start=kc == 0, stop=kc == 1)
                    last.then_inc(s["pv_mm"], 1)

                for n in range(4):
                    head(n)
                after("kk_saved", 1)
                after("ckvn_saved", 1)
                score(0)
                score(1)
                for q in range(QUADS):
                    turn_p(q, 4, SEQ)
                    if q + 2 < QUADS:
                        score(q + 2)
                    if q + 4 < NH:
                        head(q + 4)
                    if q:
                        if q - 1 == QUADS // 2:
                            after("head_saved", NH)
                        values(q - 1)
                values(QUADS - 1)
                after("o_act", 1)
                after("o_dve", 1)
                rows_times(D[0], o_t, fold_v, "out1_mm", by_bank=True)
                if more:
                    context_k1(it + 1)
                turn(3)
                turned(3)
                after("x_added", 8)
                rows_times(D[0], x_t, wq1, "q1_mm")
                if more:
                    wait("c_sq", it + 1, 1)
                rows_times(D[1], x_t, wlkv1, "k1l_mm")
                rows_times(D[3], x_t, wlkv1, "v1l_mm", lo=DM)
                after("q1_normed", 1)
                turn_rows(TB, qk_n[:, 0, :, :], "q1_turned")
                after("v1l_saved", 1)
                after("k1l_normed", 1)
                turn_rows(D[3], qk_n[:, 1, :, :], "k1l_turned")

                def score1(q):
                    b, h = cross_quad(q)
                    at = h % 2 * DH
                    for c in range(2):
                        last = pe.matmul(D[q % 2][:, c * BANK:(c + 1) * BANK], q1_t[at:at + DH, h // 2, b * SEQ + c * P:b * SEQ + (c + 1) * P],
                                         k1_t[at:at + DH, h // 2, b, :], start=True, stop=True)
                    last.then_inc(s["scored"], 1)

                def values1(q):
                    b, h = cross_quad(q)
                    after("pt_dve", QUADS + q + 1)
                    after("pt_act", q + 1)
                    at = h % 2 * DH
                    for kc in range(4):
                        last = pe.matmul(OB[h // 2][at:at + DH, b * SEQ:(b + 1) * SEQ], v1[:, b, kc, h * DH:(h + 1) * DH],
                                         p_t[:, q % 2, kc * SEQ:(kc + 1) * SEQ], start=kc == 0, stop=kc == 3)
                    last.then_inc(s["pv_mm"], 1)

                for name in ("q1_act", "q1_dve", "k1l_act", "k1l_dve"):
                    after(name, 1)
                score1(0)
                score1(1)
                for q in range(QUADS):
                    turn_p(QUADS + q, 2, 2 * SEQ)
                    if q + 2 < QUADS:
                        score1(q + 2)
                    if q:
                        values1(q - 1)
                values1(QUADS - 1)
                after("o_act", 2)
                after("o_dve", 2)
                rows_times(D[0], o_t, wo1, "out1_mm", by_bank=True)
                if more:
                    context_k1_turn(it + 1)
                turn(4)
                turned(4)
                if more:
                    wait("k1c_placed", it + 1, 2)
                for c in range(2):
                    last = pe.matmul(D[1][0:LR, 0:BANK], u1[:, c, :], x_t[:, c, :], start=c == 0, stop=c == 1)
                last.then_inc(s["p5_mm"], 1)
                after("p5_saved", 1)
                for m in range(FF // P + 2):
                    if m < FF // P:
                        if m >= 4:
                            after("gelu", m - 3)
                        pe.matmul([D[0], D[3]][m % 4 // 2][:, m % 2 * BANK:(m % 2 + 1) * BANK], v1w[:, m * P:(m + 1) * P],
                                  p5_t[:, :], start=True, stop=True).then_inc(s["h_mm"], 1)
                    if m >= 2:
                        after("gelu", m - 1)
                        last = pe.matmul(D[1][0:LR, BANK:2 * BANK], u2[:, m - 2, :], h_sb[:, m - 2, :], start=m == 2, stop=m == FF // P + 1)
                last.then_inc(s["qt_mm"], 1)
                after("qt_saved", 1)
                for t in range(PT_):
                    last = pe.matmul(TB[:, t * DM:(t + 1) * DM], qt5[:, t * P:(t + 1) * P], v2w[:, :], start=True, stop=True)
                    if t % 2:
                        last.then_inc(s["y_mm"], 1)
                if more:
                    context_v1(it + 1)

            context_turn(0)
            context_k0(0)
            context_v0(0)
            context_k1(0)
            context_k1_turn(0)
            context_v1(0)
            with pe.Fori(0, PAIRS - 1) as it:
                pair(it, True)
            pair(PAIRS - 1, False)

        @block.vector
        def _(dve):
            dve.wait_ge(s_in, loaded)
            dve.wait_ge(s_const, 3)
            for h in range(NH):
                last = dve.tensor_scalar(buv_rep[:, h, :], ones[:, :], col("buv", h), None, ALU.mult)
            last.then_inc(s_set, 1)
            for c in range(2):
                last = dve.tensor_scalar(bv_rep[:, c, :], ones[:, :], col("bv", c), None, ALU.mult)
            last.then_inc(s_set, 1)
            dve.tensor_scalar(mask[:, :, :], mask_u8[:, :, :], 1.0, FLT_MAX, ALU.subtract, ALU.mult).then_inc(s_set, 1)
            dve.tensor_scalar(bqs[:, :], cols[:, COLS["bq"][0]:COLS["bq"][0] + 2], sc_attn0, None, ALU.mult).then_inc(s_set, 1)
            dve.scalar_tensor_tensor(out=gamma[:, :], in0=col("qn"), scalar=sc_attn1, in1=col("kn"),
                                     op0=ALU.mult, op1=ALU.mult).then_inc(s_set, 1)
            dve.wait_ge(s_fold, 1)
            prod = D[0][0:LAT + 1, 0:NH * (LAT + 1)].rearrange("p (h n) -> p h n", h=NH)
            dve.tensor_copy(fold_q[:, :, 0:LAT], prod[:, :, 0:LAT]).then_inc(s_set, 1)
            dve.tensor_copy(fold_q[:, :, KEYW - 1:KEYW], prod[:, :, LAT:LAT + 1]).then_inc(s_set, 1)
            dve.tensor_copy(fold_v[:, :, :], D[1][:, 0:2 * DM].rearrange("p (c n) -> p c n", c=2)).then_inc(s_set, 1)
            dve.tensor_tensor(row("bo"), D[2][:, 0:DM], row("bo"), ALU.add).then_inc(s_set, 1)
            dve.tensor_tensor(row("bo0"), D[2][:, BANK:BANK + DM], row("bo0"), ALU.add).then_inc(s_set, 1)
            dve.tensor_scalar(scales[:, 1:2], D[3][:, 0:1], 1.0 / (DM * DM), EPS, ALU.mult, ALU.max).then_inc(s_set, 1)
            dve.wait_ge(s_set, 11)
            dve.tensor_scalar(scales[:, 2:3], scales[:, 1:2], 0.5, None, ALU.mult).then_inc(s_set, 1)
            dve.tensor_scalar(scales[:, 3:4], scales[:, 1:2], -0.5, None, ALU.mult).then_inc(s_set, 1)
            dve.wait_ge(s_set, 13)
            flat = wf[:, :, :].rearrange("p c n -> p (c n)")
            dve.tensor_scalar(tern[:, 1, :], flat, scales[:, 2:3], scales[:, 1:2], ALU.is_gt, ALU.mult).then_inc(s_set, 1)
            dve.tensor_scalar(tern[:, 2, :], flat, scales[:, 3:4], scales[:, 1:2], ALU.is_lt, ALU.mult).then_inc(s_set, 1)
            dve.wait_ge(s_set, 15)
            dve.tensor_tensor(flat, tern[:, 1, :], tern[:, 2, :], ALU.subtract).then_inc(s_set, 1)
            dve.memset(cq[LAT:LAT + 1, :], 1.0).then_inc(s_set, 1)
            dve.memset(kk[LAT + ROPE:KEYW, :], 1.0).then_inc(s_set, 1)

            def context_norm(j):
                def after(name, k):
                    dve.wait_ge(s[name], j * PER[name] + k)

                after("c_loaded", 16)
                for t in range(PT_):
                    dve.bn_stats(c_stats[:, t, :], ctx_sb[:, t, :]).then_inc(s["c_stats"], 1)
                after("c_stats", 4)
                dve.memset(rider[:, 0:1], 0.0)
                for t in range(PT_):
                    dve.bn_aggr(c_moments[:, t, :], c_stats[:, t, :]).then_inc(s["c_moments"], 1)
                after("c_moments", 4)
                dve.tensor_scalar(c_var[:, :], c_moments[:, :, 1], EPS, None, ALU.add).then_inc(s["c_var"], 1)

            def context_scale(j):
                dve.wait_ge(s["c_rstd"], j * PER["c_rstd"] + 1)
                for t in range(PT_):
                    dve.tensor_scalar(c_nrm[:, t, :], ctx_sb[:, t, :], c_moments[:, t, 0:1], c_rstd[:, t:t + 1],
                                      ALU.subtract, ALU.mult).then_inc(s["c_normed"], 1)

            def context_squares(j):
                dve.wait_ge(s["c_sq"], j * PER["c_sq"] + 1)
                dve.tensor_reduce(c_ss[:, :], c_sq[:, :].rearrange("p (a d) -> p a d", d=DH), AX_X, ALU.add).then_inc(s["c_ss"], 1)
                dve.wait_ge(s["c_ss"], j * PER["c_ss"] + 1)
                dve.tensor_scalar(c_ms[:, :], c_ss[:, :], 1.0 / DH, 1e-16, ALU.mult, ALU.max).then_inc(s["c_ms"], 1)

            def pair(it, more):
                def after(name, k):
                    dve.wait_ge(s[name], it * PER[name] + k)

                def tile_of(t, n=1):
                    return x_sb[:, bass.ds(it * PT_ + t, n), :]

                def statistics(n, t):
                    dve.bn_stats(stats[:, n % 2, t, :], tile_of(t).rearrange("p a d -> p (a d)")).then_inc(s["stats"], 1)

                def layernorm(n, twice=False):
                    after("stats", 4 * n + 4)
                    dve.memset(rider[:, 1:2], 0.0)
                    for t in range(PT_):
                        dve.bn_aggr(moments[:, n % 2, t, :], stats[:, n % 2, t, :]).then_inc(s["moments"], 1)
                    after("moments", 4 * n + 4)
                    dve.tensor_scalar(var[:, n % 2, :], moments[:, n % 2, :, 1], 1.0 + EPS if twice else 1.0,
                                      EPS * EPS if twice else EPS, ALU.mult, ALU.add).then_inc(s["var"], 1)
                    after("rstd", n + 1)
                    if n >= 2:
                        after("turned", 2 * (n - 1))
                    for t in range(PT_):
                        dve.tensor_scalar(nrm[:, n % 2, t, :], tile_of(t).rearrange("p a d -> p (a d)"), moments[:, n % 2, t, 0:1],
                                          rstd[:, n % 2, t:t + 1], ALU.subtract, ALU.mult).then_inc(s["normed"], 1)

                def turned(n, g=None, b=None):
                    after("turned", 2 * n + 2)
                    src = TB[:, BANK:2 * BANK]
                    if g is None:
                        dve.tensor_copy(x_t[:, 1, :], src).then_inc(s["turned_dve"], 1)
                    else:
                        dve.tensor_scalar(x_t[:, 1, :], src, col(g, 1), col(b, 1), ALU.mult, ALU.add).then_inc(s["turned_dve"], 1)

                def mean_square(k):
                    after("sq", k + 1)
                    dve.tensor_reduce(ss[:, k, :], sq[:, k, :].rearrange("p (a d) -> p a d", d=DH), AX_X, ALU.add).then_inc(s["ss"], 1)
                    after("ss", k + 1)
                    dve.tensor_scalar(ms[:, k, :], ss[:, k, :], 1.0 / DH, 1e-16, ALU.mult, ALU.max).then_inc(s["ms"], 1)

                def rms_norm(k, src, name):
                    after("rms", k + 1)
                    dve.tensor_tensor(qk_n[:, k, :, :].rearrange("p t (h d) -> p (t h) d", d=DH), src.rearrange("p (a d) -> p a d", d=DH),
                                      rms[:, k, :].unsqueeze(2).broadcast_to([P, 4 * PT_, DH]), ALU.mult).then_inc(s[name], 1)

                def add_to_x(src, name, k, done, n=None):
                    for half in range(2):
                        after(name, k + half + 1)
                        dve.tensor_tensor(tile_of(2 * half, 2), src[:, half * BANK:(half + 1) * BANK].rearrange("p (t d) -> p t d", d=DM),
                                          tile_of(2 * half, 2), ALU.add).then_inc(s["x_added"], 1)
                        if n is not None:
                            after("x_added", done + half + 1)
                            dve.memset(rider[:, 0:1], 0.0)
                            for t in range(2 * half, 2 * half + 2):
                                statistics(n, t)

                dve.memset(rider[:, 0:1], 0.0)
                for t in range(PT_):
                    statistics(0, t)
                layernorm(0, twice=True)
                turned(0, "ln1_g", "ln1_b")
                after("q0_mm", 2)
                dve.tensor_scalar(q0_t[:, 1, :], D[3][:, BANK:2 * BANK], sc_attn0, bqs[:, 1:2], ALU.mult, ALU.add).then_inc(s["q0_dve"], 1)
                after("score0", 1)
                dve.tensor_reduce(negm[:, 0, :], D[0][:, :].rearrange("p (r k) -> p r k", k=SEQ), AX_X, ALU.max, negate=True).then_inc(s["max0"], 1)
                if more:
                    context_norm(it + 1)
                after("p0_turned", 2)
                dve.tensor_copy(p_t[:, 0, BANK:2 * BANK], TB[:, BANK:2 * BANK]).then_inc(s["p0_dve"], 1)
                after("exp0", 4)
                dve.reciprocal(rinv[:, 0, :], rsum[:, 0, :]).then_inc(s["rinv0"], 1)
                if more:
                    context_scale(it + 1)
                after("ctx0_mm", 2)
                dve.tensor_copy(o_t[:, 1, :], D[1][:, BANK:2 * BANK]).then_inc(s["ctx0_dve"], 1)
                after("rinv0", 1)
                after("x_biased", 1)
                for half in range(2):
                    after("out0_mm", half + 1)
                    for t in range(2 * half, 2 * half + 2):
                        x_tile = tile_of(t).rearrange("p a d -> p (a d)")
                        dve.scalar_tensor_tensor(out=x_tile, in0=D[3][:, t * DM:(t + 1) * DM], scalar=rinv[:, 0, t:t + 1],
                                                 in1=x_tile, op0=ALU.mult, op1=ALU.add).then_inc(s["x_added"], 1)
                    after("x_added", 2 * half + 2)
                    dve.memset(rider[:, 0:1], 0.0)
                    for t in range(2 * half, 2 * half + 2):
                        statistics(1, t)
                layernorm(1)
                turned(1)
                add_to_x(D[0], "ffn0_mm", 0, 4, 2)
                layernorm(2)
                turned(2)
                after("cq_mm", 2)
                dve.tensor_scalar(kk[0:LAT + ROPE, :], D[1][0:LAT + ROPE, BANK:2 * BANK], col("bkv", 0, LAT + ROPE), None, ALU.add).then_inc(s["kk_saved"], 1)
                after("ckvn_mm", 1)
                dve.tensor_tensor(ckvn[:, :, :], D[0][:, 0:PT_ * LAT].rearrange("p (t d) -> p t d", d=LAT),
                                  row("bdkv", LAT).unsqueeze(1).broadcast_to([P, PT_, LAT]), ALU.add).then_inc(s["ckvn_saved"], 1)

                def quad_max(quad, sp, n, batch=None):
                    after("scored", quad + 1)
                    if batch is not None:
                        keys = sp[:, :].rearrange("p (c k) -> p c k", c=2)[:, :, 0:SEQ]
                        m = mask[:, bass.ds(it * 2 + batch, 1), :].broadcast_to([P, 2, SEQ])
                        dve.tensor_tensor(keys, keys, m, ALU.add).then_inc(s["masked"], 1)
                        after("masked", quad - QUADS + 1)
                    dve.tensor_reduce(negm[:, quad % 2, 0:n], sp[:, :].rearrange("p (r k) -> p r k", r=n), AX_X, ALU.max,
                                      negate=True).then_inc(s["maxed"], 1)

                def quad_norm(quad, n, keys):
                    after("pexp", pexp_before(quad + 1))
                    dve.reciprocal(rinv[:, quad % 2, 0:n], rsum[:, quad % 2, 0:n]).then_inc(s["rinv"], 1)
                    after("rinv", quad + 1)
                    for r in range(n):
                        p_row = pe_[:, quad % 2, r * keys:(r + 1) * keys]
                        dve.tensor_scalar(p_row, p_row, rinv[:, quad % 2, r:r + 1], None, ALU.mult).then_inc(s["p_normed"], 1)

                def quad_turned(quad, lo):
                    after("p_turned", quad + 1)
                    if quad >= 2:
                        after("pv_mm", quad - 1)
                    dve.tensor_copy(p_t[:, quad % 2, lo:], TB[:, lo:]).then_inc(s["pt_dve"], 1)

                def o_saved(k):
                    after("pv_mm", (k + 1) * QUADS)
                    dve.tensor_copy(o_t[:, 1, :], OB[1]).then_inc(s["o_dve"], 1)

                quad_max(0, D[0], 4)
                quad_max(1, D[1], 4)
                quad_norm(0, 4, SEQ)
                for q in range(QUADS):
                    quad_turned(q, 0)
                    if q + 1 < QUADS:
                        quad_norm(q + 1, 4, SEQ)
                    if q + 2 < QUADS:
                        quad_max(q + 2, D[q % 2], 4)
                o_saved(0)
                after("x_biased", 2)
                add_to_x(D[0], "out1_mm", 0, 6, 3)
                layernorm(3, twice=True)
                turned(3, "lnl_g", "lnl_b")
                mean_square(0)
                mean_square(1)
                rms_norm(0, D[0][:, :], "q1_normed")
                rms_norm(1, D[1][:, :], "k1l_normed")
                after("q1_turned", 2)
                dve.tensor_scalar(q1_t[:, 1, :], TB[:, BANK:2 * BANK], gamma[:, 0:1], None, ALU.mult).then_inc(s["q1_dve"], 1)
                after("k1l_turned", 2)
                dve.tensor_copy(k1_t[:, 1, :, SEQ:2 * SEQ], D[3][:, BANK:2 * BANK].rearrange("p (b k) -> p b k", b=2)).then_inc(s["k1l_dve"], 1)
                quad_max(QUADS, D[0], 2, cross_quad(0)[0])
                quad_max(QUADS + 1, D[1], 2, cross_quad(1)[0])
                if more:
                    context_squares(it + 1)
                quad_norm(QUADS, 2, 2 * SEQ)
                for q in range(QUADS):
                    quad_turned(QUADS + q, BANK)
                    if q + 1 < QUADS:
                        quad_norm(QUADS + q + 1, 2, 2 * SEQ)
                    if q + 2 < QUADS:
                        quad_max(QUADS + q + 2, D[q % 2], 2, cross_quad(q + 2)[0])
                o_saved(1)
                after("x_biased", 3)
                add_to_x(D[0], "out1_mm", 2, 8, 4)
                layernorm(4)
                turned(4)
                after("x_biased", 4)
                add_to_x(TB, "y_mm", 0, 10)

            context_norm(0)
            context_scale(0)
            context_squares(0)
            with dve.Fori(0, PAIRS - 1) as it:
                pair(it, True)
            pair(PAIRS - 1, False)




def layout(a):
    import numpy as np
    f = {k: np.asarray(v) for k, v in a.items()}

    def chunked(v):
        v = v.reshape(CH, P, -1)
        return v.transpose(1, 0, 2).reshape(P, -1)

    def column(v):
        v = np.concatenate([v, np.zeros(-len(v) % P, v.dtype)])
        return v.reshape(-1, P).T

    def with_bias(w, b):
        return np.concatenate([w, b[None]]).reshape(len(w) + 1, NH, -1)

    m, x0, a1, x1, f1 = "L0_attn_", "L0_xattn_", "L1_attn_", "L1_xattn_", "L1_ffn_"
    cols = np.stack([np.concatenate([chunked(f[m + n]) for n in names], axis=1) for names in (
        ("conv_w", "conv_b", "dt_proj_b", "D", "A_log"),
        ("conv_w_b", "conv_b_b", "dt_proj_b_b", "D_b", "A_b_log"))], axis=1)
    vectors = {
        "ln2_g": f[x0 + "ln2_g"], "ln2_b": f[x0 + "ln2_b"], "lnx_g": f[x1 + "ln_x_g"], "lnx_b": f[x1 + "ln_x_b"],
        "ln1_g": f[x0 + "ln1_g"], "ln1_b": f[x0 + "ln1_b"], "lnl_g": f[x1 + "ln_l_g"], "lnl_b": f[x1 + "ln_l_b"],
        "bq": f[x0 + "bq"], "bk": f[x0 + "bk"], "qn": np.tile(f[x1 + "qn_g"], 2), "kn": np.tile(f[x1 + "kn_g"], 2),
        "bdq": f[a1 + "b_DQ"], "bkv": np.concatenate([f[a1 + "b_DKV"], f[a1 + "b_KR"]]), "b1": f[f1 + "b1"],
        "buv": f[a1 + "b_UV"], "bv": f[x0 + "bv"],
    }
    out = {
        "x": f["x"].reshape(NBATCH * SEQ, DM),
        "ident": np.eye(P, dtype=np.float32),
        "mamba_cols": cols,
        "in_w": f[m + "in_proj_w"].T,
        "xp_w": np.stack([f[m + "x_proj_w"].T, f[m + "x_proj_w_b"].T]),
        "dt_w": np.stack([f[m + "dt_proj_w"].T, f[m + "dt_proj_w_b"].T]),
        "out_w": f[m + "out_proj_w"].T,
        "ctx": f["ctx_768"].reshape(NBATCH * SEQ, DC),
        "mask": f["mask_BxS2_bk0"].reshape(1, NBATCH * SEQ),
        "lcols": np.concatenate([column(vectors[n]) for n in COLS], axis=1),
        "lrows": np.concatenate([f[x0 + "bo"], f[a1 + "b_O"], f[x1 + "bo"], f[f1 + "b2"], f[a1 + "b_DKV"]])[None],
        "wq0": f[x0 + "Wq"], "wk0": f[x0 + "Wk"], "wv0": f[x0 + "Wv"], "wo0": f[x0 + "Wo"],
        "wf": f["L0_ffn_weight"].T,
        "w_dq": f[a1 + "W_DQ"], "w_kv": np.concatenate([f[a1 + "W_DKV"], f[a1 + "W_KR"]], axis=1),
        "uq_t": with_bias(f[a1 + "W_UQ"], f[a1 + "b_UQ"]).transpose(2, 1, 0),
        "uk_t": with_bias(f[a1 + "W_UK"], f[a1 + "b_UK"]).transpose(2, 1, 0),
        "uv_t": f[a1 + "W_UV"].reshape(LAT, NH, DK).transpose(2, 1, 0),
        "w_o": f[a1 + "W_O"],
        "fold_r": with_bias(f[a1 + "W_QR"], f[a1 + "b_QR"]),
        "wq1": f[x1 + "Wq"].T, "wkv1": f[x1 + "Wkv"].T, "wlkv1": f[x1 + "Wlkv"].T, "wo1": f[x1 + "Wo"].T,
        "u1": f[f1 + "U1"], "v1w": f[f1 + "V1"], "u2": f[f1 + "U2"], "v2w": f[f1 + "V2"],
    }
    return {k: np.ascontiguousarray(v) for k, v in out.items()}


def decoder_kernel(nc, dram):
    with nc.sbuf_tensor("x_sb", [P, TILES, DM], F32) as x_sb, nc.sbuf_tensor("ident_sb", [P, P], F32) as ident:
        mamba_block(nc, dram, x_sb, ident)
        layers_block(nc, dram, x_sb, ident)


def kernel(**inputs):
    import numpy as _np
    import concourse.bacc as _bacc
    from concourse.bass_utils import run_bass_kernel_spmd as _run

    nc = _bacc.Bacc("TRN2", target_bir_lowering=False, num_devices=1)
    arrays, dram = {}, {}
    for name, v in layout(inputs).items():
        arrays[f"{name}_dram"] = v
        dram[name] = nc.dram_tensor(f"{name}_dram", v.shape, mybir.dt.from_np(v.dtype), kind="ExternalInput").ap()
    dram["out"] = nc.dram_tensor("out_dram", (NBATCH * SEQ, DM), F32, kind="ExternalOutput").ap()
    decoder_kernel(nc, dram)
    r = _run(nc, [arrays], core_ids=[0])
    return _np.asarray(r.results[0]["out_dram"]).reshape(NBATCH, SEQ, DM)
```

```python
from contextlib import ExitStack

import concourse.bass as bass
from concourse import mybir

F32 = mybir.dt.float32
U8 = mybir.dt.uint8
ALU = mybir.AluOpType
ACT = mybir.ActivationFunctionType
AX_X = mybir.AxisListType.X

P = 128
NBATCH, SEQ, DM = 8, 256, 256
TILES = NBATCH * SEQ // P
EPS = 1e-5

DIN, NSTATE, TAPS, RANK = 512, 16, 4, 64
CH = DIN // P
HALVES = 2
HB = NBATCH // HALVES
HT = HB * SEQ
HTILES = HT // P
PAD = TAPS - 1
ROW = PAD + SEQ + PAD
BANK = 512
XD = RANK + 2 * NSTATE

C_CONVW, C_CONVB, C_DTB, C_D, C_ALOG = 0, CH * TAPS, CH * TAPS + CH, CH * TAPS + 2 * CH, CH * TAPS + 3 * CH
NCOLS = C_ALOG + CH * NSTATE


MAMBA_SHARED = (("in_w", (P, 2, 2 * DIN)), ("xp_w", (P, 2, CH, XD)), ("dt_w", (P, 2, DIN)), ("norm_t", (P, 2, HT)),
                ("xpad", (P, CH, HB, ROW)), ("xc_tail", (P, 2, HT)), ("xdbl", (P, 2, HT)))


def columns(shape):
    n = 1
    for k in shape[1:]:
        n *= k
    return n


def carve(region, shapes):
    views, at = {}, 0
    for name, shape in shapes:
        n = columns(shape)
        view = region[0:shape[0], at:at + n]
        if len(shape) == 3:
            view = view.rearrange("p (a b) -> p a b", a=shape[1])
        elif len(shape) == 4:
            view = view.rearrange("p (a b c) -> p a b c", a=shape[1], b=shape[2])
        views[name] = view
        at += n
    return views


def mamba_block(nc, dram, x_sb, ident, shared, load_next):
    with ExitStack() as ctx:
        def sb(name, shape, dt=F32):
            return ctx.enter_context(nc.sbuf_tensor(name, shape, dt))

        def sem(name):
            return ctx.enter_context(nc.semaphore(name))

        own = carve(shared, MAMBA_SHARED)
        in_w = own["in_w"]
        xp_w = own["xp_w"]
        dt_w = own["dt_w"]
        out_w = sb("out_w", [P, CH, DM])
        cols = sb("cols", [P, 2, NCOLS])
        a_neg = sb("a_neg", [P, 2, CH * NSTATE])
        a_exp = sb("a_exp", [P, 2, CH * NSTATE])
        d_diag = sb("d_diag", [P, 2, CH, P])
        pow_c = sb("pow_c", [P, 2, HTILES])

        stats = sb("stats", [P, TILES, 6])
        meanvar = sb("meanvar", [P, TILES, 2])
        rider = sb("rider", [P, 1])
        prider = sb("mamba_prider", [P, 2])
        vareps = sb("vareps", [P, TILES])
        rstd = sb("rstd", [P, TILES])
        work = sb("work", [P, CH, HT])
        normed = sb("normed", [P, HTILES, DM])
        norm_t = own["norm_t"]
        xpad = own["xpad"]
        xpad_mid = xpad[:, :, :, PAD:PAD + SEQ]
        gate = sb("gate", [P, CH, HT])
        xc_fwd = sb("xc_fwd", [P, CH, HT])
        xc_tail = own["xc_tail"]
        xc = [[xc_fwd[:, c, :] for c in range(CH)],
              [xc_tail[:, 0, :], xc_tail[:, 1, :], norm_t[:, 0, :], norm_t[:, 1, :]]]
        delta = work
        gated = work
        du = sb("du", [P, CH, HT])
        xdbl = own["xdbl"]
        bc = sb("bc", [P, 2, 2, HT])
        decay = sb("decay", [P, 2, HT])
        inject = sb("inject", [P, 2, HT])
        state = sb("state", [P, 2, HT])
        readout = sb("readout", [P, 2, HT])
        inject_of = [inject[:, 0, :], inject[:, 1, :], xc_fwd[:, 0, :], xc_fwd[:, 1, :]]
        h_of = [state[:, 0, :], state[:, 1, :], xc_fwd[:, 2, :], xc_fwd[:, 3, :]]
        soft_ln = [inject[:, 0, :], inject[:, 1, :], state[:, 0, :], state[:, 1, :]]
        soft_w = [readout[:, 0, :], readout[:, 1, :], decay[:, 0, :], decay[:, 1, :]]
        psum = ctx.enter_context(nc.psum_tensor("mamba_psum", [P, CH, 2 * BANK], F32))
        bc_dram = nc.dram_tensor("bc_rows", [2, 2 * NSTATE, HT], F32, kind="Internal").ap()

        names = """x_first x_second ident_loaded cols_loaded in_w_loaded w_loaded pads_zero xdbl_zero consts_set a_exped a_ready diag_ready stats_done mean_ready
            vareps_ready rstd_ready norm_ready tr_ready norm_t_ready inproj_ready xpad_read gate_read
            conv_first conv_step conv_sum_ready xc_ready xproj_ready xdbl_ready bc_stored b_even b_odd c_even c_odd
            dtproj_ready sp_relu sp_abs sp_exp sp_w sp_corr sp_diff_pool sp_diff_dve sp_ln delta_ready du_pool du_dve
            strip_and_scan decay_ready inject_ready readout_ready y_added y_saved_act y_saved_dve gated_ready
            outproj_ready out_read x_updated""".split()
        s = {n: sem(n) for n in names}
        bc_loaded = [[s["b_even"], s["b_odd"]], [s["c_even"], s["c_odd"]]]
        sums = [psum[:, c, :] for c in range(CH)]

        block = ctx.enter_context(nc.Block())

        def direction(hf, d):
            return hf * 2 + d

        Y_ADDS = NSTATE * CH + 2
        STRIPS = 4
        SCANS = STRIPS + NSTATE * CH

        def by_batch(ap):
            return ap.rearrange("p (b l) -> p b l", b=HB)

        @block.sync
        def _(sp):
            x_tiles = dram["x"].rearrange("(t p) d -> p t d", p=P)
            sp.dma_start(cols[:, :, :], dram["mamba_cols"]).then_inc(s["cols_loaded"], 16)
            sp.dma_start(ident[:, :], dram["ident"]).then_inc(s["ident_loaded"], 16)
            for hf in range(HALVES):
                lo, hi = hf * HTILES, (hf + 1) * HTILES
                sp.dma_start(x_sb[:, lo:hi, :], x_tiles[:, lo:hi, :]).then_inc(s[("x_first", "x_second")[hf]], 16)
            sp.dma_start(in_w[:, :, :], dram["in_w"].rearrange("(c p) n -> p c n", p=P)).then_inc(s["in_w_loaded"], 16)
            sp.dma_start(xp_w[:, :, :, :], dram["xp_w"].rearrange("d (c p) n -> p d c n", p=P)).then_inc(s["w_loaded"], 16)
            sp.dma_start(dt_w[:, :, :], dram["dt_w"].rearrange("d p n -> p d n")).then_inc(s["w_loaded"], 16)
            sp.dma_start(out_w[:, :, :], dram["out_w"].rearrange("(c p) n -> p c n", p=P)).then_inc(s["w_loaded"], 16)

            def load_row(kind, slot, d, n):
                rows = bc_dram[d].rearrange("(k n) t -> n k t", k=2)[:, kind:kind + 1, :]
                src = (rows[n:n + 1] if isinstance(n, int) else rows[bass.ds(n, 1)]).partition_broadcast(P)
                sp.dma_start(bc[:, slot, kind:kind + 1, :], src.rearrange("p a k t -> p (a k) t")).then_inc(bc_loaded[kind][slot], 16)

            with sp.Fori(0, HALVES) as hf:
                for d in range(2):
                    sp.wait_ge(s["xdbl_ready"], direction(hf, d) * 2 + 2)
                    sp.dma_start(bc_dram[d], xdbl[RANK:XD, d, :]).then_inc(s["bc_stored"], 16)
                    sp.wait_ge(s["bc_stored"], direction(hf, d) * 16 + 16)
                    for k in range(2):
                        if d:
                            sp.wait_ge(s["inject_ready"], direction(hf, d) * (NSTATE * CH) - (1 - k) * CH)
                        load_row(0, k, d, k)
                    for k in range(2):
                        if d:
                            sp.wait_ge(s["readout_ready"], direction(hf, d) * (NSTATE * CH) - (1 - k) * CH)
                        load_row(1, k, d, k)
                    with sp.Fori(0, NSTATE // 2 - 1) as j:
                        for k in range(2):
                            used = direction(hf, d) * (NSTATE * CH) + j * (2 * CH) + (k + 1) * CH
                            sp.wait_ge(s["inject_ready"], used)
                            load_row(0, k, d, j * 2 + (2 + k))
                            sp.wait_ge(s["readout_ready"], used)
                            load_row(1, k, d, j * 2 + (2 + k))
            sp.wait_ge(s["readout_ready"], HALVES * 2 * NSTATE * CH - 2 * CH)
            load_next(sp)

        @block.gpsimd
        def _(pool):
            pool.memset(pow_c[:, 0, :], EPS).then_inc(s["consts_set"], 1)
            pool.memset(pow_c[:, 1, :], -0.5).then_inc(s["consts_set"], 1)
            pool.memset(xpad[:, :, :, 0:PAD], 0.0).then_inc(s["pads_zero"], 1)
            pool.memset(xpad[:, :, :, PAD + SEQ:ROW], 0.0).then_inc(s["pads_zero"], 1)
            pool.memset(prider[:, :], 0.0).then_inc(s["x_updated"], 1)
            pool.wait_ge(s["consts_set"], 2)
            pool.wait_ge(s["x_updated"], 1)
            for hf in range(HALVES):
                half = slice(hf * HTILES, (hf + 1) * HTILES)
                pool.wait_ge(s["mean_ready"], (hf + 1) * HTILES)
                pool.tensor_tensor(vareps[:, half], meanvar[:, half, 1], pow_c[:, 0, :], ALU.add).then_inc(s["vareps_ready"], 1)
                pool.wait_ge(s["vareps_ready"], hf + 1)
                pool.tensor_tensor(rstd[:, half], vareps[:, half], pow_c[:, 1, :], ALU.pow).then_inc(s["rstd_ready"], 1)
            with pool.Fori(0, HALVES) as hf:
                for d in range(2):
                    dirs = direction(hf, d)
                    for c in range(0, CH, 2):
                        pool.wait_ge(s["sp_corr"], dirs * CH + c + 1)
                        pool.tensor_tensor(delta[:, c, :], delta[:, c, :], soft_w[c], ALU.subtract).then_inc(s["sp_diff_pool"], 1)
                    pool.wait_ge(s["delta_ready"], dirs * CH + 1)
                    pool.wait_ge(s["y_added"], dirs * Y_ADDS + 1)
                    pool.tensor_tensor(du[:, 0, :], delta[:, 0, :], xc[d][0], ALU.mult).then_inc(s["du_pool"], 1)
                    with pool.Fori(0, NSTATE // 2) as j:
                        for k in range(2):
                            pool.wait_ge(bc_loaded[0][k], dirs * (8 * NSTATE) + j * 16 + 16)
                            for c in range(CH):
                                if k == 0:
                                    if c == 0:
                                        pool.wait_ge(s["du_pool"], dirs + 1)
                                    else:
                                        pool.wait_ge(s["du_dve"], dirs * (CH - 1) + c)
                                step = k * CH + c
                                pool.wait_ge(s["strip_and_scan"], dirs * SCANS + j * (2 * CH) + step + 1)
                                pool.tensor_tensor(inject_of[c], du[:, c, :], bc[:, k, 0, :], ALU.mult).then_inc(s["inject_ready"], 1)
                for g in range(2):
                    pool.wait_ge(s["out_read"], hf * 2 + g + 1)
                    pool.tensor_tensor(prider[:, g:g + 1], prider[:, g:g + 1], prider[:, g:g + 1], ALU.mult)
                    x_rows = x_sb[:, bass.ds(hf * HTILES + 4 * g, 4), :]
                    pool.tensor_tensor(x_rows, du[:, g, :].rearrange("p (t d) -> p t d", d=DM),
                                       x_rows, ALU.add).then_inc(s["x_updated"], 1)

        @block.scalar
        def _(act):
            act.wait_ge(s["cols_loaded"], 16)
            act.activation(a_exp[:, :, :], cols[:, :, C_ALOG:NCOLS], ACT.Exp).then_inc(s["a_exped"], 1)
            with act.Fori(0, HALVES) as hf:
                def conv_first(d, c):
                    at = PAD * 2 if d else 0
                    act.activation(by_batch(xc[d][c]), xpad[:, c, :, at:at + SEQ],
                                   ACT.Identity, bias=cols[:, d, C_CONVB + c:C_CONVB + c + 1],
                                   scale=cols[:, d, C_CONVW + TAPS * c:C_CONVW + TAPS * c + 1]).then_inc(s["conv_first"], 1)

                def conv_silu(d, c):
                    act.wait_ge(s["conv_sum_ready"], direction(hf, d) * CH + c + 1)
                    act.activation(xc[d][c], xc[d][c], ACT.Silu).then_inc(s["xc_ready"], 1)

                def gate_silu(c):
                    act.wait_ge(s["inproj_ready"], hf * (2 * CH) + CH + c + 1)
                    act.activation(gate[:, c, :], sums[c], ACT.Silu).then_inc(s["gate_read"], 1)

                def save_xdbl(d):
                    for b in range(2):
                        act.wait_ge(s["xproj_ready"], direction(hf, d) * 2 + b + 1)
                        src = sums[CH - 1 if d else 0][0:XD, b * BANK:(b + 1) * BANK]
                        act.activation(xdbl[0:XD, d, b * BANK:(b + 1) * BANK], src, ACT.Copy).then_inc(s["xdbl_ready"], 1)

                act.wait_ge(s["tr_ready"], hf * 2 + 2)
                act.activation(norm_t[:, 1, :], sums[1], ACT.Copy).then_inc(s["norm_t_ready"], 1)
                act.wait_ge(s["pads_zero"], 2)
                for c in range(CH):
                    act.wait_ge(s["inproj_ready"], hf * (2 * CH) + c + 1)
                    act.activation(xpad_mid[:, c, :, :], by_batch(sums[c]), ACT.Copy).then_inc(s["xpad_read"], 1)
                    act.wait_ge(s["xpad_read"], hf * CH + c + 1)
                    conv_first(0, c)
                act.wait_ge(s["x_updated"], hf * 2 + 1)
                for c in range(2):
                    conv_silu(0, c)
                gate_silu(0)
                conv_silu(0, 2)
                gate_silu(1)
                conv_silu(0, 3)
                conv_first(1, 0)
                conv_first(1, 1)
                gate_silu(2)
                gate_silu(3)
                conv_silu(1, 0)
                conv_first(1, 2)
                conv_first(1, 3)
                conv_silu(1, 1)
                save_xdbl(0)
                conv_silu(1, 2)
                for d in range(2):
                    dirs = direction(hf, d)
                    if d:
                        for c in range(0, CH, 2):
                            act.wait_ge(s["y_added"], dirs * Y_ADDS - (CH - 1 - c))
                            act.activation(xpad_mid[:, c, :, :], by_batch(sums[c]), ACT.Copy).then_inc(s["y_saved_act"], 1)
                    def relu_abs(c):
                        act.wait_ge(s["dtproj_ready"], dirs * CH + c + 1)
                        bias = cols[:, d, C_DTB + c:C_DTB + c + 1]
                        act.activation(delta[:, c, :], sums[c], ACT.Relu, bias=bias).then_inc(s["sp_relu"], 1)
                        if d:
                            act.wait_ge(s["readout_ready"], dirs * (NSTATE * CH))
                        act.activation(soft_ln[c], sums[c], ACT.Abs, bias=bias).then_inc(s["sp_abs"], 1)

                    def exponential(c):
                        act.wait_ge(s["sp_abs"], dirs * CH + c + 1)
                        act.activation(du[:, c, :], soft_ln[c], ACT.Exp, scale=-1.0).then_inc(s["sp_exp"], 1)

                    for c in range(CH):
                        relu_abs(c)
                        if d == 0 and c == 0:
                            continue
                        if d == 0 and c == 1:
                            conv_silu(1, 3)
                            exponential(0)
                        exponential(c)
                    for c in range(CH):
                        act.wait_ge(s["sp_exp"], dirs * CH + c + 1)
                        act.activation(soft_ln[c], du[:, c, :], ACT.Ln, bias=1.0).then_inc(s["sp_ln"], 1)
                    if d == 0:
                        save_xdbl(1)
                    act.wait_ge(s["a_ready"], 1)
                    lo, hi = (1, SEQ) if d == 0 else (0, SEQ - 1)
                    with act.Fori(0, NSTATE // 2) as j:
                        for k in range(2):
                            for c in range(CH):
                                step = k * CH + c
                                if k == 0:
                                    act.wait_ge(s["delta_ready"], dirs * CH + c + 1)
                                act.wait_ge(s["strip_and_scan"], dirs * SCANS + j * (2 * CH) + step + 3)
                                act.activation(by_batch(decay[:, c % 2, :])[:, :, lo:hi], by_batch(delta[:, c, :])[:, :, lo:hi],
                                               ACT.Exp, scale=a_neg[:, d, bass.ds(j * 2 + (c * NSTATE + k), 1)]).then_inc(s["decay_ready"], 1)

                for g in range(2):
                    act.wait_ge(s["outproj_ready"], hf * 2 + g + 1)
                    act.activation(du[:, g, :], sums[2 + g], ACT.Copy).then_inc(s["out_read"], 1)

        @block.tensor
        def _(pe):
            pe.wait_ge(s["ident_loaded"], 16)
            with pe.Fori(0, HALVES) as hf:
                def x_proj(d):
                    for b in range(2):
                        for c in range(CH):
                            last = pe.matmul(sums[CH - 1 if d else 0][0:XD, b * BANK:(b + 1) * BANK], xp_w[:, d, c, :],
                                             xc[d][c][:, b * BANK:(b + 1) * BANK], start=c == 0, stop=c == CH - 1)
                        last.then_inc(s["xproj_ready"], 1)

                for c in range(2):
                    for t in range(HTILES):
                        pe.wait_ge(s["norm_ready"], hf * HTILES + t + 1)
                        last = pe.transpose(sums[c][:, t * P:(t + 1) * P], normed[:, t, c * P:(c + 1) * P], ident[:, :])
                    last.then_inc(s["tr_ready"], 1)
                pe.wait_ge(s["in_w_loaded"], 16)
                pe.wait_ge(s["norm_t_ready"], hf * 2 + 2)
                for m in range(2 * CH):
                    if m >= CH:
                        pe.wait_ge(s["xpad_read"], hf * CH + m - CH + 1)
                    for b in range(2):
                        for c in range(2):
                            last = pe.matmul(sums[m % CH][:, b * BANK:(b + 1) * BANK], in_w[:, c, m * P:(m + 1) * P],
                                             norm_t[:, c, b * BANK:(b + 1) * BANK], start=c == 0, stop=c == 1)
                    last.then_inc(s["inproj_ready"], 1)
                pe.wait_ge(s["xdbl_zero"], 1)
                pe.wait_ge(s["xc_ready"], direction(hf, 0) * CH + CH)
                pe.wait_ge(s["gate_read"], hf * CH + 1)
                pe.wait_ge(s["w_loaded"], 48)
                x_proj(0)
                for d in range(2):
                    dirs = direction(hf, d)
                    for c in range(CH):
                        if d == 0:
                            pe.wait_ge(s["xdbl_ready"], dirs * 2 + 2)
                            pe.wait_ge(s["gate_read"], hf * CH + c + 1)
                        elif c % 2 == 0:
                            pe.wait_ge(s["y_saved_act"], hf * 2 + c // 2 + 1)
                        else:
                            pe.wait_ge(s["y_saved_dve"], hf * 2 + c // 2 + 1)
                        for b in range(2):
                            last = pe.matmul(sums[c][:, b * BANK:(b + 1) * BANK], dt_w[:, d, c * P:(c + 1) * P],
                                             xdbl[:, d, b * BANK:(b + 1) * BANK], start=True, stop=True)
                        last.then_inc(s["dtproj_ready"], 1)
                    pe.wait_ge(s["diag_ready"], 2 * CH)
                    for c in range(CH):
                        pe.wait_ge(s["sp_relu"], dirs * CH + c + 1)
                        pe.wait_ge(s["sp_abs"], dirs * CH + c + 1)
                        if d == 0 and c == CH - 1:
                            pe.wait_ge(s["xc_ready"], direction(hf, 1) * CH + CH)
                            x_proj(1)
                            pe.wait_ge(s["xdbl_ready"], direction(hf, 1) * 2 + 2)
                        for b in range(2):
                            cut = slice(b * BANK, (b + 1) * BANK)
                            last = pe.matmul(sums[c][:, cut], d_diag[:, d, c, :], xc[d][c][:, cut],
                                             start=True, stop=False, skip_group_check=True)
                            if d:
                                y_fwd = xpad_mid[:, c, b * HB // 2:(b + 1) * HB // 2, :]
                                last = pe.matmul(sums[c][:, cut], ident[:, :], y_fwd, start=False, stop=False, skip_group_check=True)
                        if c >= 2:
                            last.then_inc(s["y_added"], 1)
                    with pe.Fori(0, NSTATE // 2) as j:
                        for k in range(2):
                            for c in range(CH):
                                pe.wait_ge(s["readout_ready"], dirs * (NSTATE * CH) + j * (2 * CH) + k * CH + c + 1)
                                for b in range(2):
                                    last = pe.matmul(sums[c][:, b * BANK:(b + 1) * BANK], ident[:, :],
                                                     readout[:, c % 2, b * BANK:(b + 1) * BANK], start=False, stop=False, skip_group_check=True)
                                last.then_inc(s["y_added"], 1)
                pe.wait_ge(s["gated_ready"], hf * CH + CH)
                for t in range(HTILES):
                    dst = sums[2 + t // 4][:, t % 4 * DM:(t % 4 + 1) * DM]
                    for c in range(CH):
                        last = pe.matmul(dst, gated[:, c, t * P:(t + 1) * P], out_w[:, c, :], start=c == 0, stop=c == CH - 1)
                    if t % 4 == 3:
                        last.then_inc(s["outproj_ready"], 1)

        @block.vector
        def _(dve):
            dve.memset(xdbl[XD:P, :, :], 0.0).then_inc(s["xdbl_zero"], 1)
            dve.wait_ge(s["cols_loaded"], 16)
            dve.wait_ge(s["ident_loaded"], 16)
            dve.wait_ge(s["a_exped"], 1)
            dve.tensor_scalar(a_neg[:, :, :], a_exp[:, :, :], -1.0, None, ALU.mult).then_inc(s["a_ready"], 1)
            for d in range(2):
                for c in range(CH):
                    dve.tensor_scalar(d_diag[:, d, c, :], ident[:, :], cols[:, d, C_D + c:C_D + c + 1], None,
                                      ALU.mult).then_inc(s["diag_ready"], 1)
            for hf in range(HALVES):
                dve.wait_ge(s[("x_first", "x_second")[hf]], 16)
                for t in range(hf * HTILES, (hf + 1) * HTILES):
                    dve.bn_stats(stats[:, t, :], x_sb[:, t, :]).then_inc(s["stats_done"], 1)
                dve.wait_ge(s["stats_done"], (hf + 1) * HTILES)
                for t in range(hf * HTILES, (hf + 1) * HTILES):
                    dve.bn_aggr(meanvar[:, t, :], stats[:, t, :]).then_inc(s["mean_ready"], 1)
            with dve.Fori(0, HALVES) as hf:
                dve.wait_ge(s["rstd_ready"], hf + 1)
                dve.memset(rider[:, :], 0.0)
                for t in range(HTILES):
                    tile = hf * HTILES + t
                    dve.tensor_scalar(normed[:, t, :], x_sb[:, bass.ds(tile, 1), :].rearrange("p a d -> p (a d)"),
                                      meanvar[:, bass.ds(tile, 1), 0], rstd[:, bass.ds(tile, 1)],
                                      ALU.subtract, ALU.mult).then_inc(s["norm_ready"], 1)
                dve.wait_ge(s["tr_ready"], hf * 2 + 1)
                dve.tensor_copy(norm_t[:, 0, :], sums[0]).then_inc(s["norm_t_ready"], 1)
                for d in range(2):
                    dirs = direction(hf, d)
                    for c in range(CH):
                        dve.wait_ge(s["conv_first"], dirs * CH + c + 1)
                        acc = by_batch(xc[d][c])
                        for k in range(1, TAPS):
                            at = PAD * 2 - k if d else k
                            if k > 1:
                                dve.wait_ge(s["conv_step"], dirs * (CH * 2) + c * 2 + k - 1)
                            w = cols[:, d, C_CONVW + TAPS * c + k:C_CONVW + TAPS * c + k + 1]
                            step = dve.scalar_tensor_tensor(out=acc, in0=xpad[:, c, :, at:at + SEQ], scalar=w, in1=acc,
                                                            op0=ALU.mult, op1=ALU.add)
                            step.then_inc(s["conv_sum_ready"] if k == TAPS - 1 else s["conv_step"], 1)
                for d in range(2):
                    dirs = direction(hf, d)
                    if d:
                        for c in range(1, CH, 2):
                            dve.wait_ge(s["y_added"], dirs * Y_ADDS - (CH - 1 - c))
                            dve.tensor_copy(xpad_mid[:, c, :, :], by_batch(sums[c])).then_inc(s["y_saved_dve"], 1)
                    for c in range(CH):
                        dve.wait_ge(s["sp_exp"], dirs * CH + c + 1)
                        dve.tensor_scalar(soft_w[c], du[:, c, :], 1.0, None, ALU.add).then_inc(s["sp_w"], 1)
                        dve.wait_ge(s["sp_w"], dirs * CH + c + 1)
                        dve.scalar_tensor_tensor(out=soft_w[c], in0=soft_w[c], scalar=1.0,
                                                 in1=du[:, c, :], op0=ALU.subtract, op1=ALU.subtract).then_inc(s["sp_corr"], 1)
                        if c % 2:
                            dve.wait_ge(s["sp_corr"], dirs * CH + c + 1)
                            dve.tensor_tensor(delta[:, c, :], delta[:, c, :], soft_w[c], ALU.subtract).then_inc(s["sp_diff_dve"], 1)
                    dve.wait_ge(s["sp_diff_pool"], dirs * (CH // 2) + CH // 2)
                    dve.wait_ge(s["sp_diff_dve"], dirs * (CH // 2) + CH // 2)
                    at = SEQ - 1 if d else 0
                    for k in range(2):
                        for b in range(0, HB, 2):
                            dve.memset(by_batch(decay[:, k, :])[:, b:b + 2, at:at + 1], 0.0).then_inc(s["strip_and_scan"], 1)
                    for c in range(CH):
                        dve.wait_ge(s["sp_diff_dve" if c % 2 else "sp_diff_pool"], dirs * (CH // 2) + c // 2 + 1)
                        dve.wait_ge(s["sp_ln"], dirs * CH + c + 1)
                        dve.tensor_tensor(delta[:, c, :], delta[:, c, :], soft_ln[c], ALU.add).then_inc(s["delta_ready"], 1)
                        if c:
                            dve.wait_ge(s["delta_ready"], dirs * CH + c + 1)
                            dve.tensor_tensor(du[:, c, :], delta[:, c, :], xc[d][c], ALU.mult).then_inc(s["du_dve"], 1)
                    with dve.Fori(0, NSTATE // 2) as j:
                        def scan(step):
                            nth = dirs * (NSTATE * CH) + j * (2 * CH) + step
                            slot, h = step % 2, h_of[step % CH]
                            dve.wait_ge(s["decay_ready"], nth + 1)
                            dve.wait_ge(s["inject_ready"], nth + 1)
                            way = slice(None, None, -1) if d else slice(None)
                            dve.tensor_tensor_scan(h[:, way], decay[:, slot, :][:, way], inject_of[step % CH][:, way],
                                                   0.0, ALU.mult, ALU.add).then_inc(s["strip_and_scan"], 1)

                        def read_out(step):
                            dve.wait_ge(s["strip_and_scan"], dirs * SCANS + j * (2 * CH) + step + 5)
                            dve.wait_ge(s["y_added"], dirs * Y_ADDS + j * (2 * CH) + step + 1)
                            if step % CH == 0:
                                dve.wait_ge(bc_loaded[1][step // CH], dirs * (8 * NSTATE) + j * 16 + 16)
                            dve.tensor_tensor(readout[:, step % 2, :], h_of[step % CH], bc[:, step // CH, 1, :],
                                              ALU.mult).then_inc(s["readout_ready"], 1)

                        scan(0)
                        for step in range(1, 2 * CH):
                            scan(step)
                            read_out(step - 1)
                        read_out(2 * CH - 1)
                for c in range(CH):
                    dve.wait_ge(s["y_added"], hf * (2 * Y_ADDS) + 2 * Y_ADDS - (CH - 1 - c))
                    dve.scalar_tensor_tensor(out=gated[:, c, :], in0=sums[c], scalar=0.5, in1=gate[:, c, :],
                                             op0=ALU.mult, op1=ALU.mult).then_inc(s["gated_ready"], 1)


SET = {"bias_columns": 2, "folded": 5, "scale": 11, "thresholds": 13, "signs": 15, "all": 18}
PAIRS = NBATCH // 2
PT_, PTOK = 2 * SEQ // P, 2 * SEQ
DC = 192
CK = (P, DC - P)
E0 = 256
NH, DK, LAT, ROPE = 8, 128, 32, 32
KEYW = LAT + ROPE + 1
DH = 64
FF, LR = 1024, 64
FLT_MAX = 3.4028234663852886e38
QUADS = 8

COLS = {}
for _name, _n in (("ln2_g", 2), ("ln2_b", 2), ("lnx_g", 2), ("lnx_b", 2), ("ln1_g", 2), ("ln1_b", 2), ("lnl_g", 2),
                  ("lnl_b", 2), ("bq", 2), ("bk", 2), ("qn", 1), ("kn", 1), ("bdq", 1), ("bkv", 1), ("b1", 8), ("buv", 8),
                  ("bv", 2)):
    COLS[_name] = (sum(n for _, n in COLS.values()), _n)
NLCOLS = sum(n for _, n in COLS.values())
ROWS = {"bo0": 0, "bo": DM, "bo1": 2 * DM, "b2": 3 * DM, "bdkv": 4 * DM}
NROWS = 4 * DM + LAT

WEIGHTS = (
    ("wq0", (P, 2, E0)), ("wk0", (P, 2, E0)), ("wv0", (P, 2, E0)), ("wo0", (P, 2, DM)),
    ("wf", (P, 2, DM)),
    ("w_dq", (P, 2, LAT)), ("w_kv", (P, 2, LAT + ROPE)),
    ("uq_t", (DK, NH, LAT + 1)), ("uk_t", (DK, NH, LAT + 1)),
    ("uv_t", (DK, NH, LAT)), ("w_o", (DK, NH, DM)),
    ("fold_q", (P, NH, KEYW)),
    ("wq1", (P, 2, DM)), ("wkv1", (P, 2, 2 * DM)), ("wlkv1", (P, 2, 2 * DM)), ("wo1", (P, 2, DM)),
    ("u1", (P, 2, LR)), ("v1w", (P, FF)), ("u2", (P, FF // P, LR)), ("v2w", (P, DM)),
    ("cols", (P, NLCOLS)), ("rows", (P, NROWS)), ("ctx", (P, PT_, DC)),
    ("q1_even", (P, 2, PTOK)),
)
REGION = max(sum(columns(shape) for _, shape in shapes) for shapes in (MAMBA_SHARED, WEIGHTS))

PER = {
    "c_loaded": 16, "c_stats": 4, "c_moments": 4, "c_var": 1, "c_rstd": 1, "c_normed": 4, "c_turned": 2, "c0_saved": 2, "c1_saved": 2,
    "k0_mm": 2, "k0_saved": 2, "v0_mm": 1, "v0_saved": 1, "k1c_mm": 1, "k1c_saved": 1, "c_sq": 1, "c_ss": 1, "c_ms": 1, "c_rms": 1,
    "k1c_normed": 1, "k1c_turned": 2, "k1c_placed": 2, "v1c_mm": 1, "v1c_saved": 1,
    "stats": 20, "moments": 20, "var": 10, "rstd": 10, "normed": 20, "turned": 10, "turned_act": 5, "turned_dve": 5,
    "q0_mm": 2, "q0_act": 1, "q0_dve": 1, "score0": 2, "max0": 2, "exp0": 4, "rinv0": 1, "p0_turned": 2, "p0_act": 1, "p0_dve": 1,
    "ctx0_mm": 2, "ctx0_act": 1, "ctx0_dve": 1, "out0_mm": 2, "x_biased": 4, "x_added": 12, "ffn0_mm": 2,
    "cq_mm": 2, "cq_saved": 1, "kk_saved": 1, "ckvn_mm": 1, "ckvn_saved": 1,
    "head_mm": 8, "head_saved": 8, "scored": 16, "masked": 8, "maxed": 16, "pexp": 48, "rinv": 16, "p_normed": 48,
    "p_turned": 16, "pt_dve": 16, "pt_act": 16, "pv_mm": 16, "o_act": 2, "o_dve": 2, "out1_mm": 4,
    "q1_mm": 1, "k1l_mm": 1, "v1l_mm": 1, "v1l_saved": 1, "sq": 2, "ss": 2, "ms": 2, "rms": 2, "q1_normed": 1, "k1l_normed": 1,
    "q1_turned": 2, "k1l_turned": 2, "q1_act": 2, "q1_dve": 2, "k1l_act": 1, "k1l_dve": 1,
    "p5_mm": 1, "p5_saved": 1, "h_mm": 8, "gelu": 8, "qt_mm": 1, "qt_saved": 1, "y_mm": 2,
}


def pexp_before(quad):
    return 4 * quad if quad <= QUADS else 4 * QUADS + 2 * (quad - QUADS)


def latent_quad(q):
    return q // 2, q % 2


def cross_quad(q):
    return q // 2 % 2, 2 * (q // 4) + q % 2


LOADS = 23


def load_layers(sp, dram, shared, mask_u8, s_in, s_ctx):
    w = carve(shared, WEIGHTS)

    def load(dst, src):
        sp.dma_start(dst, src).then_inc(s_in, 16)

    def two(m):
        return m.rearrange("(c p) n -> p c n", p=P)

    ctx_rows = dram["ctx"].rearrange("(t p) d -> p t d", p=P)
    sp.dma_start(w["ctx"][:, :, :], ctx_rows[:, 0:PT_, :]).then_inc(s_ctx, 16)
    load(w["cols"][:, :], dram["lcols"])
    load(w["wk0"][:, :, :], two(dram["wk0"]))
    load(w["wv0"][:, :, :], two(dram["wv0"]))
    load(w["wkv1"][:, :, :], two(dram["wkv1"]))
    load(w["rows"][:, :], dram["lrows"].partition_broadcast(P).rearrange("p a n -> p (a n)"))
    load(w["wf"][:, :, :], two(dram["wf"]))
    load(w["uq_t"][:, :, :], dram["uq_t"])
    load(w["uk_t"][:, :, :], dram["uk_t"])
    load(w["uv_t"][:, :, :], dram["uv_t"])
    load(w["w_o"][:, :, :], dram["w_o"].rearrange("(h p) n -> p h n", p=P))
    load(mask_u8[:, :, :], dram["mask"].partition_broadcast(P).rearrange("p a (b k) -> p (a b) k", k=SEQ))
    load(w["fold_q"][:, :, :], dram["fold_r"])
    load(w["wq0"][:, :, :], two(dram["wq0"]))
    load(w["wo0"][:, :, :], two(dram["wo0"]))
    load(w["w_dq"][:, :, :], two(dram["w_dq"]))
    load(w["w_kv"][:, :, :], two(dram["w_kv"]))
    load(w["wq1"][:, :, :], two(dram["wq1"]))
    load(w["wlkv1"][:, :, :], two(dram["wlkv1"]))
    load(w["wo1"][:, :, :], two(dram["wo1"]))
    load(w["u1"][:, :, :], two(dram["u1"]))
    load(w["v1w"][:, :], dram["v1w"])
    load(w["u2"][:, :, :], two(dram["u2"]))
    load(w["v2w"][:, :], dram["v2w"])


def layers_block(nc, dram, x_sb, ident, shared, mask_u8, s_in, s_ctx):
    with ExitStack() as ctx:
        def sb(name, shape, dt=F32):
            return ctx.enter_context(nc.sbuf_tensor(name, shape, dt))

        s = {n: ctx.enter_context(nc.semaphore(n)) for n in PER if n != "c_loaded"}
        s["c_loaded"] = s_ctx
        s_out = ctx.enter_context(nc.semaphore("out_stored"))
        s_const = ctx.enter_context(nc.semaphore("pool_consts"))
        s_zero = ctx.enter_context(nc.semaphore("zero_rows_set"))
        s_set = ctx.enter_context(nc.semaphore("setup_dve"))
        s_abs = ctx.enter_context(nc.semaphore("ternary_abs"))
        s_fold = ctx.enter_context(nc.semaphore("folds_mm"))

        w = carve(shared, WEIGHTS)
        wq0, wk0, wv0, wo0, wf, w_dq, w_kv, uq_t, uk_t, uv_t, w_o, fold_q = (
            w[n] for n in "wq0 wk0 wv0 wo0 wf w_dq w_kv uq_t uk_t uv_t w_o fold_q".split())
        wq1, wkv1, wlkv1, wo1, u1, v1w, u2, v2w, cols, rows, ctx_sb = (
            w[n] for n in "wq1 wkv1 wlkv1 wo1 u1 v1w u2 v2w cols rows ctx".split())
        fold_v = sb("fold_v", [P, 2, DM])
        mask = sb("mask_bias", [P, NBATCH, SEQ])
        ones = sb("ones", [P, P])
        h_sb = sb("h_sb", [P, FF // P, PTOK])
        spare = h_sb[:, :, :].rearrange("p m n -> p (m n)")
        tern = spare[:, 0:6 * DM].rearrange("p (k n) -> p k n", k=3)
        buv_rep = spare[:, 6 * DM:6 * DM + NH * P].rearrange("p (h n) -> p h n", h=NH)
        sq = spare[:, 0:2 * PT_ * DM].rearrange("p (k n) -> p k n", k=2)
        qk_n = spare[:, 2 * PT_ * DM:4 * PT_ * DM].rearrange("p (k t n) -> p k t n", k=2, t=PT_)
        scales = sb("scales", [P, 8])
        bqs = sb("bqs", [P, 2])
        gamma = sb("gamma", [P, 1])
        bv_rep = spare[:, 6 * DM + NH * P:6 * DM + NH * P + 2 * P].rearrange("p (c n) -> p c n", c=2)
        c_stats = sb("c_stats_sb", [P, PT_, 6])
        c_moments = sb("c_moments_sb", [P, PT_, 2])
        c_var = sb("c_var_sb", [P, PT_])
        c_rstd = sb("c_rstd_sb", [P, PT_])
        c_nrm = sb("c_nrm", [P, PT_, DC])
        c0_t = sb("c0_t", [P, 2, PTOK])
        c1_t = sb("c1_t", [P, 2, PTOK])
        k0_t = sb("k0_t", [P, 2, PTOK])
        v0 = sb("v0", [P, PT_, E0])
        k1c = sb("k1c", [P, PT_, DM])
        c_sq = sb("c_sq_sb", [P, PT_ * DM])
        c_ss = sb("c_ss_sb", [P, 4 * PT_])
        c_ms = sb("c_ms_sb", [P, 4 * PT_])
        c_rms = sb("c_rms_sb", [P, 4 * PT_])
        stats = sb("lstats", [P, 2, PT_, 6])
        moments = sb("lmoments", [P, 2, PT_, 2])
        var = sb("lvar", [P, 2, PT_])
        rider = sb("lrider", [P, 2])
        prider = sb("prider", [P, 1])
        half_c = sb("half_c", [P, 4 * PT_])
        rstd = sb("lrstd", [P, 2, PT_])
        nrm = sb("nrm", [P, 2, PT_, DM])
        x_t = sb("x_t", [P, 2, PTOK])
        q0_t = sb("q0_t", [P, 2, PTOK])
        o_t = sb("o_t", [P, 2, PTOK])
        k1_t = sb("k1_t", [P, 2, 2, 2 * SEQ])
        q1_z = [w["q1_even"], sb("q1_odd", [P, 2, PTOK])]
        v1 = sb("v1", [P, 2, 4, DM])
        ss = sb("ss", [P, 2, 4 * PT_])
        ms = sb("ms", [P, 2, 4 * PT_])
        rms = sb("rms_sb", [P, 2, 4 * PT_])
        negm = sb("negm", [P, 2, 4])
        rsum = sb("rsum", [P, 2, 4])
        rinv = sb("rinv_sb", [P, 2, 4])
        pe_ = sb("pexp_sb", [P, 2, 1024])
        p_t = sb("p_t", [P, 2, 1024])
        cq = sb("cq", [P, PTOK])
        kk = sb("kk", [P, PTOK])
        ckvn = sb("ckvn", [P, PT_, LAT])
        qh = sb("qh", [P, 4, PTOK])
        p5_t = sb("p5_t", [P, PTOK])
        qt5 = sb("qt5", [P, PTOK])
        ZERO_ROWS = [cq[LAT:2 * LAT, :], cq[2 * LAT:P, :], kk[LAT + ROPE:P, :], qh[LAT + ROPE:P, :, :], p5_t[LR:P, :], qt5[LR:P, :],
                     c0_t[CK[1]:P, 1, :], c1_t[CK[1]:P, 1, :], q1_z[0][DH:P, :, :], q1_z[1][0:DH, :, :]]

        D = [ctx.enter_context(nc.psum_tensor(f"D{i}", [P, 1024], F32)) for i in range(4)]
        TB = D[2]
        OB = [D[3][:, BANK:2 * BANK], D[3][:, 0:BANK]]

        def head_bank(n):
            return OB[0] if n < 4 and n % 2 else OB[1]

        def col(name, c=0, n=P):
            at = COLS[name][0] + c
            return cols[0:n, at:at + 1]

        def row(name, n=DM):
            return rows[:, ROWS[name]:ROWS[name] + n]

        sc_attn0 = float(E0) ** -0.5
        sc_mla = 1.0 / float(DK + ROPE) ** 0.5
        sc_attn1 = float(DH) ** -0.5
        loaded = 16 * LOADS
        block = ctx.enter_context(nc.Block())

        @block.sync
        def _(sp):
            ctx_rows = dram["ctx"].rearrange("(t p) d -> p t d", p=P)
            out_rows = dram["out"].rearrange("(t p) d -> p t d", p=P)

            def store(it):
                sp.wait_ge(s["x_added"], it * PER["x_added"] + PER["x_added"])
                sp.dma_start(out_rows[:, bass.ds(it * PT_, PT_), :], x_sb[:, bass.ds(it * PT_, PT_), :]).then_inc(s_out, 16)

            with sp.Fori(0, PAIRS - 1) as it:
                sp.wait_ge(s["c_normed"], it * PER["c_normed"] + PT_)
                sp.dma_start(ctx_sb[:, :, :], ctx_rows[:, bass.ds(it * PT_ + PT_, PT_), :]).then_inc(s["c_loaded"], 16)
                store(it)
            store(PAIRS - 1)
            sp.wait_ge(s_out, 16 * PAIRS)

        @block.gpsimd
        def _(pool):
            pool.memset(half_c[:, :], -0.5).then_inc(s_const, 1)
            pool.memset(ones[:, :], 1.0).then_inc(s_const, 1)
            pool.memset(prider[:, :], 0.0).then_inc(s_const, 1)
            pool.wait_ge(s_const, 3)

            def context_norm(j):
                pool.wait_ge(s["c_var"], j * PER["c_var"] + 1)
                pool.tensor_tensor(c_rstd[:, :], c_var[:, :], half_c[:, 0:PT_], ALU.pow).then_inc(s["c_rstd"], 1)

            def context_keys(j):
                pool.wait_ge(s["c_ms"], j * PER["c_ms"] + 1)
                pool.tensor_tensor(c_rms[:, :], c_ms[:, :], half_c[:, :], ALU.pow).then_inc(s["c_rms"], 1)
                pool.wait_ge(s["c_rms"], j * PER["c_rms"] + 1)
                pool.wait_ge(s["k1c_saved"], j * PER["k1c_saved"] + 1)
                k = k1c[:, :, :].rearrange("p t (h d) -> p (t h) d", d=DH)
                pool.tensor_tensor(k, k, c_rms[:, :].unsqueeze(2).broadcast_to([P, 4 * PT_, DH]), ALU.mult).then_inc(s["k1c_normed"], 1)

            def pair(it, more):
                def after(name, k):
                    pool.wait_ge(s[name], it * PER[name] + k)

                def inverse_root(n):
                    for half in range(2):
                        after("var", 2 * n + half + 1)
                        t = slice(2 * half, 2 * half + 2)
                        pool.tensor_tensor(rstd[:, n % 2, t], var[:, n % 2, t], half_c[:, 0:2], ALU.pow).then_inc(s["rstd"], 1)

                def rms_root(k):
                    after("ms", k + 1)
                    pool.tensor_tensor(rms[:, k, :], ms[:, k, :], half_c[:, :], ALU.pow).then_inc(s["rms"], 1)

                def add_bias(n, bias):
                    after("normed", 4 * n + 4)
                    pool.tensor_tensor(prider[:, :], prider[:, :], prider[:, :], ALU.mult)
                    xr = x_sb[:, bass.ds(it * PT_, PT_), :]
                    pool.tensor_tensor(xr, xr, bias.unsqueeze(1).broadcast_to([P, PT_, DM]), ALU.add).then_inc(s["x_biased"], 1)

                inverse_root(0)
                add_bias(0, row("bo0"))
                if more:
                    context_norm(it + 1)
                inverse_root(1)
                inverse_root(2)
                add_bias(2, row("bo"))
                inverse_root(3)
                rms_root(0)
                rms_root(1)
                add_bias(3, row("bo1"))
                if more:
                    context_keys(it + 1)
                inverse_root(4)
                add_bias(4, row("b2"))

            context_norm(0)
            pool.wait_ge(s["c_rstd"], 1)
            for n, zeros in enumerate(ZERO_ROWS):
                pool.memset(zeros, 0.0).then_inc(s_zero, 1)
                pool.wait_ge(s_zero, n + 1)
            context_keys(0)
            with pool.Fori(0, PAIRS - 1) as it:
                pair(it, True)
            pair(PAIRS - 1, False)

        @block.scalar
        def _(act):
            act.wait_ge(s_in, loaded)
            act.activation(tern[:, 0, :], wf[:, :, :].rearrange("p c n -> p (c n)"), ACT.Abs,
                           accum_out=scales[:, 0:1]).then_inc(s_abs, 1)
            def context_turned(j):
                for dst, g, b, name in ((c0_t, "ln2_g", "ln2_b", "c0_saved"), (c1_t, "lnx_g", "lnx_b", "c1_saved")):
                    for c in range(2):
                        act.wait_ge(s["c_turned"], j * PER["c_turned"] + c + 1)
                        act.activation(dst[0:CK[c], c, :], D[0][0:CK[c], c * BANK:(c + 1) * BANK], ACT.Identity,
                                       scale=col(g, c, CK[c]), bias=col(b, c, CK[c])).then_inc(s[name], 1)

            def context_k0(j):
                for e in range(2):
                    act.wait_ge(s["k0_mm"], j * PER["k0_mm"] + e + 1)
                    act.activation(k0_t[:, e, :], D[1][:, e * BANK:(e + 1) * BANK], ACT.Identity, bias=col("bk", e)).then_inc(s["k0_saved"], 1)

            def context_v0(j):
                act.wait_ge(s["v0_mm"], j * PER["v0_mm"] + 1)
                act.activation(v0[:, :, :].rearrange("p t d -> p (t d)"), D[3][:, :], ACT.Copy).then_inc(s["v0_saved"], 1)

            def context_k1(j):
                act.wait_ge(s["k1c_mm"], j * PER["k1c_mm"] + 1)
                act.activation(k1c[:, :, :].rearrange("p t d -> p (t d)"), D[1][:, :], ACT.Copy).then_inc(s["k1c_saved"], 1)
                act.activation(c_sq[:, :], D[1][:, :], ACT.Square).then_inc(s["c_sq"], 1)

            def context_k1_turned(j):
                for c in range(2):
                    act.wait_ge(s["k1c_turned"], j * PER["k1c_turned"] + c + 1)
                    act.activation(k1_t[:, c, :, 0:SEQ], D[1][:, c * BANK:(c + 1) * BANK].rearrange("p (b k) -> p b k", b=2),
                                   ACT.Copy).then_inc(s["k1c_placed"], 1)

            def context_v1(j):
                act.wait_ge(s["v1c_mm"], j * PER["v1c_mm"] + 1)
                act.activation(v1[:, :, 0:2, :], D[3][:, :].rearrange("p (b k n) -> p b k n", b=2, k=2), ACT.Copy).then_inc(s["v1c_saved"], 1)

            def pair(it, more):
                def after(name, k):
                    act.wait_ge(s[name], it * PER[name] + k)

                def turned(n, g=None, b=None):
                    after("turned", 2 * n + 1)
                    if g is None:
                        act.activation(x_t[:, 0, :], TB[:, 0:BANK], ACT.Copy).then_inc(s["turned_act"], 1)
                    else:
                        act.activation(x_t[:, 0, :], TB[:, 0:BANK], ACT.Identity, scale=col(g), bias=col(b)).then_inc(s["turned_act"], 1)

                def exps(quad, sp, n, keys):
                    after("maxed", quad + 1)
                    if quad >= 2:
                        after("p_turned", quad - 1)
                    for r in range(n):
                        act.activation(pe_[:, quad % 2, r * keys:(r + 1) * keys], sp[:, r * keys:(r + 1) * keys], ACT.Exp,
                                       bias=negm[:, quad % 2, r:r + 1], accum_out=rsum[:, quad % 2, r:r + 1]).then_inc(s["pexp"], 1)

                turned(0, "ln1_g", "ln1_b")
                after("q0_mm", 1)
                act.activation(q0_t[:, 0, :], D[3][:, 0:BANK], ACT.Identity, scale=sc_attn0, bias=bqs[:, 0:1]).then_inc(s["q0_act"], 1)
                for r in range(4):
                    after("max0", r // 2 + 1)
                    act.activation(pe_[:, 0, r * SEQ:(r + 1) * SEQ], D[0][:, r * SEQ:(r + 1) * SEQ], ACT.Exp,
                                   bias=negm[:, 0, r:r + 1], accum_out=rsum[:, 0, r:r + 1]).then_inc(s["exp0"], 1)
                after("p0_turned", 1)
                act.activation(p_t[:, 0, 0:BANK], TB[:, 0:BANK], ACT.Copy).then_inc(s["p0_act"], 1)
                after("ctx0_mm", 1)
                act.activation(o_t[:, 0, :], D[1][:, 0:BANK], ACT.Copy).then_inc(s["ctx0_act"], 1)
                if more:
                    context_turned(it + 1)
                    context_k0(it + 1)
                turned(1)
                turned(2)
                if more:
                    context_v0(it + 1)
                after("cq_mm", 1)
                act.activation(cq[0:LAT, :], D[1][0:LAT, 0:BANK], ACT.Identity, bias=col("bdq", 0, LAT)).then_inc(s["cq_saved"], 1)

                def head_saved(n):
                    after("head_mm", n + 1)
                    act.activation(qh[0:KEYW, n % 4, :], head_bank(n)[0:KEYW, :], ACT.Copy, scale=sc_mla).then_inc(s["head_saved"], 1)

                def quad_turned(quad):
                    after("p_turned", quad + 1)
                    if quad >= 2:
                        after("pv_mm", quad - 1)
                    act.activation(p_t[:, quad % 2, 0:BANK], TB[:, 0:BANK], ACT.Copy).then_inc(s["pt_act"], 1)

                def o_saved(k):
                    after("pv_mm", k * QUADS + QUADS // 2)
                    act.activation(o_t[:, 0, :], OB[0], ACT.Copy).then_inc(s["o_act"], 1)

                for n in range(4):
                    head_saved(n)
                exps(0, D[0], 4, SEQ)
                exps(1, D[1], 4, SEQ)
                for q in range(QUADS):
                    if q + 4 < NH:
                        head_saved(q + 4)
                    quad_turned(q)
                    if q + 2 < QUADS:
                        exps(q + 2, D[q % 2], 4, SEQ)
                    if q == QUADS // 2 + 1:
                        o_saved(0)
                turned(3, "lnl_g", "lnl_b")
                if more:
                    context_k1(it + 1)
                after("q1_mm", 1)
                act.activation(sq[:, 0, :], D[0][:, :], ACT.Square).then_inc(s["sq"], 1)
                after("k1l_mm", 1)
                act.activation(sq[:, 1, :], D[1][:, :], ACT.Square).then_inc(s["sq"], 1)
                after("v1l_mm", 1)
                act.activation(v1[:, :, 2:4, :], D[3][:, :].rearrange("p (b k n) -> p b k n", b=2, k=2), ACT.Copy).then_inc(s["v1l_saved"], 1)
                after("q1_turned", 1)
                for odd in range(2):
                    lo = odd * DH
                    act.activation(q1_z[odd][lo:lo + DH, 0, :], TB[lo:lo + DH, 0:BANK], ACT.Copy,
                                   scale=gamma[lo:lo + DH, 0:1]).then_inc(s["q1_act"], 1)
                after("k1l_turned", 1)
                act.activation(k1_t[:, 0, :, SEQ:2 * SEQ], D[3][:, 0:BANK].rearrange("p (b k) -> p b k", b=2), ACT.Copy).then_inc(s["k1l_act"], 1)
                exps(QUADS, D[0], 2, 2 * SEQ)
                exps(QUADS + 1, D[1], 2, 2 * SEQ)
                for q in range(QUADS):
                    quad_turned(QUADS + q)
                    if q + 2 < QUADS:
                        exps(QUADS + q + 2, D[q % 2], 2, 2 * SEQ)
                    if q == QUADS // 2 + 1:
                        o_saved(1)
                if more:
                    context_k1_turned(it + 1)
                act.preload_act_table(ACT.Gelu_apprx_tanh)
                turned(4)
                after("p5_mm", 1)
                act.activation(p5_t[0:LR, :], D[1][0:LR, 0:BANK], ACT.Copy).then_inc(s["p5_saved"], 1)
                for m in range(FF // P):
                    after("h_mm", m + 1)
                    act.activation(h_sb[:, m, :], [D[0], D[3]][m % 4 // 2][:, m % 2 * BANK:(m % 2 + 1) * BANK],
                                   ACT.Gelu_apprx_tanh, bias=col("b1", m)).then_inc(s["gelu"], 1)
                after("qt_mm", 1)
                act.activation(qt5[0:LR, :], D[1][0:LR, BANK:2 * BANK], ACT.Copy).then_inc(s["qt_saved"], 1)
                act.preload_act_table(ACT.Exp)
                if more:
                    context_v1(it + 1)

            context_turned(0)
            context_k0(0)
            context_v0(0)
            context_k1(0)
            context_v1(0)
            context_k1_turned(0)
            act.wait_ge(s_set, SET["all"])
            with act.Fori(0, PAIRS - 1) as it:
                pair(it, True)
            pair(PAIRS - 1, False)

        @block.tensor
        def _(pe):
            pe.wait_ge(s_in, loaded)
            for h in range(NH):
                at = BANK + h * (LAT + 1)
                pe.matmul(D[3][0:LAT + 1, at:at + LAT + 1], uq_t[:, h, :], uk_t[:, h, :], start=True, stop=True)
            for h in range(NH):
                at = h % 4 * LAT
                last = pe.matmul(D[1][at:at + LAT, h // 4 * DM:(h // 4 + 1) * DM], uv_t[:, h, :], w_o[:, h, :], start=True, stop=True)
            last.then_inc(s_fold, 1)
            def wait(name, j, k):
                pe.wait_ge(s[name], j * PER[name] + k)

            def rows_times(dst, src_t, w, name, lo=0, n=DM, by_bank=False):
                for t in range(PT_):
                    for c in range(2):
                        last = pe.matmul(dst[:, t * n:(t + 1) * n], src_t[:, c, t * P:(t + 1) * P],
                                         w[:, c, lo:lo + n], start=c == 0, stop=c == 1)
                    if t == PT_ - 1 or (by_bank and t == 1):
                        last.then_inc(s[name], 1)

            def cols_times(dst, w, src_t, name):
                for e in range(2):
                    for c in range(2):
                        last = pe.matmul(dst[:, e * BANK:(e + 1) * BANK], w[:, c, e * P:(e + 1) * P],
                                         src_t[:, c, :], start=c == 0, stop=c == 1)
                    last.then_inc(s[name], 1)

            def turn_rows(dst, src, name, width=DM):
                for c in range(2):
                    w = min(P, width - c * P)
                    for t in range(PT_):
                        last = pe.transpose(dst[0:w, c * BANK + t * P:c * BANK + (t + 1) * P], src[:, t, c * P:c * P + w], ident[:, :])
                    last.then_inc(s[name], 1)

            def context_turn(j):
                wait("c_normed", j, PT_)
                turn_rows(D[0], c_nrm, "c_turned", DC)

            def context_k0(j):
                wait("c0_saved", j, 2)
                cols_times(D[1], wk0, c0_t, "k0_mm")

            def context_v0(j):
                rows_times(D[3], c0_t, wv0, "v0_mm")

            def context_k1(j):
                wait("k0_saved", j, 2)
                wait("c1_saved", j, 2)
                rows_times(D[1], c1_t, wkv1, "k1c_mm")

            def context_k1_turn(j):
                wait("c_sq", j, 1)
                wait("k1c_normed", j, 1)
                turn_rows(D[1], k1c, "k1c_turned")

            def context_v1(j):
                wait("v0_saved", j, 1)
                rows_times(D[3], c1_t, wkv1, "v1c_mm", lo=DM)

            def pair(it, more):
                def after(name, k):
                    wait(name, it, k)

                def turn(n):
                    for t in range(PT_):
                        after("normed", 4 * n + t + 1)
                        for c in range(2):
                            last = pe.transpose(TB[:, c * BANK + t * P:c * BANK + (t + 1) * P], nrm[:, n % 2, t, c * P:(c + 1) * P], ident[:, :])
                            if t == PT_ - 1:
                                last.then_inc(s["turned"], 1)

                def turned(n):
                    after("turned_act", n + 1)
                    after("turned_dve", n + 1)

                turn(0)
                turned(0)
                after("v1c_saved", 1)
                cols_times(D[3], wq0, x_t, "q0_mm")
                after("k0_saved", 2)
                after("c1_saved", 2)
                after("q0_act", 1)
                after("q0_dve", 1)
                for b in range(2):
                    for c in range(2):
                        at = (b * 2 + c) * SEQ
                        for e in range(2):
                            last = pe.matmul(D[0][:, at:at + SEQ], q0_t[:, e, b * SEQ + c * P:b * SEQ + (c + 1) * P],
                                             k0_t[:, e, b * SEQ:(b + 1) * SEQ], start=e == 0, stop=e == 1)
                    last.then_inc(s["score0"], 1)
                for b in range(2):
                    after("exp0", 2 * b + 2)
                    for kc in range(2):
                        for c in range(2):
                            at = (b * 2 + kc) * SEQ + c * P
                            src = (b * 2 + c) * SEQ + kc * P
                            last = pe.transpose(TB[:, at:at + P], pe_[:, 0, src:src + P], ident[:, :])
                    last.then_inc(s["p0_turned"], 1)
                after("k1c_placed", 2)
                after("p0_act", 1)
                after("p0_dve", 1)
                for e in range(2):
                    for b in range(2):
                        for kc in range(2):
                            last = pe.matmul(D[1][:, e * BANK + b * SEQ:e * BANK + (b + 1) * SEQ], v0[:, b * 2 + kc, e * P:(e + 1) * P],
                                             p_t[:, 0, (b * 2 + kc) * SEQ:(b * 2 + kc + 1) * SEQ], start=kc == 0, stop=kc == 1)
                    last.then_inc(s["ctx0_mm"], 1)
                after("ctx0_act", 1)
                after("ctx0_dve", 1)
                rows_times(D[3], o_t, wo0, "out0_mm", by_bank=True)
                if more:
                    context_turn(it + 1)
                    context_k0(it + 1)
                turn(1)
                turned(1)
                if more:
                    wait("c1_saved", it + 1, 2)
                rows_times(D[0], x_t, wf, "ffn0_mm", by_bank=True)
                if more:
                    context_v0(it + 1)
                turn(2)
                turned(2)
                if more:
                    wait("k0_saved", it + 1, 2)
                for c in range(2):
                    last = pe.matmul(D[1][0:LAT, 0:BANK], w_dq[:, c, :], x_t[:, c, :], start=c == 0, stop=c == 1)
                last.then_inc(s["cq_mm"], 1)
                for c in range(2):
                    last = pe.matmul(D[1][0:LAT + ROPE, BANK:2 * BANK], w_kv[:, c, :], x_t[:, c, :], start=c == 0, stop=c == 1)
                last.then_inc(s["cq_mm"], 1)
                rows_times(D[0], x_t, w_kv, "ckvn_mm", n=LAT)
                after("cq_saved", 1)
                if more:
                    wait("v0_saved", it + 1, 1)

                def head(n):
                    if n >= 2:
                        after("head_saved", n if n >= 4 else n - 1)
                    pe.matmul(head_bank(n)[0:KEYW, :], fold_q[:, n, :], cq[:, :], start=True, stop=True).then_inc(s["head_mm"], 1)

                def score(q):
                    hp, b = latent_quad(q)
                    if q >= 2:
                        after("pexp", pexp_before(q - 1))
                    after("head_saved", 2 * hp + 2)
                    for c in range(2):
                        for hh in range(2):
                            at = (c * 2 + hh) * SEQ
                            last = pe.matmul(D[q % 2][:, at:at + SEQ], qh[:, (2 * hp + hh) % 4, b * SEQ + c * P:b * SEQ + (c + 1) * P],
                                             kk[:, b * SEQ:(b + 1) * SEQ], start=True, stop=True)
                    last.then_inc(s["scored"], 1)

                def turn_p(quad, n, keys):
                    after("p_normed", pexp_before(quad + 1))
                    if quad:
                        after("pt_dve", quad)
                        after("pt_act", quad)
                    for r in range(n):
                        c, hh = r // (n // 2), r % (n // 2)
                        for kc in range(keys // P):
                            at = (hh * (keys // P) + kc) * SEQ + c * P
                            last = pe.transpose(TB[:, at:at + P], pe_[:, quad % 2, r * keys + kc * P:r * keys + (kc + 1) * P], ident[:, :])
                    last.then_inc(s["p_turned"], 1)

                def values(q):
                    hp, b = latent_quad(q)
                    after("pt_dve", q + 1)
                    after("pt_act", q + 1)
                    for hh in range(2):
                        h = 2 * hp + hh
                        at = h % 4 * LAT
                        for kc in range(2):
                            last = pe.matmul(OB[h // 4][at:at + LAT, b * SEQ:(b + 1) * SEQ], ckvn[:, b * 2 + kc, :],
                                             p_t[:, q % 2, (hh * 2 + kc) * SEQ:(hh * 2 + kc + 1) * SEQ], start=kc == 0, stop=kc == 1)
                    last.then_inc(s["pv_mm"], 1)

                for n in range(4):
                    head(n)
                after("kk_saved", 1)
                after("ckvn_saved", 1)
                score(0)
                score(1)
                for q in range(QUADS):
                    if q + 4 < NH:
                        head(q + 4)
                    if q + 2 < QUADS:
                        score(q + 2)
                    if q >= 2:
                        if q - 2 == QUADS // 2:
                            after("head_saved", NH)
                        values(q - 2)
                    turn_p(q, 4, SEQ)
                values(QUADS - 2)
                values(QUADS - 1)
                after("o_act", 1)
                after("o_dve", 1)
                rows_times(D[0], o_t, fold_v, "out1_mm", by_bank=True)
                if more:
                    context_k1(it + 1)
                turn(3)
                turned(3)
                after("x_added", 8)
                rows_times(D[0], x_t, wq1, "q1_mm")
                if more:
                    wait("c_sq", it + 1, 1)
                rows_times(D[1], x_t, wlkv1, "k1l_mm")
                rows_times(D[3], x_t, wlkv1, "v1l_mm", lo=DM)
                after("q1_normed", 1)
                turn_rows(TB, qk_n[:, 0, :, :], "q1_turned")
                after("v1l_saved", 1)
                after("k1l_normed", 1)
                turn_rows(D[3], qk_n[:, 1, :, :], "k1l_turned")

                def score1(q):
                    b, h = cross_quad(q)
                    if q >= 2:
                        after("pexp", pexp_before(QUADS + q - 1))
                    for c in range(2):
                        last = pe.matmul(D[q % 2][:, c * BANK:(c + 1) * BANK],
                                         q1_z[h % 2][:, h // 2, b * SEQ + c * P:b * SEQ + (c + 1) * P],
                                         k1_t[:, h // 2, b, :], start=True, stop=True)
                    last.then_inc(s["scored"], 1)

                def values1(q):
                    b, h = cross_quad(q)
                    after("pt_dve", QUADS + q + 1)
                    after("pt_act", QUADS + q + 1)
                    at = h % 2 * DH
                    for kc in range(4):
                        last = pe.matmul(OB[h // 2][at:at + DH, b * SEQ:(b + 1) * SEQ], v1[:, b, kc, h * DH:(h + 1) * DH],
                                         p_t[:, q % 2, kc * SEQ:(kc + 1) * SEQ], start=kc == 0, stop=kc == 3)
                    last.then_inc(s["pv_mm"], 1)

                for name in ("q1_act", "q1_dve", "k1l_act", "k1l_dve"):
                    after(name, PER[name])
                score1(0)
                score1(1)
                for q in range(QUADS):
                    if q + 2 < QUADS:
                        score1(q + 2)
                    if q >= 2:
                        values1(q - 2)
                    turn_p(QUADS + q, 2, 2 * SEQ)
                values1(QUADS - 2)
                values1(QUADS - 1)
                after("o_act", 2)
                after("o_dve", 2)
                rows_times(D[0], o_t, wo1, "out1_mm", by_bank=True)
                if more:
                    context_k1_turn(it + 1)
                turn(4)
                turned(4)
                if more:
                    wait("k1c_placed", it + 1, 2)
                for c in range(2):
                    last = pe.matmul(D[1][0:LR, 0:BANK], u1[:, c, :], x_t[:, c, :], start=c == 0, stop=c == 1)
                last.then_inc(s["p5_mm"], 1)
                after("p5_saved", 1)
                for m in range(FF // P + 2):
                    if m < FF // P:
                        if m >= 4:
                            after("gelu", m - 3)
                        pe.matmul([D[0], D[3]][m % 4 // 2][:, m % 2 * BANK:(m % 2 + 1) * BANK], v1w[:, m * P:(m + 1) * P],
                                  p5_t[:, :], start=True, stop=True).then_inc(s["h_mm"], 1)
                    if m >= 2:
                        after("gelu", m - 1)
                        last = pe.matmul(D[1][0:LR, BANK:2 * BANK], u2[:, m - 2, :], h_sb[:, m - 2, :], start=m == 2, stop=m == FF // P + 1)
                last.then_inc(s["qt_mm"], 1)
                after("qt_saved", 1)
                for t in range(PT_):
                    last = pe.matmul(TB[:, t * DM:(t + 1) * DM], qt5[:, t * P:(t + 1) * P], v2w[:, :], start=True, stop=True)
                    if t % 2:
                        last.then_inc(s["y_mm"], 1)
                if more:
                    context_v1(it + 1)

            context_turn(0)
            pe.wait_ge(s_set, SET["bias_columns"])
            for h in range(NH):
                pe.matmul(D[2][:, 0:DM], buv_rep[:, h, :], w_o[:, h, :], start=h == 0, stop=h == NH - 1)
            for c in range(2):
                pe.matmul(D[2][:, BANK:BANK + DM], bv_rep[:, c, :], wo0[:, c, :], start=c == 0, stop=c == 1)
            pe.wait_ge(s_abs, 1)
            pe.matmul(D[3][:, 0:1], ones[:, :], scales[:, 0:1], start=True, stop=True).then_inc(s_fold, 1)
            pe.wait_ge(s_set, SET["folded"])
            pe.wait_ge(s_zero, len(ZERO_ROWS))
            context_k0(0)
            pe.wait_ge(s_set, SET["scale"])
            context_v0(0)
            context_k1(0)
            context_v1(0)
            context_k1_turn(0)
            pe.wait_ge(s_set, SET["all"])
            with pe.Fori(0, PAIRS - 1) as it:
                pair(it, True)
            pair(PAIRS - 1, False)

        @block.vector
        def _(dve):
            def context_norm(j):
                def after(name, k):
                    dve.wait_ge(s[name], j * PER[name] + k)

                after("c_loaded", 16)
                for t in range(PT_):
                    dve.bn_stats(c_stats[:, t, :], ctx_sb[:, t, :]).then_inc(s["c_stats"], 1)
                after("c_stats", 4)
                dve.memset(rider[:, 0:1], 0.0)
                for t in range(PT_):
                    dve.bn_aggr(c_moments[:, t, :], c_stats[:, t, :]).then_inc(s["c_moments"], 1)
                after("c_moments", 4)
                dve.tensor_scalar(c_var[:, :], c_moments[:, :, 1], EPS, None, ALU.add).then_inc(s["c_var"], 1)

            def context_scale(j):
                dve.wait_ge(s["c_rstd"], j * PER["c_rstd"] + 1)
                for t in range(PT_):
                    dve.tensor_scalar(c_nrm[:, t, :], ctx_sb[:, t, :], c_moments[:, t, 0:1], c_rstd[:, t:t + 1],
                                      ALU.subtract, ALU.mult).then_inc(s["c_normed"], 1)

            def context_squares(j):
                dve.wait_ge(s["c_sq"], j * PER["c_sq"] + 1)
                dve.tensor_reduce(c_ss[:, :], c_sq[:, :].rearrange("p (a d) -> p a d", d=DH), AX_X, ALU.add).then_inc(s["c_ss"], 1)
                dve.wait_ge(s["c_ss"], j * PER["c_ss"] + 1)
                dve.tensor_scalar(c_ms[:, :], c_ss[:, :], 1.0 / DH, 1e-16, ALU.mult, ALU.max).then_inc(s["c_ms"], 1)

            def pair(it, more):
                def after(name, k):
                    dve.wait_ge(s[name], it * PER[name] + k)

                def tile_of(t, n=1):
                    return x_sb[:, bass.ds(it * PT_ + t, n), :]

                def statistics(n, t):
                    dve.bn_stats(stats[:, n % 2, t, :], tile_of(t).rearrange("p a d -> p (a d)")).then_inc(s["stats"], 1)

                def variances(n, half):
                    twice = n in (0, 3)
                    after("stats", 4 * n + 2 * half + 2)
                    dve.memset(rider[:, 1:2], 0.0)
                    for t in range(2 * half, 2 * half + 2):
                        dve.bn_aggr(moments[:, n % 2, t, :], stats[:, n % 2, t, :]).then_inc(s["moments"], 1)
                    after("moments", 4 * n + 2 * half + 2)
                    t = slice(2 * half, 2 * half + 2)
                    dve.tensor_scalar(var[:, n % 2, t], moments[:, n % 2, t, 1], 1.0 + EPS if twice else 1.0,
                                      EPS * EPS if twice else EPS, ALU.mult, ALU.add).then_inc(s["var"], 1)

                def layernorm(n):
                    for t in range(PT_):
                        if t % 2 == 0:
                            after("rstd", 2 * n + t // 2 + 1)
                        if t == 0 and n >= 2:
                            after("turned", 2 * (n - 1))
                        dve.tensor_scalar(nrm[:, n % 2, t, :], tile_of(t).rearrange("p a d -> p (a d)"), moments[:, n % 2, t, 0:1],
                                          rstd[:, n % 2, t:t + 1], ALU.subtract, ALU.mult).then_inc(s["normed"], 1)

                def turned(n, g=None, b=None):
                    after("turned", 2 * n + 2)
                    src = TB[:, BANK:2 * BANK]
                    if g is None:
                        dve.tensor_copy(x_t[:, 1, :], src).then_inc(s["turned_dve"], 1)
                    else:
                        dve.tensor_scalar(x_t[:, 1, :], src, col(g, 1), col(b, 1), ALU.mult, ALU.add).then_inc(s["turned_dve"], 1)

                def mean_square(k):
                    after("sq", k + 1)
                    dve.tensor_reduce(ss[:, k, :], sq[:, k, :].rearrange("p (a d) -> p a d", d=DH), AX_X, ALU.add).then_inc(s["ss"], 1)
                    after("ss", k + 1)
                    dve.tensor_scalar(ms[:, k, :], ss[:, k, :], 1.0 / DH, 1e-16, ALU.mult, ALU.max).then_inc(s["ms"], 1)

                def rms_norm(k, src, name):
                    after("rms", k + 1)
                    dve.tensor_tensor(qk_n[:, k, :, :].rearrange("p t (h d) -> p (t h) d", d=DH), src.rearrange("p (a d) -> p a d", d=DH),
                                      rms[:, k, :].unsqueeze(2).broadcast_to([P, 4 * PT_, DH]), ALU.mult).then_inc(s[name], 1)

                def add_to_x(src, name, k, done, n=None):
                    for half in range(2):
                        after(name, k + half + 1)
                        dve.tensor_tensor(tile_of(2 * half, 2), src[:, half * BANK:(half + 1) * BANK].rearrange("p (t d) -> p t d", d=DM),
                                          tile_of(2 * half, 2), ALU.add).then_inc(s["x_added"], 1)
                        if n is not None:
                            after("x_added", done + half + 1)
                            dve.memset(rider[:, 0:1], 0.0)
                            for t in range(2 * half, 2 * half + 2):
                                statistics(n, t)
                            variances(n, half)

                dve.memset(rider[:, 0:1], 0.0)
                for t in range(PT_):
                    statistics(0, t)
                for half in range(2):
                    variances(0, half)
                layernorm(0)
                turned(0, "ln1_g", "ln1_b")
                after("q0_mm", 2)
                dve.tensor_scalar(q0_t[:, 1, :], D[3][:, BANK:2 * BANK], sc_attn0, bqs[:, 1:2], ALU.mult, ALU.add).then_inc(s["q0_dve"], 1)
                for b in range(2):
                    after("score0", b + 1)
                    dve.tensor_reduce(negm[:, 0, 2 * b:2 * b + 2], D[0][:, b * BANK:(b + 1) * BANK].rearrange("p (r k) -> p r k", k=SEQ),
                                      AX_X, ALU.max, negate=True).then_inc(s["max0"], 1)
                if more:
                    context_norm(it + 1)
                after("p0_turned", 2)
                dve.tensor_copy(p_t[:, 0, BANK:2 * BANK], TB[:, BANK:2 * BANK]).then_inc(s["p0_dve"], 1)
                after("exp0", 4)
                dve.reciprocal(rinv[:, 0, :], rsum[:, 0, :]).then_inc(s["rinv0"], 1)
                if more:
                    context_scale(it + 1)
                after("ctx0_mm", 2)
                dve.tensor_copy(o_t[:, 1, :], D[1][:, BANK:2 * BANK]).then_inc(s["ctx0_dve"], 1)
                after("rinv0", 1)
                after("x_biased", 1)
                for half in range(2):
                    after("out0_mm", half + 1)
                    for t in range(2 * half, 2 * half + 2):
                        x_tile = tile_of(t).rearrange("p a d -> p (a d)")
                        dve.scalar_tensor_tensor(out=x_tile, in0=D[3][:, t * DM:(t + 1) * DM], scalar=rinv[:, 0, t:t + 1],
                                                 in1=x_tile, op0=ALU.mult, op1=ALU.add).then_inc(s["x_added"], 1)
                    after("x_added", 2 * half + 2)
                    dve.memset(rider[:, 0:1], 0.0)
                    for t in range(2 * half, 2 * half + 2):
                        statistics(1, t)
                    variances(1, half)
                layernorm(1)
                turned(1)
                add_to_x(D[0], "ffn0_mm", 0, 4, 2)
                layernorm(2)
                turned(2)
                after("cq_mm", 2)
                dve.tensor_scalar(kk[0:LAT + ROPE, :], D[1][0:LAT + ROPE, BANK:2 * BANK], col("bkv", 0, LAT + ROPE), None, ALU.add).then_inc(s["kk_saved"], 1)
                after("ckvn_mm", 1)
                dve.tensor_tensor(ckvn[:, :, :], D[0][:, 0:PT_ * LAT].rearrange("p (t d) -> p t d", d=LAT),
                                  row("bdkv", LAT).unsqueeze(1).broadcast_to([P, PT_, LAT]), ALU.add).then_inc(s["ckvn_saved"], 1)

                def quad_max(quad, sp, n, batch=None):
                    after("scored", quad + 1)
                    if batch is not None:
                        keys = sp[:, :].rearrange("p (c k) -> p c k", c=2)[:, :, 0:SEQ]
                        m = mask[:, bass.ds(it * 2 + batch, 1), :].broadcast_to([P, 2, SEQ])
                        dve.tensor_tensor(keys, keys, m, ALU.add).then_inc(s["masked"], 1)
                        after("masked", quad - QUADS + 1)
                    dve.tensor_reduce(negm[:, quad % 2, 0:n], sp[:, :].rearrange("p (r k) -> p r k", r=n), AX_X, ALU.max,
                                      negate=True).then_inc(s["maxed"], 1)

                def quad_norm(quad, n, keys):
                    after("pexp", pexp_before(quad + 1))
                    dve.reciprocal(rinv[:, quad % 2, 0:n], rsum[:, quad % 2, 0:n]).then_inc(s["rinv"], 1)
                    after("rinv", quad + 1)
                    for r in range(n):
                        p_row = pe_[:, quad % 2, r * keys:(r + 1) * keys]
                        dve.tensor_scalar(p_row, p_row, rinv[:, quad % 2, r:r + 1], None, ALU.mult).then_inc(s["p_normed"], 1)

                def quad_turned(quad):
                    after("p_turned", quad + 1)
                    if quad >= 2:
                        after("pv_mm", quad - 1)
                    dve.tensor_copy(p_t[:, quad % 2, BANK:2 * BANK], TB[:, BANK:2 * BANK]).then_inc(s["pt_dve"], 1)

                def o_saved(k):
                    after("pv_mm", (k + 1) * QUADS)
                    dve.tensor_copy(o_t[:, 1, :], OB[1]).then_inc(s["o_dve"], 1)

                quad_max(0, D[0], 4)
                quad_max(1, D[1], 4)
                quad_norm(0, 4, SEQ)
                for q in range(QUADS):
                    if q + 2 < QUADS:
                        quad_max(q + 2, D[q % 2], 4)
                    if q + 1 < QUADS:
                        quad_norm(q + 1, 4, SEQ)
                    quad_turned(q)
                o_saved(0)
                after("x_biased", 2)
                add_to_x(D[0], "out1_mm", 0, 6, 3)
                layernorm(3)
                turned(3, "lnl_g", "lnl_b")
                mean_square(0)
                mean_square(1)
                rms_norm(0, D[0][:, :], "q1_normed")
                rms_norm(1, D[1][:, :], "k1l_normed")
                after("q1_turned", 2)
                for odd in range(2):
                    lo = odd * DH
                    dve.tensor_scalar(q1_z[odd][lo:lo + DH, 1, :], TB[lo:lo + DH, BANK:2 * BANK], gamma[lo:lo + DH, 0:1], None,
                                      ALU.mult).then_inc(s["q1_dve"], 1)
                after("k1l_turned", 2)
                dve.tensor_copy(k1_t[:, 1, :, SEQ:2 * SEQ], D[3][:, BANK:2 * BANK].rearrange("p (b k) -> p b k", b=2)).then_inc(s["k1l_dve"], 1)
                quad_max(QUADS, D[0], 2, cross_quad(0)[0])
                quad_max(QUADS + 1, D[1], 2, cross_quad(1)[0])
                if more:
                    context_squares(it + 1)
                quad_norm(QUADS, 2, 2 * SEQ)
                for q in range(QUADS):
                    if q + 2 < QUADS:
                        quad_max(QUADS + q + 2, D[q % 2], 2, cross_quad(q + 2)[0])
                    if q + 1 < QUADS:
                        quad_norm(QUADS + q + 1, 2, 2 * SEQ)
                    quad_turned(QUADS + q)
                o_saved(1)
                after("x_biased", 3)
                add_to_x(D[0], "out1_mm", 2, 8, 4)
                layernorm(4)
                turned(4)
                after("x_biased", 4)
                add_to_x(TB, "y_mm", 0, 10)

            context_norm(0)
            dve.wait_ge(s_in, loaded)
            dve.wait_ge(s_const, 3)
            for h in range(NH):
                last = dve.tensor_scalar(buv_rep[:, h, :], ones[:, :], col("buv", h), None, ALU.mult)
            last.then_inc(s_set, 1)
            for c in range(2):
                last = dve.tensor_scalar(bv_rep[:, c, :], ones[:, :], col("bv", c), None, ALU.mult)
            last.then_inc(s_set, 1)
            dve.wait_ge(s_fold, 1)
            prod = D[3][0:LAT + 1, BANK:BANK + NH * (LAT + 1)].rearrange("p (h n) -> p h n", h=NH)
            dve.tensor_copy(fold_q[0:LAT + 1, :, 0:LAT], prod[:, :, 0:LAT]).then_inc(s_set, 1)
            dve.tensor_copy(fold_q[0:LAT + 1, :, KEYW - 1:KEYW], prod[:, :, LAT:LAT + 1]).then_inc(s_set, 1)
            dve.tensor_copy(fold_v[:, :, :], D[1][:, 0:2 * DM].rearrange("p (c n) -> p c n", c=2)).then_inc(s_set, 1)
            context_scale(0)
            dve.tensor_scalar(mask[:, :, :], mask_u8[:, :, :], 1.0, FLT_MAX, ALU.subtract, ALU.mult).then_inc(s_set, 1)
            dve.tensor_scalar(bqs[:, :], cols[:, COLS["bq"][0]:COLS["bq"][0] + 2], sc_attn0, None, ALU.mult).then_inc(s_set, 1)
            dve.scalar_tensor_tensor(out=gamma[:, :], in0=col("qn"), scalar=sc_attn1, in1=col("kn"),
                                     op0=ALU.mult, op1=ALU.mult).then_inc(s_set, 1)
            dve.wait_ge(s_fold, 2)
            dve.tensor_tensor(row("bo"), D[2][:, 0:DM], row("bo"), ALU.add).then_inc(s_set, 1)
            dve.tensor_tensor(row("bo0"), D[2][:, BANK:BANK + DM], row("bo0"), ALU.add).then_inc(s_set, 1)
            dve.tensor_scalar(scales[:, 1:2], D[3][:, 0:1], 1.0 / (DM * DM), EPS, ALU.mult, ALU.max).then_inc(s_set, 1)
            dve.wait_ge(s_set, SET["scale"])
            dve.tensor_scalar(scales[:, 2:3], scales[:, 1:2], 0.5, None, ALU.mult).then_inc(s_set, 1)
            dve.tensor_scalar(scales[:, 3:4], scales[:, 1:2], -0.5, None, ALU.mult).then_inc(s_set, 1)
            dve.wait_ge(s_set, SET["thresholds"])
            flat = wf[:, :, :].rearrange("p c n -> p (c n)")
            dve.tensor_scalar(tern[:, 1, :], flat, scales[:, 2:3], scales[:, 1:2], ALU.is_gt, ALU.mult).then_inc(s_set, 1)
            dve.tensor_scalar(tern[:, 2, :], flat, scales[:, 3:4], scales[:, 1:2], ALU.is_lt, ALU.mult).then_inc(s_set, 1)
            dve.wait_ge(s_set, SET["signs"])
            dve.tensor_tensor(flat, tern[:, 1, :], tern[:, 2, :], ALU.subtract).then_inc(s_set, 1)
            dve.wait_ge(s_zero, len(ZERO_ROWS))
            dve.memset(cq[LAT:LAT + 1, :], 1.0).then_inc(s_set, 1)
            dve.memset(kk[LAT + ROPE:KEYW, :], 1.0).then_inc(s_set, 1)
            context_squares(0)
            with dve.Fori(0, PAIRS - 1) as it:
                pair(it, True)
            pair(PAIRS - 1, False)




def layout(a):
    import numpy as np
    f = {k: np.asarray(v) for k, v in a.items()}

    def chunked(v):
        v = v.reshape(CH, P, -1)
        return v.transpose(1, 0, 2).reshape(P, -1)

    def column(v):
        v = np.concatenate([v, np.zeros(-len(v) % P, v.dtype)])
        return v.reshape(-1, P).T

    def below(v, n):
        return np.concatenate([v, np.zeros((n - len(v),) + v.shape[1:], v.dtype)])

    def with_bias(w, b):
        return np.concatenate([w, b[None]]).reshape(len(w) + 1, NH, -1)

    m, x0, a1, x1, f1 = "L0_attn_", "L0_xattn_", "L1_attn_", "L1_xattn_", "L1_ffn_"
    cols = np.stack([np.concatenate([chunked(f[m + n]) for n in names], axis=1) for names in (
        ("conv_w", "conv_b", "dt_proj_b", "D", "A_log"),
        ("conv_w_b", "conv_b_b", "dt_proj_b_b", "D_b", "A_b_log"))], axis=1)
    vectors = {
        "ln2_g": f[x0 + "ln2_g"], "ln2_b": f[x0 + "ln2_b"], "lnx_g": f[x1 + "ln_x_g"], "lnx_b": f[x1 + "ln_x_b"],
        "ln1_g": f[x0 + "ln1_g"], "ln1_b": f[x0 + "ln1_b"], "lnl_g": f[x1 + "ln_l_g"], "lnl_b": f[x1 + "ln_l_b"],
        "bq": f[x0 + "bq"], "bk": f[x0 + "bk"], "qn": np.tile(f[x1 + "qn_g"], 2), "kn": np.tile(f[x1 + "kn_g"], 2),
        "bdq": f[a1 + "b_DQ"], "bkv": np.concatenate([f[a1 + "b_DKV"], f[a1 + "b_KR"]]), "b1": f[f1 + "b1"],
        "buv": f[a1 + "b_UV"], "bv": f[x0 + "bv"],
    }
    w_qr = with_bias(f[a1 + "W_QR"], f[a1 + "b_QR"])
    fold_r = np.zeros((P, NH, KEYW), w_qr.dtype)
    fold_r[0:LAT + 1, :, LAT:LAT + ROPE] = w_qr
    out = {
        "x": f["x"].reshape(NBATCH * SEQ, DM),
        "ident": np.eye(P, dtype=np.float32),
        "mamba_cols": cols,
        "in_w": f[m + "in_proj_w"].T,
        "xp_w": np.stack([f[m + "x_proj_w"].T, f[m + "x_proj_w_b"].T]),
        "dt_w": np.stack([below(f[m + "dt_proj_w"].T, P), below(f[m + "dt_proj_w_b"].T, P)]),
        "out_w": f[m + "out_proj_w"].T,
        "ctx": f["ctx_768"].reshape(NBATCH * SEQ, DC),
        "mask": f["mask_BxS2_bk0"].reshape(1, NBATCH * SEQ),
        "lcols": np.concatenate([column(vectors[n]) for n in COLS], axis=1),
        "lrows": np.concatenate([f[x0 + "bo"], f[a1 + "b_O"], f[x1 + "bo"], f[f1 + "b2"], f[a1 + "b_DKV"]])[None],
        "wq0": f[x0 + "Wq"], "wk0": below(f[x0 + "Wk"], 2 * P), "wv0": below(f[x0 + "Wv"], 2 * P), "wo0": f[x0 + "Wo"],
        "wf": f["L0_ffn_weight"].T,
        "w_dq": f[a1 + "W_DQ"], "w_kv": np.concatenate([f[a1 + "W_DKV"], f[a1 + "W_KR"]], axis=1),
        "uq_t": with_bias(f[a1 + "W_UQ"], f[a1 + "b_UQ"]).transpose(2, 1, 0),
        "uk_t": with_bias(f[a1 + "W_UK"], f[a1 + "b_UK"]).transpose(2, 1, 0),
        "uv_t": f[a1 + "W_UV"].reshape(LAT, NH, DK).transpose(2, 1, 0),
        "w_o": f[a1 + "W_O"],
        "fold_r": fold_r,
        "wq1": f[x1 + "Wq"].T, "wkv1": below(f[x1 + "Wkv"].T, 2 * P), "wlkv1": f[x1 + "Wlkv"].T, "wo1": f[x1 + "Wo"].T,
        "u1": f[f1 + "U1"], "v1w": below(f[f1 + "V1"], P), "u2": f[f1 + "U2"], "v2w": below(f[f1 + "V2"], P),
    }
    return {k: np.ascontiguousarray(v) for k, v in out.items()}


def decoder_kernel(nc, dram):
    with ExitStack() as ctx:
        x_sb = ctx.enter_context(nc.sbuf_tensor("x_sb", [P, TILES, DM], F32))
        ident = ctx.enter_context(nc.sbuf_tensor("ident_sb", [P, P], F32))
        shared = ctx.enter_context(nc.sbuf_tensor("shared_sb", [P, REGION], F32))
        mask_u8 = ctx.enter_context(nc.sbuf_tensor("mask_u8", [P, NBATCH, SEQ], U8))
        s_in = ctx.enter_context(nc.semaphore("inputs_loaded"))
        s_ctx = ctx.enter_context(nc.semaphore("c_loaded"))
        mamba_block(nc, dram, x_sb, ident, shared, lambda sp: load_layers(sp, dram, shared, mask_u8, s_in, s_ctx))
        layers_block(nc, dram, x_sb, ident, shared, mask_u8, s_in, s_ctx)


def kernel(**inputs):
    import numpy as _np
    import concourse.bacc as _bacc
    from concourse.bass_utils import run_bass_kernel_spmd as _run

    nc = _bacc.Bacc("TRN2", target_bir_lowering=False, num_devices=1)
    arrays, dram = {}, {}
    for name, v in layout(inputs).items():
        arrays[f"{name}_dram"] = v
        dram[name] = nc.dram_tensor(f"{name}_dram", v.shape, mybir.dt.from_np(v.dtype), kind="ExternalInput").ap()
    dram["out"] = nc.dram_tensor("out_dram", (NBATCH * SEQ, DM), F32, kind="ExternalOutput").ap()
    decoder_kernel(nc, dram)
    r = _run(nc, [arrays], core_ids=[0])
    return _np.asarray(r.results[0]["out_dram"]).reshape(NBATCH, SEQ, DM)
```
